# Optimizing a Trainium2 kernel written in Bass

```python
import numpy as np
import jax
import jax.numpy as jnp

def _softmax(x, axis=-1):
    return jax.nn.softmax(x, axis=axis)

def _gelu(x):
    return jax.nn.gelu(x, approximate=True)

def _silu(x):
    return jax.nn.silu(x)

def _sigmoid(x):
    return jax.nn.sigmoid(x)

def _layernorm(x, axis=-1, eps=1e-05):
    m = jnp.mean(x, axis=axis, keepdims=True)
    v = jnp.var(x, axis=axis, keepdims=True)
    return (x - m) / jnp.sqrt(v + eps)

def _scatter_add(tgt, idx, src, axis=0):
    return tgt.at[idx].add(src)

def _segment_sum(src, seg, n):
    return jax.ops.segment_sum(src, seg, n)
kernel_name = 'mk_gnn_resnorm_d4_gnn_r64_8f9c4b'

def setup_inputs(seed: int=0):
    np.random.seed(seed)
    _w = jnp.asarray

    def _rec_inputs():
        import jax
        import jax.numpy as jnp
        _gk = jax.random.key(seed)
        x = -0.0005121 + 1.001 * jax.random.normal(jax.random.fold_in(_gk, 1), (100000, 64), jnp.float32)
        src = jax.random.randint(jax.random.fold_in(_gk, 2), (50000,), 0, 100000, jnp.int32)
        dst = jnp.minimum((100000 * jax.random.uniform(jax.random.fold_in(_gk, 3), (50000,)) ** 2.0).astype(jnp.int32), 99999)
        _o = jnp.argsort(dst, stable=True)
        src = src[_o]
        dst = dst[_o]
        edge_attr_16 = 0.000254156 + 0.999948 * jax.random.normal(jax.random.fold_in(_gk, 12), (50000, 16), jnp.float32)
        edge_attr_64 = -6.74381e-05 + 0.999835 * jax.random.normal(jax.random.fold_in(_gk, 13), (50000, 64), jnp.float32)
        return (x, src, dst, edge_attr_16, edge_attr_64)
    x, src, dst, edge_attr_16, edge_attr_64 = _rec_inputs()

    def _L0_gnn_setup():
        import jax, jax.numpy as jnp
        import numpy as np
        N, E = (50000, 12500)
        IN_DIM, OUT_DIM = (64, 64)
        key = jax.random.key(seed)
        k = jax.random.split(key, 8)
        node_features = jax.random.normal(k[0], (N, IN_DIM), dtype=jnp.float32)
        edge_index = jax.random.randint(k[1], (2, E), 0, N, dtype=jnp.int32)
        s_msg = 1.0 / np.sqrt(2 * IN_DIM)
        W_msg = jax.random.uniform(k[2], (2 * IN_DIM, OUT_DIM), minval=-s_msg, maxval=s_msg, dtype=jnp.float32)
        b_msg = jax.random.uniform(k[3], (OUT_DIM,), minval=-s_msg, maxval=s_msg, dtype=jnp.float32)
        s_upd = 1.0 / np.sqrt(IN_DIM + OUT_DIM)
        W_upd = jax.random.uniform(k[4], (IN_DIM + OUT_DIM, OUT_DIM), minval=-s_upd, maxval=s_upd, dtype=jnp.float32)
        b_upd = jax.random.uniform(k[5], (OUT_DIM,), minval=-s_upd, maxval=s_upd, dtype=jnp.float32)
        gamma = jnp.ones((OUT_DIM,), dtype=jnp.float32)
        beta = jnp.zeros((OUT_DIM,), dtype=jnp.float32)
        return {'node_features': node_features, 'edge_index': edge_index, 'W_msg': W_msg, 'b_msg': b_msg, 'W_upd': W_upd, 'b_upd': b_upd, 'gamma': gamma, 'beta': beta}
    _L0_gnn_all = _L0_gnn_setup()
    _L0_gnn_in = {k: v for k, v in _L0_gnn_all.items() if k in ('W_msg', 'b_msg', 'W_upd', 'b_upd', 'gamma', 'beta')}
    del _L0_gnn_all

    def _L1_gnn_setup():
        import jax, jax.numpy as jnp
        import numpy as np
        N, E = (50000, 12500)
        EMB, HEADS, EDGE_DIM = (64, 4, 16)
        NEG_SLOPE = 0.2
        LN_EPS = 1e-05
        key = jax.random.key(seed)
        ks = jax.random.split(key, 12)
        HC = HEADS * EMB
        inp = {'x': jax.random.normal(ks[0], (N, EMB), jnp.float32), 'edge_index': jax.random.randint(ks[1], (2, E), 0, N, jnp.int32), 'edge_attr': jax.random.normal(ks[2], (E, EDGE_DIM), jnp.float32), 'W': jax.random.normal(ks[3], (EMB, HC), jnp.float32) * 0.1, 'W_edge': jax.random.normal(ks[4], (EDGE_DIM, HC), jnp.float32) * 0.1, 'att_src': jax.random.normal(ks[5], (HEADS, EMB), jnp.float32) * 0.1, 'att_dst': jax.random.normal(ks[6], (HEADS, EMB), jnp.float32) * 0.1, 'att_edge': jax.random.normal(ks[7], (HEADS, EMB), jnp.float32) * 0.1, 'bias': jnp.zeros((HC,), jnp.float32), 'Wp': jax.random.normal(ks[8], (HC, EMB), jnp.float32) * 0.05, 'bp': jnp.zeros((EMB,), jnp.float32), 'gamma': jnp.ones((EMB,), jnp.float32), 'beta': jnp.zeros((EMB,), jnp.float32)}
        return inp
    _L1_gnn_all = _L1_gnn_setup()
    _L1_gnn_in = {k: v for k, v in _L1_gnn_all.items() if k in ('W', 'W_edge', 'att_src', 'att_dst', 'att_edge', 'bias', 'Wp', 'bp', 'gamma', 'beta')}
    del _L1_gnn_all

    def _L2_gnn_setup():
        import jax, jax.numpy as jnp
        import numpy as np
        N, E, D, H, ED = (50000, 12500, 64, 8, 16)
        DH = D // H
        key = jax.random.key(seed)
        ks = jax.random.split(key, 16)
        s = 0.05
        return {'x': jax.random.normal(ks[0], (N, D), jnp.float32), 'edge_index': jax.random.randint(ks[1], (2, E), 0, N, jnp.int32), 'edge_attr': jax.random.normal(ks[2], (E, ED), jnp.float32), 'Wq': jax.random.normal(ks[3], (D, D), jnp.float32) * s, 'bq': jnp.zeros((D,), jnp.float32), 'Wk': jax.random.normal(ks[4], (D, D), jnp.float32) * s, 'bk': jnp.zeros((D,), jnp.float32), 'Wv': jax.random.normal(ks[5], (D, D), jnp.float32) * s, 'bv': jnp.zeros((D,), jnp.float32), 'We': jax.random.normal(ks[6], (ED, D), jnp.float32) * s, 'be': jnp.zeros((D,), jnp.float32), 'Wskip': jax.random.normal(ks[7], (D, D), jnp.float32) * s, 'bskip': jnp.zeros((D,), jnp.float32), 'Wbeta': jax.random.normal(ks[8], (3 * D, 1), jnp.float32) * s, 'gamma': jnp.ones((D,), jnp.float32), 'beta_bn': jnp.zeros((D,), jnp.float32)}
    _L2_gnn_all = _L2_gnn_setup()
    _L2_gnn_in = {k: v for k, v in _L2_gnn_all.items() if k in ('Wq', 'bq', 'Wk', 'bk', 'Wv', 'bv', 'We', 'be', 'Wskip', 'bskip', 'Wbeta', 'gamma', 'beta_bn')}
    del _L2_gnn_all

    def _L3_gnn_setup():
        import jax, jax.numpy as jnp
        import numpy as np
        V, E, D = (50000, 1250000, 64)
        LOG2 = float(np.log(2.0))

        def ssp(x):
            return jax.nn.softplus(x) - LOG2
        key = jax.random.key(seed)
        ks = jax.random.split(key, 10)
        s = 1.0 / np.sqrt(D)
        return {'node_feats': jax.random.normal(ks[0], (V, D), jnp.float32), 'edge_feats': jax.random.normal(ks[1], (E, D), jnp.float32), 'src': jax.random.randint(ks[2], (E,), 0, V, jnp.int32), 'dst': jax.random.randint(ks[3], (E,), 0, V, jnp.int32), 'We1': jax.random.normal(ks[4], (D, D), jnp.float32) * s, 'be1': jnp.zeros((D,), jnp.float32), 'We2': jax.random.normal(ks[5], (D, D), jnp.float32) * s, 'be2': jnp.zeros((D,), jnp.float32), 'Wn': jax.random.normal(ks[6], (D, D), jnp.float32) * s, 'bn': jnp.zeros((D,), jnp.float32), 'Wc': jax.random.normal(ks[7], (D, D), jnp.float32) * s, 'bc': jnp.zeros((D,), jnp.float32), 'Wo': jax.random.normal(ks[8], (D, D), jnp.float32) * s, 'bo': jnp.zeros((D,), jnp.float32)}
    _L3_gnn_all = _L3_gnn_setup()
    _L3_gnn_in = {k: v for k, v in _L3_gnn_all.items() if k in ('We1', 'be1', 'We2', 'be2', 'Wn', 'bn', 'Wc', 'bc', 'Wo', 'bo')}
    del _L3_gnn_all
    return {'x': x, 'src': src, 'dst': dst, 'edge_attr_16': edge_attr_16, 'edge_attr_64': edge_attr_64, 'L0_gnn_W_msg': _L0_gnn_in['W_msg'], 'L0_gnn_b_msg': _L0_gnn_in['b_msg'], 'L0_gnn_W_upd': _L0_gnn_in['W_upd'], 'L0_gnn_b_upd': _L0_gnn_in['b_upd'], 'L0_gnn_gamma': _L0_gnn_in['gamma'], 'L0_gnn_beta': _L0_gnn_in['beta'], 'L1_gnn_W': _L1_gnn_in['W'], 'L1_gnn_W_edge': _L1_gnn_in['W_edge'], 'L1_gnn_att_src': _L1_gnn_in['att_src'], 'L1_gnn_att_dst': _L1_gnn_in['att_dst'], 'L1_gnn_att_edge': _L1_gnn_in['att_edge'], 'L1_gnn_bias': _L1_gnn_in['bias'], 'L1_gnn_Wp': _L1_gnn_in['Wp'], 'L1_gnn_bp': _L1_gnn_in['bp'], 'L1_gnn_gamma': _L1_gnn_in['gamma'], 'L1_gnn_beta': _L1_gnn_in['beta'], 'L2_gnn_Wq': _L2_gnn_in['Wq'], 'L2_gnn_bq': _L2_gnn_in['bq'], 'L2_gnn_Wk': _L2_gnn_in['Wk'], 'L2_gnn_bk': _L2_gnn_in['bk'], 'L2_gnn_Wv': _L2_gnn_in['Wv'], 'L2_gnn_bv': _L2_gnn_in['bv'], 'L2_gnn_We': _L2_gnn_in['We'], 'L2_gnn_be': _L2_gnn_in['be'], 'L2_gnn_Wskip': _L2_gnn_in['Wskip'], 'L2_gnn_bskip': _L2_gnn_in['bskip'], 'L2_gnn_Wbeta': _L2_gnn_in['Wbeta'], 'L2_gnn_gamma': _L2_gnn_in['gamma'], 'L2_gnn_beta_bn': _L2_gnn_in['beta_bn'], 'L3_gnn_We1': _L3_gnn_in['We1'], 'L3_gnn_be1': _L3_gnn_in['be1'], 'L3_gnn_We2': _L3_gnn_in['We2'], 'L3_gnn_be2': _L3_gnn_in['be2'], 'L3_gnn_Wn': _L3_gnn_in['Wn'], 'L3_gnn_bn': _L3_gnn_in['bn'], 'L3_gnn_Wc': _L3_gnn_in['Wc'], 'L3_gnn_bc': _L3_gnn_in['bc'], 'L3_gnn_Wo': _L3_gnn_in['Wo'], 'L3_gnn_bo': _L3_gnn_in['bo']}

def reference(x, src, dst, edge_attr_16, edge_attr_64, L0_gnn_W_msg, L0_gnn_b_msg, L0_gnn_W_upd, L0_gnn_b_upd, L0_gnn_gamma, L0_gnn_beta, L1_gnn_W, L1_gnn_W_edge, L1_gnn_att_src, L1_gnn_att_dst, L1_gnn_att_edge, L1_gnn_bias, L1_gnn_Wp, L1_gnn_bp, L1_gnn_gamma, L1_gnn_beta, L2_gnn_Wq, L2_gnn_bq, L2_gnn_Wk, L2_gnn_bk, L2_gnn_Wv, L2_gnn_bv, L2_gnn_We, L2_gnn_be, L2_gnn_Wskip, L2_gnn_bskip, L2_gnn_Wbeta, L2_gnn_gamma, L2_gnn_beta_bn, L3_gnn_We1, L3_gnn_be1, L3_gnn_We2, L3_gnn_be2, L3_gnn_Wn, L3_gnn_bn, L3_gnn_Wc, L3_gnn_bc, L3_gnn_Wo, L3_gnn_bo):
    import jax
    import jax.numpy as jnp

    def _L0_gnn_ref(node_features, edge_index, W_msg, b_msg, W_upd, b_upd, gamma, beta):
        import jax, jax.numpy as jnp
        import numpy as np
        N, E = (50000, 12500)
        IN_DIM, OUT_DIM = (64, 64)
        row, col = (edge_index[0], edge_index[1])
        msg_in = jnp.concatenate([node_features[row], node_features[col]], axis=1)
        messages = jax.nn.relu(msg_in @ W_msg + b_msg)
        aggregated = jax.ops.segment_sum(messages, col, num_segments=node_features.shape[0])
        upd_in = jnp.concatenate([node_features, aggregated], axis=1)
        updated = jax.nn.relu(upd_in @ W_upd + b_upd)
        mu = jnp.mean(updated, axis=-1, keepdims=True)
        var = jnp.var(updated, axis=-1, keepdims=True)
        normed = (updated - mu) * jax.lax.rsqrt(var + 1e-05)
        return normed * gamma + beta

    def _L1_gnn_ref(x, edge_index, edge_attr, W, W_edge, att_src, att_dst, att_edge, bias, Wp, bp, gamma, beta):
        import jax, jax.numpy as jnp
        import numpy as np
        N, E = (50000, 12500)
        EMB, HEADS, EDGE_DIM = (64, 4, 16)
        NEG_SLOPE = 0.2
        LN_EPS = 1e-05
        n = x.shape[0]
        H, C = att_src.shape
        xw = (x @ W).reshape(n, H, C)
        a_src_n = jnp.einsum('nhc,hc->nh', xw, att_src)
        a_dst_n = jnp.einsum('nhc,hc->nh', xw, att_dst)
        src, dst = (edge_index[0], edge_index[1])
        loop = jnp.arange(n, dtype=edge_index.dtype)
        cnt = jax.ops.segment_sum(jnp.ones_like(dst, jnp.float32), dst, num_segments=n)
        loop_attr = jax.ops.segment_sum(edge_attr, dst, num_segments=n) / jnp.maximum(cnt, 1.0)[:, None]
        src2 = jnp.concatenate([src, loop])
        dst2 = jnp.concatenate([dst, loop])
        ea = jnp.concatenate([edge_attr, loop_attr], axis=0)
        ew = (ea @ W_edge).reshape(-1, H, C)
        a_edge = jnp.einsum('ehc,hc->eh', ew, att_edge)
        alpha = a_src_n[src2] + a_dst_n[dst2] + a_edge
        alpha = jnp.where(alpha >= 0, alpha, NEG_SLOPE * alpha)
        amax = jax.ops.segment_max(alpha, dst2, num_segments=n)
        ae = jnp.exp(alpha - amax[dst2])
        denom = jax.ops.segment_sum(ae, dst2, num_segments=n)
        attn = ae / denom[dst2]
        msg = xw[src2] * attn[:, :, None]
        agg = jax.ops.segment_sum(msg, dst2, num_segments=n)
        gat_out = agg.reshape(n, H * C) + bias
        proj = gat_out @ Wp + bp
        h = x + jax.nn.elu(proj)
        mu = jnp.mean(h, axis=-1, keepdims=True)
        var = jnp.mean((h - mu) ** 2, axis=-1, keepdims=True)
        out = (h - mu) * jax.lax.rsqrt(var + LN_EPS) * gamma + beta
        return out

    def _L2_gnn_ref(x, edge_index, edge_attr, Wq, bq, Wk, bk, Wv, bv, We, be, Wskip, bskip, Wbeta, gamma, beta_bn):
        import jax, jax.numpy as jnp
        import numpy as np
        N, E, D, H, ED = (50000, 12500, 64, 8, 16)
        DH = D // H
        n, d = x.shape
        src, dst = (edge_index[0], edge_index[1])
        q = (x @ Wq + bq).reshape(n, H, DH)
        k = (x @ Wk + bk).reshape(n, H, DH)
        v = (x @ Wv + bv).reshape(n, H, DH)
        e = (edge_attr @ We + be).reshape(-1, H, DH)
        ke = k[src] + e
        ve = v[src] + e
        logits = (q[dst] * ke).sum(-1) / jnp.sqrt(jnp.float32(DH))
        m = jax.ops.segment_max(logits, dst, num_segments=n)
        p = jnp.exp(logits - m[dst])
        denom = jax.ops.segment_sum(p, dst, num_segments=n)
        alpha = p / (denom[dst] + 1e-16)
        out = jax.ops.segment_sum(alpha[:, :, None] * ve, dst, num_segments=n)
        out = out.reshape(n, d)
        x_r = x @ Wskip + bskip
        g = jax.nn.sigmoid(jnp.concatenate([out, x_r, out - x_r], axis=-1) @ Wbeta)
        out = g * x_r + (1.0 - g) * out
        mean = out.mean(axis=0)
        var = out.var(axis=0)
        out = (out - mean) * jax.lax.rsqrt(var + 1e-05) * gamma + beta_bn
        return jnp.where(out >= 0, out, 0.01 * out)

    def _L3_gnn_ref(node_feats, edge_feats, src, dst, We1, be1, We2, be2, Wn, bn, Wc, bc, Wo, bo):
        import jax, jax.numpy as jnp
        import numpy as np
        V, E, D = (50000, 1250000, 64)
        LOG2 = float(np.log(2.0))

        def ssp(x):
            return jax.nn.softplus(x) - LOG2
        f = ssp(edge_feats @ We1 + be1)
        f = ssp(f @ We2 + be2)
        h = node_feats @ Wn + bn
        msg = h[src] * f
        agg = jax.ops.segment_sum(msg, dst, num_segments=node_feats.shape[0])
        out = ssp(agg @ Wc + bc)
        return out @ Wo + bo
    edge_index = jnp.stack([src, dst])
    x = _layernorm(x + _L0_gnn_ref(x, edge_index, L0_gnn_W_msg, L0_gnn_b_msg, L0_gnn_W_upd, L0_gnn_b_upd, L0_gnn_gamma, L0_gnn_beta), axis=-1)
    x = _layernorm(x + _L1_gnn_ref(x, edge_index, edge_attr_16, L1_gnn_W, L1_gnn_W_edge, L1_gnn_att_src, L1_gnn_att_dst, L1_gnn_att_edge, L1_gnn_bias, L1_gnn_Wp, L1_gnn_bp, L1_gnn_gamma, L1_gnn_beta), axis=-1)
    x = _layernorm(x + _L2_gnn_ref(x, edge_index, edge_attr_16, L2_gnn_Wq, L2_gnn_bq, L2_gnn_Wk, L2_gnn_bk, L2_gnn_Wv, L2_gnn_bv, L2_gnn_We, L2_gnn_be, L2_gnn_Wskip, L2_gnn_bskip, L2_gnn_Wbeta, L2_gnn_gamma, L2_gnn_beta_bn), axis=-1)
    x = _layernorm(x + _L3_gnn_ref(x, edge_attr_64, src, dst, L3_gnn_We1, L3_gnn_be1, L3_gnn_We2, L3_gnn_be2, L3_gnn_Wn, L3_gnn_bn, L3_gnn_Wc, L3_gnn_bc, L3_gnn_Wo, L3_gnn_bo), axis=-1)
    return x

_drawn_inputs = setup_inputs


def setup_inputs(seed=0):
    import zlib

    import numpy as np

    out = dict(_drawn_inputs(seed))
    spreads = {'L0_gnn_gamma': (1.0, 0.2),
     'L0_gnn_beta': (0.0, 0.1),
     'L1_gnn_bias': (0.0, 0.1),
     'L1_gnn_bp': (0.0, 0.269),
     'L1_gnn_gamma': (1.0, 0.2),
     'L1_gnn_beta': (0.0, 0.1),
     'L2_gnn_bq': (0.0, 0.8),
     'L2_gnn_bk': (0.0, 0.8),
     'L2_gnn_bv': (0.0, 0.1),
     'L2_gnn_be': (0.0, 0.1),
     'L2_gnn_bskip': (0.0, 0.386),
     'L2_gnn_gamma': (1.0, 0.2),
     'L2_gnn_beta_bn': (0.0, 0.1),
     'L3_gnn_be1': (0.0, 0.778),
     'L3_gnn_be2': (0.0, 0.519),
     'L3_gnn_bn': (0.0, 0.76),
     'L3_gnn_bc': (0.0, 0.1),
     'L3_gnn_bo': (0.0, 0.1)}
    factors = {'L1_gnn_W_edge': 6.545,
     'L1_gnn_att_dst': 5.165,
     'L1_gnn_att_edge': 7.94,
     'L2_gnn_Wq': 3.719,
     'L2_gnn_Wk': 4.102}
    for name, (base, spread) in spreads.items():
        noise = np.random.default_rng([zlib.crc32(name.encode()), seed]).standard_normal(out[name].shape)
        drawn = base * np.exp(spread * noise) if base else spread * noise
        out[name] = jnp.asarray(drawn.astype(out[name].dtype))
    for name, factor in factors.items():
        out[name] = (out[name] * factor).astype(out[name].dtype)
    return out
```

```python
from contextlib import ExitStack

import numpy as np
import concourse.bass as bass
from concourse import mybir
from concourse.alu_op_type import AluOpType as ALU

F32 = mybir.dt.float32
I32 = mybir.dt.int32
ACT = mybir.ActivationFunctionType
AX = mybir.AxisListType

N, E, D = 100000, 50000, 64
W = 500
TE = 125
J = W // TE
L = 4
NB = E // W
IT = NB // L
H1, H2 = 4, 8
EPS = 1e-5
LN2 = float(np.log(2.0))
NEG = -1.0e30
FAR = float(1 << 23)
MP, MN = 80, N // 80


class Chain:

    def __init__(self, *stages):
        self.stages = stages

    def at(self, i, stage):
        return i * len(self.stages) + self.stages.index(stage) + 2

    def end(self):
        return IT * len(self.stages) + 1


LN_STEPS = ("cen", "sq", "var", "ln", "rstd", "norm")


def ln_names(k):
    return tuple(f"{s}{k}" for s in LN_STEPS)


def program(nc, x, xT, src, dst, ea16T, ea64T, w, out):
    ctx = ExitStack()
    with ctx:
        def sb(name, shape, dt=F32):
            return ctx.enter_context(nc.sbuf_tensor(name, shape, dt))

        def sem(name):
            return ctx.enter_context(nc.semaphore(name))

        T1 = nc.dram_tensor("T1", (N + E, D), F32).ap()
        T2 = nc.dram_tensor("T2", (N + E, D), F32).ap()
        T3 = nc.dram_tensor("T3", (N + E, 2 * D), F32).ap()
        MAP = nc.dram_tensor("MAP", (N, 2), I32).ap()
        MASKS = nc.dram_tensor("MASKS", (6, E), F32).ap()
        SAME, FIRST, SAMEN, LAST, NEGP, NEGN = range(6)
        NOE = nc.dram_tensor("NOE", (N,), F32).ap()

        def lanes(name, cols, dt=F32):
            return [sb(f"{name}{l}", [128, cols], dt) for l in range(L)]

        CT, CO, Y, H, SQ = (lanes(n, W) for n in ("CT", "CO", "Y", "H", "SQ"))
        S0, S1, WD = (lanes(n, W) for n in ("S0", "S1", "WD"))
        MX = lanes("MX", W + 1)
        RW = lanes("RW", 2 * W)
        MA, MB, MC, MD = (lanes(n, W) for n in ("MA", "MB", "MC", "MD"))
        EA, EAS = (lanes(n, W) for n in ("EA", "EAS"))
        TILE, TILEO = (lanes(n, J * 128) for n in ("TILE", "TILEO"))
        ROWS = lanes("ROWS", 2 * J * 128)
        PA = [ctx.enter_context(nc.psum_tensor(f"PA{l}", [128, 512], F32)) for l in range(L)]
        PB = [ctx.enter_context(nc.psum_tensor(f"PB{l}", [128, 512], F32)) for l in range(L)]

        mats = {}
        WALL = sb("WALL", [128, 2336])
        used = [0]

        def mat(name, cols):
            mats[name] = WALL[:, used[0]:used[0] + cols]
            used[0] += cols
            return mats[name]

        w_msg, w_upd, w_updb = mat("w_msg", 64), mat("w_upd", 64), mat("w_updb", 128)
        wT = mat("wT", 4 * 64)
        weT = mat("weT", 4 * 16)
        wp = mat("wp", 4 * 64)
        att = mat("att", 12)
        g_cat = mat("g_cat", 128)
        g_sum, g_sumb = mat("g_sum", 64), mat("g_sumb", 128)
        a_log, a_self, a_edge, a_cnt = mat("a_log", 4), mat("a_self", 4), mat("a_edge", 4), mat("a_cnt", 4)
        w_q, w_kv, w_ekv, w_skip, w_skipb = (mat("w_q", 64), mat("w_kv", 128), mat("w_ekv", 128),
                                             mat("w_skip", 64), mat("w_skipb", 128))
        w_z, w_zb = mat("w_z", 64), mat("w_zb", 128)
        w_e1, w_e2, w_n, w_c = mat("w_e1", 64), mat("w_e2", 64), mat("w_n", 64), mat("w_c", 64)
        w_o, w_oT, w_oc = mat("w_o", 64), mat("w_oT", 64), mat("w_oc", 64)
        assert used[0] <= 2336, used[0]
        vec_names = ["bmsg", "bupd", "g0", "b0", "bp", "g1", "b1", "bq", "bskip", "g2", "b2", "be1", "be2", "bn",
                     "bc", "bo", "wb1", "wb2", "wb3", "bk", "bv", "be", "hb0", "hb1", "hb2", "hb3", "bproj", "wcol", "wb",
                     "cb", "sp0", "cvec", "mean", "var", "bs", "bt", "m64", "t0", "t1", "eps", "tiny"]
        VEC = sb("VEC", [128, len(vec_names)])
        v = {n: VEC[:, k:k + 1] for k, n in enumerate(vec_names)}
        STAT = sb("STAT", [128, 4, NB])
        SUMS = sb("SUMS", [128, 4])
        IDN = sb("IDN", [128, 128])
        AVG = sb("AVG", [128, 128])
        CEN = sb("CEN", [128, 128])
        CEN2 = sb("CEN2", [128, 64])
        ADD2 = sb("ADD2", [128, 64])
        DUPD = sb("DUPD", [128, 128])
        SUBX = sb("SUBX", [128, 64])
        WOCEN = sb("WOCEN", [128, 64])
        B4 = sb("B4", [4, 256])
        B8 = sb("B8", [8, 128])
        HSEL = sb("HSEL", [64, 8])
        ONES = sb("ONES", [128, 128])
        CAR = sb("CAR", [128, 8])

        NT = E // TE
        SRCI, DSTI, SCATI = (sb(n, [TE, NT], I32) for n in ("SRCI", "DSTI", "SCATI"))
        MAPV = sb("MAPV", [TE, NT, 2], I32)
        RINGI = sb("RINGI", [TE, L, 2, J], I32)
        RINGV = sb("RINGV", [TE, L, J, 2], I32)

        MAPBUF = sb("MAPBUF", [MP, 2 * MN], I32)
        NOEBUF = sb("NOEBUF", [MP, MN])
        wsem, built, pdma = sem("weights_in"), sem("constants_built"), sem("prep_dma")
        masks_ready, starts, indices_ready = sem("masks_ready"), sem("starts"), sem("indices_ready")
        built_pool, dve_link, derived = sem("pool_link"), sem("dve_link"), sem("derived")
        rows_free = [sem(f"rows_free{l}") for l in range(L)]
        bc_steps, bias_row, bias_row_in = sem("bc_steps"), sem("bias_row"), sem("bias_row_in")
        CARRY = {n: sem("carry_" + n) for n in ("agg0", "hold1", "mx1", "den1", "eas1", "s10", "s11", "hold2", "mx2",
                                                "den2", "s2", "agg3")}
        wdone, ptr = sem("weights_ready"), sem("prep_transposed")
        idx_ready, map_moved, map_done = sem("idx_ready"), [sem(f"map_moved{l}") for l in range(L)], sem("map_done")
        noe_dma, noe_ready, bn_done = sem("noe_dma"), sem("noe_ready"), sem("bn_done")
        map_got, map_copied = sem("map_got"), sem("map_copied")
        fin = sem("stat_done")

        class Phase:
            def __init__(self, tag, *stages):
                self.chain = Chain(*stages)
                self.at, self.end = self.chain.at, self.chain.end
                self.s = [sem(f"{tag}_chain{l}") for l in range(L)]
                self.load = [sem(f"{tag}_load{l}") for l in range(L)]
                self.got = [sem(f"{tag}_gather{l}") for l in range(L)]
                self.store = [sem(f"{tag}_store{l}") for l in range(L)]

        out_steps = ("outT", "rows")
        P0 = Phase("l0", "tT", "cat", "msg", "relu", "agg", "upd", "updrelu", *ln_names(1), "aff1", "res1",
                   *ln_names(2), *out_steps)
        PD = Phase("d1", "upd", "updrelu", *ln_names(1), "aff1", "res1", *ln_names(2), "outT1", "rows1",
                   "proj", "elu_n", "elu_e", "elu_p", "elu", "elu_res", *ln_names(3), "aff3", "res3", *ln_names(4),
                   "outT2", "rows2", "xr", "xrb", "z", "zc", "ze", "zl", "zg", "u", "outT3", "rows3",
                   "um", "us", "uq")
        P1 = Phase("l1", "tT", "cat", "own", "hold", "logit", "lg", "leaky", "mcar", "mx", "dr", "drn", "dw", "exp",
                   "den", "eas", "dxs", "dx", "bw0", "wd0", "br0", "s0", "bw1", "wd1", "br1", "s1",
                   "esum", "lcnt", "rcnt", "emean", "sself", "sadd", "sleaky", "mfin", "g1", "g2", "gexp",
                   "dfac", "dsum", "dln", "drec", "fac", "bf0", "sf0", "bf1", "sf1", "proj",
                   "elu_n", "elu_e", "elu_p", "elu", "elu_res", *ln_names(3), "aff3", "res3", *ln_names(4),
                   *out_steps)
        P2 = Phase("l2", "tT", "cat", "own", "hold", "q", "qb", "kv", "qk", "vc", "logit", "lg", "mcar", "mx", "dr",
                   "drn", "dw", "exp", "den", "bw", "wv", "br", "s", "dln", "drec", "bd", "o", "xr", "xrb", "z",
                   "zc", "ze", "zl", "zg", "gd", "u", "um", "us", "uq", *out_steps)
        P3 = Phase("l3", "tT", "cat", "oT", "ocat", "aff", "lrelu", "oaff", "olrelu", *ln_names(1),
                   "f1", "f1a", "f1e", "f1l", "f1r", "f1s", "f2", "f2a", "f2e", "f2l", "f2r", "f2s",
                   "h", "hb", "msg", "agg", "c", "ca", "ce", "cl", "cr", "cs", "cen2", "cb2", "sq2", "var2", "ln2",
                   "rstd2", "norm2", *out_steps)
        P4 = Phase("d3", "tT", "cat", "oT", "ocat", "aff", "lrelu", "oaff", "olrelu", *ln_names(1),
                   "cen2", "cb2", "sq2", "var2", "ln2", "rstd2", "norm2", *out_steps)
        PHASES = (P0, PD, P1, P2, P4, P3)

        block = ctx.enter_context(nc.Block())
        NWDMA_TOTAL = 3 + 4 + 3 * H1 + 3 + H1 + 6 + 6 + 4 + 2 * 16 + 2 * 3

        def blk(i, lane, back):
            return (NB - 1 - lane) - i * L if back else i * L + lane

        def rows_of(table, base, i, lane, back=False, c0=0, c1=None):
            b = blk(i, lane, back)
            c1 = table.shape[1] if c1 is None else c1
            return table[bass.ds(base + b * W, W), c0:c1].rearrange("(j p) c -> p j c", p=TE)

        def cols_of(a, i, lane, back=False, base=0):
            return a[:, bass.ds(base + blk(i, lane, back) * W, W)]

        def mask_of(k, rows, i, lane, back=False):
            return MASKS[k:k + 1, bass.ds(blk(i, lane, back) * W, W)].to_broadcast([rows, W])

        def wait_phase_done(eng, P, stores=True):
            for l in range(L):
                eng.wait_ge(P.s[l], P.end())
                if stores:
                    eng.wait_ge(P.store[l], P.stored)

        P0.stored = 16 * (IT + 1)
        P1.stored = 16 * (IT + 1)
        P2.stored = 16 * (IT + 1)
        P3.stored = 16 * J * IT
        PD.stored = 16 * (6 * IT + 6)
        P4.stored = 16 * (2 * IT + 2)

        @block.sync
        def _(sp):
            sp.wait_ge(built, 1)

            loaded = [0]

            def ld(o, i):
                sp.dma_start(o, i).then_inc(wsem, 16)
                loaded[0] += 1

            ld(w_msg[0:64, :], w["L0_gnn_W_msg"][64:128, :])
            ld(w_msg[64:128, :], w["L0_gnn_W_msg"][0:64, :])
            ld(w_upd, w["L0_gnn_W_upd"])
            wide = [(w_updb, w["L0_gnn_W_upd"][0:64, :]), (w_skipb, w["L2_gnn_Wskip"])]
            for m, a in wide:
                ld(m[0:64, 0:64], a)
                ld(m[64:128, 64:128], a)
            for h in range(H1):
                ld(wT[0:64, 64 * h:64 * h + 64], w["WT"][64 * h:64 * h + 64, :])
                ld(weT[0:64, 16 * h:16 * h + 16], w["WeT"][64 * h:64 * h + 64, :])
                ld(wp[0:64, 64 * h:64 * h + 64], w["L1_gnn_Wp"][64 * h:64 * h + 64, :])
            for k, n in enumerate(("att_src", "att_dst", "att_edge")):
                ld(att[0:64, 4 * k:4 * k + 4], w[n + "T"])
            for h in range(H1):
                ld(v[f"hb{h}"][0:64, :], w["L1_gnn_bias"][64 * h:64 * h + 64].unsqueeze(1))
            ld(w_q[0:64, :], w["L2_gnn_Wq"])
            ld(w_kv[64:128, 0:64], w["L2_gnn_Wk"])
            ld(w_kv[64:128, 64:128], w["L2_gnn_Wv"])
            ld(w_ekv[0:16, 0:64], w["L2_gnn_We"])
            ld(w_ekv[0:16, 64:128], w["L2_gnn_We"])
            ld(w_skip[0:64, :], w["L2_gnn_Wskip"])
            for m, n in ((w_e1, "We1"), (w_e2, "We2"), (w_n, "Wn"), (w_c, "Wc"), (w_o, "Wo")):
                ld(m[0:64, :], w["L3_gnn_" + n])
            ld(w_oT[0:64, :], w["WoT"])
            sp_rows = (("L2_gnn_bk", 0), ("L2_gnn_bv", 64))
            for n, c in sp_rows:
                ld(RW[0][0:1, c:c + 64], w[n].unsqueeze(0))
                ld(RW[1][0:1, c:c + 64], w["L2_gnn_be"].unsqueeze(0))
            for name, a in (("bmsg", "L0_gnn_b_msg"), ("bupd", "L0_gnn_b_upd"), ("g0", "L0_gnn_gamma"),
                            ("b0", "L0_gnn_beta"), ("bp", "L1_gnn_bp"), ("g1", "L1_gnn_gamma"),
                            ("b1", "L1_gnn_beta"), ("bq", "L2_gnn_bq"), ("bskip", "L2_gnn_bskip"),
                            ("g2", "L2_gnn_gamma"), ("b2", "L2_gnn_beta_bn"), ("be1", "L3_gnn_be1"),
                            ("be2", "L3_gnn_be2"), ("bn", "L3_gnn_bn"), ("bc", "L3_gnn_bc"), ("bo", "L3_gnn_bo")):
                ld(v[name][0:64, :], w[a].unsqueeze(1))
                ld(v[name][64:128, :], w[a].unsqueeze(1))
            wb = w["L2_gnn_Wbeta"]
            for k, name in enumerate(("wb1", "wb2", "wb3")):
                ld(v[name][0:64, :], wb[64 * k:64 * k + 64, :])
                ld(v[name][64:128, :], wb[64 * k:64 * k + 64, :])

            assert loaded[0] == NWDMA_TOTAL, loaded
            d2, s2 = dst.rearrange("(r c) -> r c", c=W), src.rearrange("(r c) -> r c", c=W)
            DI, DP, DN, SI = (t[0:NB, 0:W].bitcast(I32) for t in (CT[0], CT[1], CT[2], CT[3]))
            sp.wait_ge(built, 2)
            sp.dma_start(DI, d2).then_inc(pdma, 16)
            sp.dma_start(SI, s2).then_inc(pdma, 16)
            sp.dma_start(DP[:, 1:W], d2[:, 0:W - 1]).then_inc(pdma, 16)
            sp.dma_start(DP[1:NB, 0:1], d2[0:NB - 1, W - 1:W], allow_slow_non_contiguous=True).then_inc(pdma, 16)
            sp.dma_start(DN[:, 0:W - 1], d2[:, 1:W]).then_inc(pdma, 16)
            sp.dma_start(DN[0:NB - 1, W - 1:W], d2[1:NB, 0:1], allow_slow_non_contiguous=True).then_inc(pdma, 16)
            sp.wait_ge(built, 3)
            sp.dma_start(MAP.rearrange("(p n) k -> p (n k)", p=MP),
                         MAPBUF[0:MP, :]).then_inc(pdma, 16)
            sp.wait_ge(masks_ready, 1)
            for k, t in enumerate((Y[0], Y[1], Y[2], Y[3], H[0], H[1])):
                sp.dma_start(MASKS[k, :].rearrange("(r c) -> r c", c=W), t[0:NB, 0:W]).then_inc(pdma, 16)
            sp.wait_ge(pdma, 16 * 13)
            sp.wait_ge(bias_row, 1)
            sp.dma_start(w_ekv[16:17, :], RW[0][0:1, 0:128]).then_inc(bias_row_in, 16)
            sp.wait_ge(bias_row_in, 16)

            def first_credit(P, n):
                for l in range(L):
                    sp.sem_inc(P.s[l], 1)
                    if n:
                        sp.sem_inc(P.store[l], 16 * n)

            sp.wait_ge(wdone, 1)
            first_credit(P0, 1)

            def loads0(i, l):
                sp.dma_start(MA[l][64:128, :], mask_of(SAME, 64, i, l)).then_inc(P0.load[l], 16)

            def waited(P, i, l, stage):
                sp.wait_ge(P.s[l], P.at(i, stage))
                sp.nop(nofuse=True)

            def run(P, loads, used, stores, n=1):
                for l in range(L):
                    loads(0, l)
                with sp.Fori(0, IT - 1) as i:
                    for l in range(L):
                        waited(P, i, l, used)
                        loads(i + 1, l)
                    for l in range(L):
                        stores(i, l)
                for l in range(L):
                    stores(IT - 1, l)

            def stores0(i, l):
                waited(P0, i, l, "rows")
                sp.dma_start(rows_of(T1, N, i, l), ROWS[l][0:TE, 0:J * D].rearrange("p (j c) -> p j c", j=J))\
                    .then_inc(P0.store[l], 16)

            run(P0, loads0, "agg", stores0)

            wait_phase_done(sp, P0)
            sp.wait_ge(map_done, 1)
            sp.dma_start(MAPBUF[0:MP, :], MAP.rearrange("(p n) k -> p (n k)", p=MP)).then_inc(noe_dma, 16)
            sp.wait_ge(noe_ready, 1)
            sp.dma_start(NOE.rearrange("(p n) -> p n", p=MP), NOEBUF[0:MP, :]).then_inc(noe_dma, 16)
            sp.wait_ge(noe_dma, 32)
            first_credit(PD, 6)

            def loadsD(i, l):
                for half in range(2):
                    hs = slice(64 * half, 64 * half + 64)
                    sp.dma_start(CT[l][hs, :], cols_of(xT, i, l, base=half * (N // 2))).then_inc(PD.load[l], 16)
                    b = blk(i, l, False)
                    sp.dma_start(MA[l][hs, :], NOE[bass.ds(half * (N // 2) + b * W, W)].unsqueeze(0)
                                 .to_broadcast([64, W])).then_inc(PD.load[l], 16)

            def storesD(i, l):
                waited(PD, i, l, "rows1")
                r1 = TILE[l][0:TE, :].rearrange("p (j h c) -> p h j c", j=J, h=2)
                r3 = ROWS[l][0:TE, :].rearrange("p (j h c) -> p h j c", j=J, h=2)
                for half in range(2):
                    sp.dma_start(rows_of(T1, half * (N // 2), i, l), r1[:, half]).then_inc(PD.store[l], 16)
                waited(PD, i, l, "rows3")
                for half in range(2):
                    sp.dma_start(rows_of(T2, half * (N // 2), i, l), r3[:, half, :, 0:D]).then_inc(PD.store[l], 16)
                    sp.dma_start(rows_of(T3, half * (N // 2), i, l), r3[:, half]).then_inc(PD.store[l], 16)

            run(PD, loadsD, "um", storesD, 6)

            wait_phase_done(sp, PD)
            first_credit(P1, 1)

            def own(tile, T, c, i, l, back=False):
                return (tile[l][0:TE, :].rearrange("p (j c) -> p j c", j=J)[:, :, 0:c],
                        rows_of(T, N, i, l, back, 0, c))

            def loads1(i, l):
                sp.dma_start(*own(TILE, T1, D, i, l, True)).then_inc(P1.load[l], 16)
                sp.dma_start(MA[l][:, :], mask_of(SAMEN, 128, i, l, True)).then_inc(P1.load[l], 16)
                sp.dma_start(MB[l][0:64, :], mask_of(LAST, 64, i, l, True)).then_inc(P1.load[l], 16)
                sp.dma_start(MC[l][0:8, :], mask_of(NEGN, 8, i, l, True)).then_inc(P1.load[l], 16)
                sp.dma_start(EA[l][0:16, :], cols_of(ea16T, i, l, True)).then_inc(P1.load[l], 16)

            def stores1(i, l):
                waited(P1, i, l, "rows")
                sp.dma_start(rows_of(T2, N, i, l, True), ROWS[l][0:TE, 0:J * D].rearrange("p (j c) -> p j c", j=J))\
                    .then_inc(P1.store[l], 16)

            run(P1, loads1, "eas", stores1)

            wait_phase_done(sp, P1)
            first_credit(P2, 1)

            def loads2(i, l):
                sp.dma_start(*own(TILE, T2, D, i, l)).then_inc(P2.load[l], 16)
                sp.dma_start(MA[l][0:64, :], mask_of(SAME, 64, i, l)).then_inc(P2.load[l], 16)
                sp.dma_start(MB[l][0:64, :], mask_of(FIRST, 64, i, l)).then_inc(P2.load[l], 16)
                sp.dma_start(MC[l][0:8, :], mask_of(NEGP, 8, i, l)).then_inc(P2.load[l], 16)
                sp.dma_start(MD[l][64:128, :], mask_of(LAST, 64, i, l)).then_inc(P2.load[l], 16)
                sp.dma_start(EA[l][0:16, :], cols_of(ea16T, i, l)).then_inc(P2.load[l], 16)

            def stores2(i, l):
                waited(P2, i, l, "rows")
                sp.dma_start(rows_of(T3, N, i, l), ROWS[l][0:TE, 0:J * 128].rearrange("p (j c) -> p j c", j=J))\
                    .then_inc(P2.store[l], 16)

            run(P2, loads2, "um", stores2)

            wait_phase_done(sp, P2)
            first_credit(P4, 2)

            def loads4(i, l):
                for half, t in enumerate((TILE, TILEO)):
                    sp.dma_start(t[l][0:TE, :].rearrange("p (j c) -> p j c", j=J), rows_of(T3, half * (N // 2), i, l))\
                        .then_inc(P4.load[l], 16)

            def stores4(i, l):
                waited(P4, i, l, "rows")
                r = ROWS[l][0:TE, 0:J * 128].rearrange("p (j h c) -> p h j c", j=J, h=2)
                for half in range(2):
                    sp.dma_start(rows_of(out, half * (N // 2), i, l), r[:, half]).then_inc(P4.store[l], 16)

            run(P4, loads4, "oT", stores4, 2)

            wait_phase_done(sp, P4)
            first_credit(P3, 0)

            def loads3(i, l):
                sp.dma_start(*own(TILEO, T3, 128, i, l)).then_inc(P3.load[l], 16)
                sp.dma_start(MA[l][0:64, :], mask_of(SAME, 64, i, l)).then_inc(P3.load[l], 16)
                sp.dma_start(MB[l][0:64, :], cols_of(ea64T, i, l)).then_inc(P3.load[l], 16)

            run(P3, loads3, "agg", lambda i, l: None)
            wait_phase_done(sp, P3)

        @block.gpsimd
        def _(g):
            n = [0]

            def step(ins):
                n[0] += 1
                ins.then_inc(built_pool, 1)
                g.wait_ge(built_pool, n[0])

            step(g.memset(WALL[:, :], 0.0))
            step(g.memset(VEC[:, :], 0.0))
            step(g.memset(v["m64"], -LN2))
            step(g.memset(v["eps"], EPS))
            step(g.memset(v["tiny"], 1e-16))
            for l in range(L):
                step(g.memset(EA[l][0:32, :], 1.0))
            g.sem_inc(built, 1)
            step(g.memset(CT[1][0:NB, 0:W].bitcast(I32), -1))
            step(g.memset(CT[2][0:NB, 0:W].bitcast(I32), -1))
            g.sem_inc(built, 1)
            step(g.iota(MAPBUF[0:MP, :].rearrange("p (n k) -> p n k", k=2), pattern=[[1, MN], [0, 2]], base=0,
                        channel_multiplier=MN))
            g.sem_inc(built, 1)
            step(g.iota(MAPV[:, :, 0], pattern=[[TE, NT]], base=N, channel_multiplier=1))
            step(g.iota(CO[0][0:NB, 0:W].bitcast(I32), pattern=[[1, W]], base=0, channel_multiplier=W))
            step(g.memset(IDN[:, :], 0.0))
            step(g.affine_select(out=IDN[:, :], in_=IDN[:, :], compare_op=ALU.not_equal, fill=1.0, base=0,
                                 pattern=[[-1, 128]], channel_multiplier=1))
            step(g.memset(AVG[:, :], 0.0))
            step(g.memset(AVG[0:64, 0:64], 1.0 / D))
            step(g.memset(AVG[64:128, 64:128], 1.0 / D))
            step(g.memset(ONES[:, :], 1.0))
            step(g.memset(CAR[:, :], 0.0))

            def band(t, pattern, mult, base):
                step(g.affine_select(out=t, in_=t, compare_op=ALU.is_ge, fill=0.0, base=base, pattern=pattern,
                                     channel_multiplier=mult))

            step(g.memset(B4[:, :], 1.0))
            band(B4[:, :], [[1, 256]], -64, 0)
            band(B4[:, :], [[-1, 256]], 64, 63)
            step(g.memset(B8[:, :], 1.0))
            b8 = B8[:, :].rearrange("p (a c) -> p a c", a=2)
            band(b8, [[0, 2], [1, 64]], -8, 0)
            band(b8, [[0, 2], [-1, 64]], 8, 7)
            step(g.memset(HSEL[:, :], 1.0))
            band(HSEL[:, :], [[-8, 8]], 1, 0)
            band(HSEL[:, :], [[8, 8]], -1, 7)
            step(g.memset(a_cnt[0:32, :], 1.0))
            band(a_cnt[0:32, :], [[0, 4]], 1, -16)
            band(a_cnt[0:32, :], [[0, 4]], -1, 16)
            g.sem_inc(built, 1)

            def free(P, i, l, stage):
                g.wait_ge(P.s[l], P.at(i, stage))
                g.nop(nofuse=True)

            g.wait_ge(indices_ready, 1)
            g.wait_ge(pdma, 16 * 13)
            cnt = [0]

            def ring(i, l, pairs, base):
                for k, (o, a) in enumerate(pairs):
                    g.tensor_copy(o, a).then_inc(idx_ready, 1)

            def scat_map(i, l, value):
                b = blk(i, l, False)
                g.tensor_copy(RINGI[:, l, 0, :], SCATI[:, bass.ds(b * J, J)]).then_inc(idx_ready, 1)
                g.tensor_copy(RINGV[:, l, :, :], MAPV[:, bass.ds(b * J, J), :]).then_inc(idx_ready, 1)
                g.wait_ge(idx_ready, value)
                g.nop(nofuse=True)
                for j in range(J):
                    g.indirect_dma_start(MAP, bass.IndirectOffsetOnAxis(RINGI[:, l, 0, j:j + 1], 0),
                                         RINGV[:, l, j, :], None, bounds_check=N - 1, oob_is_err=False)\
                        .then_inc(map_moved[l], 16)

            for l in range(L):
                scat_map(0, l, 2 * (l + 1))
            with g.Fori(0, IT - 1) as i:
                for l in range(L):
                    g.wait_ge(map_moved[l], i * (16 * J) + 16 * J)
                    g.nop(nofuse=True)
                    scat_map(i + 1, l, i * (2 * L) + 2 * L + 2 * (l + 1))
            for l in range(L):
                g.wait_ge(map_moved[l], 16 * J * IT)
            g.sem_inc(map_done, 1)
            done = 2 * NB

            def gather(P, tile, c0, c1, table, l, k):
                for j in range(J):
                    g.indirect_dma_start(tile[l][0:TE, j * 128 + c0:j * 128 + c1], None, table,
                                         bass.IndirectOffsetOnAxis(RINGI[:, l, k, j:j + 1], 0)).then_inc(P.got[l], 16)

            def gathers(P, base, used, sets, back=False, scatter=None):
                def one(i, l, value):
                    b = blk(i, l, back)
                    for k, (idx, *_) in enumerate(sets):
                        g.tensor_copy(RINGI[:, l, k, :], idx(b)).then_inc(idx_ready, 1)
                    g.wait_ge(idx_ready, value)
                    g.nop(nofuse=True)
                    for k, (_, tile, c0, c1, table) in enumerate(sets):
                        gather(P, tile, c0, c1, table, l, k)

                m = len(sets)
                for l in range(L):
                    one(0, l, base + m * (l + 1))
                with g.Fori(0, IT - 1) as i:
                    for l in range(L):
                        free(P, i, l, used)
                        one(i + 1, l, i * (m * L) + (base + m * L + m * (l + 1)))
                return base + m * NB

            done = gathers(P0, done, "tT", [
                (lambda b: DSTI[:, bass.ds(b * J, J)], TILE, 0, 64, x),
                (lambda b: SRCI[:, bass.ds(b * J, J)], TILE, 64, 128, x)])

            GR = L * J

            def map_gather(i, value, got):
                g.tensor_copy(RINGI[:, :, 0, :], SRCI[:, bass.ds(i * GR, GR)].rearrange("p (l j) -> p l j", l=L))\
                    .then_inc(idx_ready, 1)
                g.wait_ge(idx_ready, value)
                g.nop(nofuse=True)
                for l in range(L):
                    for j in range(J):
                        g.indirect_dma_start(RINGV[:, l, j, :], None, MAP,
                                             bass.IndirectOffsetOnAxis(RINGI[:, l, 0, j:j + 1], 0))\
                            .then_inc(map_got, 16)
                g.wait_ge(map_got, got)
                g.tensor_copy(MAPV[:, bass.ds(i * GR, GR), :].rearrange("p (l j) k -> p l j k", l=L), RINGV[:, :, :, :])\
                    .then_inc(map_copied, 1)

            for l in range(L):
                g.wait_ge(P0.got[l], 16 * 2 * J * IT)
            with g.Fori(0, IT) as i:
                map_gather(i, i + (done + 1), i * (16 * GR) + 16 * GR)
                g.wait_ge(map_copied, i + 1)
                g.nop(nofuse=True)
            done += IT

            wait_phase_done(g, PD)
            done = gathers(P1, done, "tT", [(lambda b: MAPV[:, bass.ds(b * J, J), 0], TILE, 64, 128, T1)], back=True)
            wait_phase_done(g, P1)
            done = gathers(P2, done, "tT", [(lambda b: MAPV[:, bass.ds(b * J, J), 1], TILE, 64, 128, T2)])
            wait_phase_done(g, P4)

            def one3(i, l, value):
                b = blk(i, l, False)
                g.tensor_copy(RINGI[:, l, 0, :], MAPV[:, bass.ds(b * J, J), 0]).then_inc(idx_ready, 1)
                g.wait_ge(idx_ready, value)
                g.nop(nofuse=True)
                gather(P3, TILE, 0, 128, T3, l, 0)

            def scatter3(i, l, value):
                g.tensor_copy(RINGI[:, l, 1, :], SCATI[:, bass.ds(blk(i, l, False) * J, J)]).then_inc(idx_ready, 1)
                g.wait_ge(idx_ready, value)
                g.nop(nofuse=True)
                g.wait_ge(P3.s[l], P3.at(i, "rows"))
                g.nop(nofuse=True)
                for j in range(J):
                    g.indirect_dma_start(out, bass.IndirectOffsetOnAxis(RINGI[:, l, 1, j:j + 1], 0),
                                         ROWS[l][0:TE, j * D:j * D + D], None, bounds_check=N - 1, oob_is_err=False)\
                        .then_inc(P3.store[l], 16)

            for l in range(L):
                g.sem_inc(rows_free[l], 1)
                one3(0, l, done + l + 1)
            base = done + L
            for l in range(L):
                free(P3, 0, l, "tT")
                one3(1, l, base + l + 1)
            for l in range(L):
                scatter3(0, l, base + L + l + 1)
            base += 2 * L

            def scattered(l, value):
                g.wait_ge(P3.store[l], value)
                g.nop(nofuse=True)
                g.sem_inc(rows_free[l], 1)

            with g.Fori(0, IT - 2) as i:
                for l in range(L):
                    free(P3, i + 1, l, "tT")
                    one3(i + 2, l, i * (2 * L) + (base + l + 1))
                for l in range(L):
                    scattered(l, i * (16 * J) + 16 * J)
                    scatter3(i + 1, l, i * (2 * L) + (base + L + l + 1))
            base += 2 * L * (IT - 2)
            for l in range(L):
                scattered(l, 16 * J * (IT - 1))
                scatter3(IT - 1, l, base + l + 1)

        @block.tensor
        def _(t):
            t.wait_ge(built, 4)

            def after(P, i, l, stage, odd=False):
                t.wait_ge(P.s[l], P.at(i, stage))
                if odd:
                    t.nop(nofuse=True)

            def mm(o, a, b, start=True, stop=True):
                return t.matmul(o, a, b, start=start, stop=stop)

            t.wait_ge(starts, 1)
            t.transpose(PA[0][0:1, 0:NB], CO[1][0:NB, W - 1:W], IDN[0:NB, 0:NB]).then_inc(ptr, 1)
            t.wait_ge(starts, 2)
            mm(PA[1][0:NB, 0:1], CO[2][0:1, 0:NB], ONES[0:1, 0:1]).then_inc(ptr, 1)
            t.wait_ge(starts, 3)
            for a, t_in in enumerate((S0[0], S0[1], S0[2], S0[3])):
                for j in range(J):
                    t.transpose(PB[a][0:TE, j * NB:(j + 1) * NB], t_in[0:NB, j * TE:(j + 1) * TE], IDN[0:NB, 0:NB])\
                        .then_inc(ptr, 1)

            t.wait_ge(wsem, 16 * NWDMA_TOTAL)
            t.wait_ge(derived, 1)
            for h in range(H1):
                hp = PA[0][0:64, 64 * h:64 * h + 64] if h % 2 == 0 else PA[0][64:128, 64 * h:64 * h + 64]
                mm(hp, wT[0:64, 64 * h:64 * h + 64], wp[0:64, 64 * h:64 * h + 64])
            for h in range(H1):
                mm(PB[0][0:64, 0:64], wT[0:64, 64 * h:64 * h + 64], wp[0:64, 64 * h:64 * h + 64],
                   start=h == 0, stop=h == H1 - 1)
            for h in range(H1):
                mm(PB[1][64:128, 0:64], wT[0:64, 64 * h:64 * h + 64], wp[0:64, 64 * h:64 * h + 64],
                   start=h == 0, stop=h == H1 - 1)
            for h in range(H1):
                hs = wT[0:64, 64 * h:64 * h + 64]
                mm(PB[1][64:128, 128 + h:129 + h], hs, att[0:64, h:h + 1])
                mm(PA[1][0:64, h:h + 1], hs, att[0:64, 4 + h:5 + h])
                mm(PA[1][0:64, 4 + h:5 + h], hs, att[0:64, h:h + 1], start=True, stop=False)
                mm(PA[1][0:64, 4 + h:5 + h], hs, att[0:64, 4 + h:5 + h], start=False, stop=True)
                mm(PA[1][0:16, 8 + h:9 + h], weT[0:64, 16 * h:16 * h + 16], att[0:64, 8 + h:9 + h])
            for half, o in ((0, PA[2][0:64, 0:1]), (1, PA[2][64:128, 0:1])):
                for h in range(H1):
                    mm(o, wp[0:64, 64 * h:64 * h + 64], v[f"hb{h}"][0:64, :], start=h == 0, stop=h == H1 - 1)
            mm(PA[2][0:64, 1:2], w_e2[0:64, :], v["m64"][0:64, :])
            mm(PA[2][0:64, 2:3], w_o[0:64, :], v["m64"][0:64, :])
            mm(PA[2][64:128, 2:3], w_o[0:64, :], v["m64"][0:64, :])
            mm(PA[3][0:64, 0:64], w_oT[0:64, :], CEN[0:64, 0:64]).then_inc(ptr, 1)
            t.wait_ge(derived, 2)
            mm(PB[2][:, 0:1], CEN[:, :], v["t0"])
            mm(PB[3][0:64, 0:1], WOCEN[0:64, :], v["sp0"][0:64, :])
            mm(PB[3][64:128, 0:1], WOCEN[0:64, :], v["sp0"][0:64, :]).then_inc(ptr, 1)

            def tileT(P, i, l, tile=TILE, dst_=PA, stage="tT", loads=1, got=None):
                for j in range(J):
                    last = t.transpose(dst_[l][:, j * TE:(j + 1) * TE], tile[l][0:TE, j * 128:(j + 1) * 128],
                                       IDN[0:TE, 0:TE])
                last.then_inc(P.s[l], 1)

            def arrived(P, i, l, loads, gathers):
                if loads:
                    t.wait_ge(P.load[l], i * (16 * loads) + 16 * loads)
                if gathers:
                    t.wait_ge(P.got[l], i * (16 * gathers) + 16 * gathers)

            def ln_pe(P, i, k, prev, y, rows):
                rs = slice(0, rows)
                for l in range(L):
                    after(P, i, l, prev, rows == 64)
                    mm(PB[l][rs, 0:W], CEN[rs, rs], y[l][rs, :]).then_inc(P.s[l], 1)
                for l in range(L):
                    after(P, i, l, f"sq{k}", rows == 64)
                    mm(PA[l][rs, 0:W], AVG[rs, rs], SQ[l][rs, :]).then_inc(P.s[l], 1)

            def outT(P, i, prev, stage, y, rows, pool=PA):
                for l in range(L):
                    after(P, i, l, prev, True)
                    for j in range(J):
                        last = t.transpose(pool[l][0:TE, j * rows:(j + 1) * rows], y[l][0:rows, j * TE:(j + 1) * TE],
                                           IDN[0:rows, 0:rows])
                    last.then_inc(P.s[l], 1)

            with t.Fori(0, IT) as i:
                for l in range(L):
                    arrived(P0, i, l, 0, 2 * J)
                    t.wait_ge(P0.s[l], i * len(P0.chain.stages) + 1)
                    tileT(P0, i, l)
                for l in range(L):
                    after(P0, i, l, "cat")
                    mm(PB[l][64:128, 0:W], w_msg, CT[l][:, :]).then_inc(P0.s[l], 1)
                for l in range(L):
                    after(P0, i, l, "agg")
                    mm(PA[l][0:64, 0:W], w_upd, CT[l][:, :]).then_inc(P0.s[l], 1)
                ln_pe(P0, i, 1, "updrelu", Y, 64)
                ln_pe(P0, i, 2, "res1", Y, 64)
                outT(P0, i, "norm2", "outT", Y, 64)

            with t.Fori(0, IT) as i:
                for l in range(L):
                    arrived(PD, i, l, 4, 0)
                    t.wait_ge(PD.s[l], i * len(PD.chain.stages) + 1)
                    mm(PA[l][:, 0:W], w_updb, CT[l][:, :]).then_inc(PD.s[l], 1)
                ln_pe(PD, i, 1, "updrelu", Y, 128)
                ln_pe(PD, i, 2, "res1", Y, 128)
                outT(PD, i, "norm2", "outT1", Y, 128)
                for l in range(L):
                    after(PD, i, l, "rows1")
                    mm(PA[l][:, 0:W], g_sumb, Y[l][:, :]).then_inc(PD.s[l], 1)
                ln_pe(PD, i, 3, "elu_res", H, 128)
                ln_pe(PD, i, 4, "res3", H, 128)
                outT(PD, i, "norm4", "outT2", H, 128)
                for l in range(L):
                    after(PD, i, l, "rows2")
                    mm(PA[l][:, 0:W], w_skipb, H[l][:, :]).then_inc(PD.s[l], 1)
                for l in range(L):
                    after(PD, i, l, "xrb")
                    mm(PB[l][:, 0:W], w_zb, CO[l][:, :]).then_inc(PD.s[l], 1)
                outT(PD, i, "u", "outT3", Y, 128)

            with t.Fori(0, IT) as i:
                for l in range(L):
                    arrived(P1, i, l, 5, J)
                    t.wait_ge(P1.s[l], i * len(P1.chain.stages) + 1)
                    tileT(P1, i, l)
                for l in range(L):
                    after(P1, i, l, "hold")
                    mm(PB[l][0:4, 0:W], a_log, CT[l][:, :], stop=False)
                    mm(PB[l][0:4, 0:W], a_edge[0:17, :], EA[l][0:17, :], start=False).then_inc(P1.s[l], 1)
                for l in range(L):
                    after(P1, i, l, "eas")
                    mm(PA[l][:, 0:W], DUPD[:, :], CT[l][:, :]).then_inc(P1.s[l], 1)
                for hp in range(2):
                    sel = B4[:, 128 * hp:128 * hp + 128]
                    for l in range(L):
                        after(P1, i, l, ("dx", "s0")[hp])
                        mm(PB[l][:, 0:W], sel, RW[l][0:4, W:2 * W]).then_inc(P1.s[l], 1)
                    for l in range(L):
                        after(P1, i, l, ("wd0", "wd1")[hp])
                        mm(PA[l][:, 0:W], sel, RW[l][0:4, 0:W]).then_inc(P1.s[l], 1)
                for l in range(L):
                    after(P1, i, l, "s1", True)
                    mm(PA[l][0:4, 0:W], a_edge[0:17, :], EAS[l][0:17, :])
                    mm(PB[l][0:4, 0:W], a_cnt[0:17, :], EAS[l][0:17, :]).then_inc(P1.s[l], 1)
                for l in range(L):
                    after(P1, i, l, "emean", True)
                    mm(PA[l][0:4, 0:W], a_self[0:64, :], CT[l][0:64, :]).then_inc(P1.s[l], 1)
                for hp in range(2):
                    sel = B4[:, 128 * hp:128 * hp + 128]
                    for l in range(L):
                        after(P1, i, l, ("fac", "sf0")[hp])
                        mm(PB[l][:, 0:W], sel, Y[l][0:4, :]).then_inc(P1.s[l], 1)
                for l in range(L):
                    after(P1, i, l, "sf1")
                    mm(PA[l][0:64, 0:W], g_cat[:, 0:64], S0[l][:, :], stop=False)
                    mm(PA[l][0:64, 0:W], g_cat[:, 64:128], S1[l][:, :], start=False, stop=False)
                    mm(PA[l][0:64, 0:W], g_sum[0:64, :], CT[l][0:64, :], start=False).then_inc(P1.s[l], 1)
                ln_pe(P1, i, 3, "elu_res", H, 64)
                ln_pe(P1, i, 4, "res3", H, 64)
                outT(P1, i, "norm4", "outT", H, 64)

            with t.Fori(0, IT) as i:
                for l in range(L):
                    arrived(P2, i, l, 6, J)
                    t.wait_ge(P2.s[l], i * len(P2.chain.stages) + 1)
                    tileT(P2, i, l)
                for l in range(L):
                    after(P2, i, l, "hold", True)
                    mm(PA[l][0:64, 0:W], w_q[0:64, :], CT[l][0:64, :]).then_inc(P2.s[l], 1)
                for l in range(L):
                    after(P2, i, l, "qb")
                    mm(PB[l][:, 0:W], w_kv, CT[l][:, :], stop=False)
                    mm(PB[l][:, 0:W], w_ekv[0:17, :], EA[l][0:17, :], start=False).then_inc(P2.s[l], 1)
                for l in range(L):
                    after(P2, i, l, "vc", True)
                    mm(PA[l][0:8, 0:W], HSEL[:, :], H[l][0:64, :]).then_inc(P2.s[l], 1)
                for l in range(L):
                    after(P2, i, l, "den")
                    mm(PA[l][:, 0:W], B8[:, :], RW[l][0:8, W:2 * W]).then_inc(P2.s[l], 1)
                for l in range(L):
                    after(P2, i, l, "wv")
                    mm(PA[l][:, 0:W], B8[:, :], RW[l][0:8, 0:W]).then_inc(P2.s[l], 1)
                for l in range(L):
                    after(P2, i, l, "drec")
                    mm(PA[l][:, 0:W], B8[:, :], SQ[l][0:8, :]).then_inc(P2.s[l], 1)
                for l in range(L):
                    after(P2, i, l, "o", True)
                    mm(PB[l][0:64, 0:W], w_skip[0:64, :], CT[l][0:64, :]).then_inc(P2.s[l], 1)
                for l in range(L):
                    after(P2, i, l, "xrb")
                    mm(PA[l][64:128, 0:W], w_z, CO[l][:, :])
                    mm(PB[l][64:128, 0:W], SUBX[:, :], CO[l][:, :]).then_inc(P2.s[l], 1)
                outT(P2, i, "uq", "outT", CT, 128)

            def ssp_pe(P, i, prev, weight, y, o):
                for l in range(L):
                    after(P, i, l, prev, True)
                    mm(o[l][0:64, 0:W], weight[0:64, :], y[l][0:64, :]).then_inc(P.s[l], 1)

            def x3_pe(P, i):
                for l in range(L):
                    after(P, i, l, "cat")
                    tileT(P, i, l, TILEO, PB)
                for l in range(L):
                    after(P, i, l, "olrelu")
                    mm(PB[l][0:64, 0:W], CEN2[:, :], CT[l][:, :])
                    mm(PB[l][64:128, 0:W], CEN2[:, :], CO[l][:, :]).then_inc(P.s[l], 1)
                for l in range(L):
                    after(P, i, l, "sq1")
                    mm(PA[l][:, 0:W], AVG[:, :], SQ[l][:, :]).then_inc(P.s[l], 1)

            t.wait_ge(fin, 1)
            mm(PA[0][64:128, 0:2], ADD2[:, :], SUMS[:, 0:2]).then_inc(bn_done, 1)
            t.wait_ge(fin, 4)

            with t.Fori(0, IT) as i:
                for l in range(L):
                    arrived(P4, i, l, 2, 0)
                    t.wait_ge(P4.s[l], i * len(P4.chain.stages) + 1)
                    tileT(P4, i, l)
                x3_pe(P4, i)
                for l in range(L):
                    after(P4, i, l, "norm1")
                    mm(PB[l][:, 0:W], CEN[:, :], Y[l][:, :]).then_inc(P4.s[l], 1)
                for l in range(L):
                    after(P4, i, l, "sq2")
                    mm(PA[l][:, 0:W], AVG[:, :], SQ[l][:, :]).then_inc(P4.s[l], 1)
                outT(P4, i, "norm2", "outT", Y, 128)

            with t.Fori(0, IT) as i:
                for l in range(L):
                    arrived(P3, i, l, 3, J)
                    t.wait_ge(P3.s[l], i * len(P3.chain.stages) + 1)
                    tileT(P3, i, l)
                x3_pe(P3, i)
                ssp_pe(P3, i, "norm1", w_e1, MB, PA)
                ssp_pe(P3, i, "f1s", w_e2, H, PB)
                ssp_pe(P3, i, "f2s", w_n, Y, PA)
                ssp_pe(P3, i, "agg", w_c, S0, PB)
                for l in range(L):
                    after(P3, i, l, "cs")
                    mm(PA[l][0:64, 0:W], WOCEN[:, :], Y[l][:, :]).then_inc(P3.s[l], 1)
                for l in range(L):
                    after(P3, i, l, "sq2", True)
                    mm(PB[l][0:64, 0:W], AVG[0:64, 0:64], SQ[l][0:64, :]).then_inc(P3.s[l], 1)
                outT(P3, i, "norm2", "outT", Y, 64)

        @block.scalar
        def _(a):
            a.preload_act_table_set("natural_log_exp_and_others")

            def do(P, i, l, prev, o, in_, f, **kw):
                a.wait_ge(P.s[l], P.at(i, prev))
                a.activation(o, in_, f, **kw).then_inc(P.s[l], 1)

            def each(P, i, prev, o, in_, f, **kw):
                for l in range(L):
                    do(P, i, l, prev, o(l), in_(l), f, **kw)

            a.wait_ge(wsem, 16 * NWDMA_TOTAL)
            a.activation(v["sp0"], v["bc"], ACT.Abs).then_inc(bc_steps, 1)
            a.wait_ge(bc_steps, 1)
            a.activation(v["sp0"], v["sp0"], ACT.Exp, scale=-1.0).then_inc(bc_steps, 1)
            a.wait_ge(bc_steps, 2)
            a.activation(v["sp0"], v["sp0"], ACT.Ln, bias=1.0).then_inc(bc_steps, 1)

            def ln_act(P, i, k, rows):
                rs = slice(0, rows)
                each(P, i, f"cen{k}", lambda l: SQ[l][rs, :], lambda l: PB[l][rs, 0:W], ACT.Square)
                each(P, i, f"var{k}", lambda l: SQ[l][rs, :], lambda l: PA[l][rs, 0:W], ACT.Ln, bias=v["eps"][rs, :])
                each(P, i, f"ln{k}", lambda l: SQ[l][rs, :], lambda l: SQ[l][rs, :], ACT.Exp, scale=-0.5)

            a.wait_ge(built, 4)

            with a.Fori(0, IT) as i:
                each(P0, i, "msg", lambda l: Y[l][64:128, :], lambda l: PB[l][64:128, 0:W], ACT.Relu,
                     bias=v["bmsg"][64:128, :])
                each(P0, i, "upd", lambda l: Y[l][0:64, :], lambda l: PA[l][0:64, 0:W], ACT.Relu,
                     bias=v["bupd"][0:64, :])
                ln_act(P0, i, 1, 64)
                ln_act(P0, i, 2, 64)

            def gate(P, i, rs):
                each(P, i, "zc", lambda l: SQ[l][rs, :], lambda l: SQ[l][rs, :], ACT.Exp)
                each(P, i, "ze", lambda l: SQ[l][rs, :], lambda l: SQ[l][rs, :], ACT.Ln, bias=1.0)
                each(P, i, "zl", lambda l: SQ[l][rs, :], lambda l: SQ[l][rs, :], ACT.Exp, scale=-1.0)

            def sums(P, i, rs, k):
                for l in range(L):
                    b = blk(i, l, False)
                    a.wait_ge(P.s[l], P.at(i, "um"))
                    a.activation(WD[l][rs, :], SQ[l][rs, :], ACT.Copy,
                                 accum_out=STAT[rs, k, bass.ds(b, 1)]).then_inc(P.s[l], 1)
                for l in range(L):
                    b = blk(i, l, False)
                    a.wait_ge(P.s[l], P.at(i, "us"))
                    a.activation(WD[l][rs, :], SQ[l][rs, :], ACT.Square,
                                 accum_out=STAT[rs, k + 1, bass.ds(b, 1)]).then_inc(P.s[l], 1)

            full = slice(0, 128)
            lo, hi = slice(0, 64), slice(64, 128)
            with a.Fori(0, IT) as i:
                each(PD, i, "upd", lambda l: Y[l][:, :], lambda l: PA[l][:, 0:W], ACT.Relu, bias=v["bupd"])
                ln_act(PD, i, 1, 128)
                ln_act(PD, i, 2, 128)
                for l in range(L):
                    a.wait_ge(PD.store[l], i * (16 * 6) + 16 * 6)
                    do(PD, i, l, "outT1", TILE[l][0:TE, :], PA[l][0:TE, 0:512], ACT.Copy)
                each(PD, i, "elu_n", lambda l: SQ[l][:, :], lambda l: SQ[l][:, :], ACT.Exp)
                ln_act(PD, i, 3, 128)
                ln_act(PD, i, 4, 128)
                each(PD, i, "outT2",
                     lambda l: ROWS[l][0:TE, :].rearrange("p (jh k c) -> p jh k c", k=2, c=D)[:, :, 0, :],
                     lambda l: PA[l][0:TE, 0:512].rearrange("p (jh c) -> p jh c", c=D), ACT.Copy)
                each(PD, i, "xr", lambda l: CO[l][:, :], lambda l: PA[l][:, 0:W], ACT.Identity, bias=v["bskip"])
                gate(PD, i, full)
                each(PD, i, "outT3",
                     lambda l: ROWS[l][0:TE, :].rearrange("p (jh k c) -> p jh k c", k=2, c=D)[:, :, 1, :],
                     lambda l: PA[l][0:TE, 0:512].rearrange("p (jh c) -> p jh c", c=D), ACT.Copy)
                sums(PD, i, full, 0)

            with a.Fori(0, IT) as i:
                each(P1, i, "logit", lambda l: Y[l][0:4, :], lambda l: PB[l][0:4, 0:W], ACT.Copy)
                each(P1, i, "dw", lambda l: RW[l][0:4, :], lambda l: RW[l][0:4, :], ACT.Exp)
                each(P1, i, "dxs", lambda l: CO[l][:, :], lambda l: PA[l][:, 0:W], ACT.Copy)
                each(P1, i, "esum", lambda l: SQ[l][0:4, :], lambda l: PB[l][0:4, 0:W], ACT.Ln)
                each(P1, i, "lcnt", lambda l: SQ[l][0:4, :], lambda l: SQ[l][0:4, :], ACT.Exp, scale=-1.0)
                each(P1, i, "g2", lambda l: RW[l][0:4, :], lambda l: RW[l][0:4, :], ACT.Exp)
                each(P1, i, "dsum", lambda l: Y[l][0:4, :], lambda l: Y[l][0:4, :], ACT.Ln)
                each(P1, i, "dln", lambda l: Y[l][0:4, :], lambda l: Y[l][0:4, :], ACT.Exp, scale=-1.0)
                each(P1, i, "elu_n", lambda l: SQ[l][lo, :], lambda l: SQ[l][lo, :], ACT.Exp)
                ln_act(P1, i, 3, 64)
                ln_act(P1, i, 4, 64)

            with a.Fori(0, IT) as i:
                each(P2, i, "q", lambda l: Y[l][lo, :], lambda l: PA[l][lo, 0:W], ACT.Identity, bias=v["bq"][lo, :])
                each(P2, i, "qk", lambda l: WD[l][hi, :], lambda l: PB[l][hi, 0:W], ACT.Copy)
                each(P2, i, "logit", lambda l: SQ[l][0:8, :], lambda l: PA[l][0:8, 0:W], ACT.Copy,
                     scale=float(H2) ** -0.5)
                each(P2, i, "dw", lambda l: RW[l][0:8, :], lambda l: RW[l][0:8, :], ACT.Exp)
                each(P2, i, "s", lambda l: SQ[l][0:8, :], lambda l: Y[l][0:8, :], ACT.Ln,
                     bias=v["tiny"][0:8, :])
                each(P2, i, "dln", lambda l: SQ[l][0:8, :], lambda l: SQ[l][0:8, :], ACT.Exp, scale=-1.0)
                each(P2, i, "xr", lambda l: CO[l][lo, :], lambda l: PB[l][lo, 0:W], ACT.Identity,
                     bias=v["bskip"][lo, :])
                gate(P2, i, hi)
                sums(P2, i, hi, 2)

            a.wait_ge(fin, 4)
            a.activation(v["bs"][hi, :], v["var"][hi, :], ACT.Ln, bias=v["eps"][hi, :]).then_inc(fin, 1)
            a.wait_ge(fin, 5)
            a.activation(v["bs"][hi, :], v["bs"][hi, :], ACT.Exp, scale=-0.5).then_inc(fin, 1)

            with a.Fori(0, IT) as i:
                ln_act(P4, i, 1, 128)
                each(P4, i, "cen2", lambda l: H[l][:, :], lambda l: PB[l][:, 0:W], ACT.Identity, bias=v["cvec"])
                each(P4, i, "cb2", lambda l: SQ[l][:, :], lambda l: H[l][:, :], ACT.Square)
                each(P4, i, "var2", lambda l: SQ[l][:, :], lambda l: PA[l][:, 0:W], ACT.Ln, bias=v["eps"][:, :])
                each(P4, i, "ln2", lambda l: SQ[l][:, :], lambda l: SQ[l][:, :], ACT.Exp, scale=-0.5)

            def ssp_act(i, k, prev, pool, bias):
                each(P3, i, prev, lambda l: SQ[l][lo, :], lambda l: pool[l][lo, 0:W], ACT.Abs, bias=bias[lo, :])
                each(P3, i, f"{k}a", lambda l: SQ[l][lo, :], lambda l: SQ[l][lo, :], ACT.Exp, scale=-1.0)
                each(P3, i, f"{k}e", lambda l: SQ[l][lo, :], lambda l: SQ[l][lo, :], ACT.Ln, bias=1.0)

            with a.Fori(0, IT) as i:
                ln_act(P3, i, 1, 128)
                ssp_act(i, "f1", "f1", PA, v["be1"])
                ssp_act(i, "f2", "f2", PB, v["be2"])
                each(P3, i, "h", lambda l: WD[l][lo, :], lambda l: PA[l][lo, 0:W], ACT.Identity, bias=v["bn"][lo, :])
                ssp_act(i, "c", "c", PB, v["bc"])
                each(P3, i, "cen2", lambda l: H[l][lo, :], lambda l: PA[l][lo, 0:W], ACT.Identity,
                     bias=v["cb"][lo, :])
                each(P3, i, "cb2", lambda l: SQ[l][lo, :], lambda l: H[l][lo, :], ACT.Square)
                each(P3, i, "var2", lambda l: SQ[l][lo, :], lambda l: PB[l][lo, 0:W], ACT.Ln, bias=v["eps"][lo, :])
                each(P3, i, "ln2", lambda l: SQ[l][lo, :], lambda l: SQ[l][lo, :], ACT.Exp, scale=-0.5)

        @block.vector
        def _(d):
            chain = [0]

            def link(ins):
                chain[0] += 1
                ins.then_inc(dve_link, 1)
                d.wait_ge(dve_link, chain[0])

            R_ = slice(0, NB)
            i32 = lambda t: t[R_, 0:W].bitcast(I32)
            d.wait_ge(pdma, 16 * 7)
            link(d.tensor_tensor(Y[0][R_, :], i32(CT[0]), i32(CT[1]), ALU.is_equal))
            link(d.tensor_tensor(Y[2][R_, :], i32(CT[0]), i32(CT[2]), ALU.is_equal))
            link(d.tensor_scalar(Y[1][R_, :], Y[0][R_, :], -1.0, 1.0, ALU.mult, ALU.add))
            link(d.tensor_scalar(Y[3][R_, :], Y[2][R_, :], -1.0, 1.0, ALU.mult, ALU.add))
            link(d.tensor_scalar(H[0][R_, :], Y[1][R_, :], NEG, None, ALU.mult))
            link(d.tensor_scalar(H[1][R_, :], Y[3][R_, :], NEG, None, ALU.mult))
            d.sem_inc(masks_ready, 1)
            d.wait_ge(built, 4)
            link(d.tensor_copy(H[2][R_, :], i32(CO[0])))
            link(d.tensor_tensor(H[2][R_, :], H[2][R_, :], Y[1][R_, :], ALU.mult))
            link(d.tensor_tensor_scan(CO[1][R_, :], H[2][R_, :], H[2][R_, :], 0.0, ALU.max, ALU.max))
            d.sem_inc(starts, 1)
            d.wait_ge(ptr, 1)
            link(d.memset(CO[2][0:1, 0:1], 0.0))
            link(d.tensor_copy(CO[3][0:1, 0:NB], PA[0][0:1, 0:NB]))
            link(d.tensor_tensor_scan(CO[2][0:1, 1:NB + 1], CO[3][0:1, 0:NB], CO[3][0:1, 0:NB], 0.0, ALU.max, ALU.max))
            d.sem_inc(starts, 1)
            d.wait_ge(ptr, 2)
            link(d.tensor_copy(CAR[R_, 7:8], PA[1][R_, 0:1]))
            link(d.tensor_scalar(S0[3][R_, :], CO[1][R_, :], CAR[R_, 7:8], float(N), ALU.max, ALU.add))
            link(d.tensor_copy(S0[0][R_, :], i32(CT[3])))
            link(d.tensor_copy(S0[1][R_, :], i32(CT[0])))
            link(d.tensor_scalar(H[3][R_, :], Y[2][R_, :], FAR, None, ALU.mult))
            link(d.tensor_tensor(S0[2][R_, :], S0[1][R_, :], H[3][R_, :], ALU.add))
            d.sem_inc(starts, 1)
            for k, o in enumerate((SRCI[:, :], DSTI[:, :], SCATI[:, :], MAPV[:, :, 1])):
                d.wait_ge(ptr, 2 + J * (k + 1))
                link(d.tensor_copy(o.rearrange("p (b j) -> p j b", j=J),
                                   PB[k][0:TE, 0:J * NB].rearrange("p (j b) -> p j b", j=J)))
            d.sem_inc(indices_ready, 1)
            link(d.tensor_tensor(CEN[:, :], IDN[:, :], AVG[:, :], ALU.subtract))
            link(d.tensor_tensor(CEN2[:, :], CEN[:, 0:64], CEN[:, 64:128], ALU.add))
            link(d.tensor_tensor(ADD2[:, :], IDN[:, 0:64], IDN[:, 64:128], ALU.add))
            link(d.tensor_scalar(SUBX[0:64, :], ADD2[0:64, :], 1.0, None, ALU.mult))
            link(d.tensor_scalar(SUBX[64:128, :], ADD2[64:128, :], -1.0, None, ALU.mult))
            for c in (0, 64):
                link(d.tensor_scalar(DUPD[:, c:c + 64], SUBX[:, :], -1.0, None, ALU.mult))
            link(d.tensor_copy(WOCEN[64:128, :], CEN2[64:128, :]))
            d.wait_ge(wsem, 16 * NWDMA_TOTAL)
            d.sem_inc(derived, 1)
            link(d.tensor_tensor(v["wb"], v["wb2"], v["wb3"], ALU.subtract))
            link(d.tensor_copy(v["wcol"][0:64, :], v["wb"][0:64, :]))
            link(d.tensor_tensor(v["wcol"][64:128, :], v["wb1"][64:128, :], v["wb3"][64:128, :], ALU.add))
            link(d.tensor_scalar(w_z, ONES[:, 0:64], v["wcol"], None, ALU.mult))
            link(d.tensor_scalar(w_zb, AVG[:, :], v["wb"], float(D), ALU.mult, ALU.mult))
            link(d.tensor_tensor(RW[0][0:1, 0:128], RW[0][0:1, 0:128], RW[1][0:1, 0:128], ALU.add))
            d.sem_inc(bias_row, 1)
            d.wait_ge(ptr, 2 + 4 * J + 1)
            for h in range(H1):
                hs = slice(0, 64) if h % 2 == 0 else slice(64, 128)
                link(d.tensor_copy(g_cat[hs, 64 * (h // 2):64 * (h // 2) + 64], PA[0][hs, 64 * h:64 * h + 64]))
            link(d.tensor_copy(g_sum[0:64, :], PB[0][0:64, 0:64]))
            link(d.tensor_copy(g_sumb[0:64, 0:64], PB[0][0:64, 0:64]))
            link(d.tensor_copy(g_sumb[64:128, 64:128], PB[1][64:128, 0:64]))
            link(d.tensor_copy(a_log[64:128, :], PB[1][64:128, 128:132]))
            link(d.tensor_copy(a_log[0:64, :], PA[1][0:64, 0:4]))
            link(d.tensor_copy(a_self[0:64, :], PA[1][0:64, 4:8]))
            link(d.tensor_copy(a_edge[0:16, :], PA[1][0:16, 8:12]))
            link(d.tensor_tensor(v["bproj"], v["bp"], PA[2][:, 0:1], ALU.add))
            link(d.tensor_tensor(v["be2"][0:64, :], v["be2"][0:64, :], PA[2][0:64, 1:2], ALU.add))
            link(d.tensor_tensor(v["t0"], v["bo"], PA[2][:, 2:3], ALU.add))
            link(d.tensor_copy(WOCEN[0:64, :], PA[3][0:64, 0:64]))
            d.wait_ge(bc_steps, 3)
            link(d.tensor_scalar(v["t1"], v["bc"], 0.0, None, ALU.max))
            link(d.tensor_tensor(v["sp0"], v["sp0"], v["t1"], ALU.add))
            d.sem_inc(derived, 1)
            d.wait_ge(ptr, 2 + 4 * J + 2)
            link(d.tensor_copy(v["cb"], PB[2][:, 0:1]))
            link(d.tensor_tensor(v["cvec"], v["cb"], PB[3][:, 0:1], ALU.add))
            d.sem_inc(wdone, 1)

            def stage(P, i, prev, f):
                for l in range(L):
                    d.wait_ge(P.s[l], P.at(i, prev))
                    f(l).then_inc(P.s[l], 1)

            def handed_on(*names):
                for n_ in names:
                    d.wait_ge(CARRY[n_], NB + 1)

            for s_ in CARRY.values():
                d.sem_inc(s_, 1)

            def ln_dve(P, i, k, y, rows, aff=None, pool=PB):
                rs = slice(0, rows)
                stage(P, i, f"rstd{k}", lambda l: d.tensor_tensor(y[l][rs, :], pool[l][rs, 0:W], SQ[l][rs, :], ALU.mult))
                if aff:
                    g_, b_, res = aff
                    stage(P, i, f"norm{k}", lambda l: d.tensor_scalar(y[l][rs, :], y[l][rs, :], v[g_][rs, :],
                                                                      v[b_][rs, :], ALU.mult, ALU.add))
                    stage(P, i, f"aff{k}", lambda l: d.tensor_tensor(y[l][rs, :], y[l][rs, :], res[l][rs, :], ALU.add))

            def rows_out(P, i, cols, n):
                for l in range(L):
                    if n:
                        d.wait_ge(P.store[l], i * (16 * n) + 16 * n)
                    else:
                        d.wait_ge(rows_free[l], i + 1)
                    d.wait_ge(P.s[l], P.at(i, "outT"))
                    d.tensor_copy(ROWS[l][0:TE, 0:cols], PA[l][0:TE, 0:cols]).then_inc(P.s[l], 1)

            def cat(P, i):
                stage(P, i, "tT", lambda l: d.tensor_copy(CT[l][:, :], PA[l][:, 0:W]))

            with d.Fori(0, IT) as i:
                cat(P0, i)
                for l in range(L):
                    d.wait_ge(P0.load[l], i * 16 + 16)
                    d.wait_ge(P0.s[l], P0.at(i, "relu"))
                    d.wait_ge(CARRY["agg0"], i * L + (l + 1))
                    d.tensor_tensor_scan(CT[l][64:128, :], MA[l][64:128, :], Y[l][64:128, :], CAR[64:128, 0:1],
                                         ALU.mult, ALU.add).then_inc(P0.s[l], 1)
                    d.wait_ge(P0.s[l], P0.at(i, "agg"))
                    d.tensor_copy(CAR[64:128, 0:1], CT[l][64:128, W - 1:W]).then_inc(CARRY["agg0"], 1)
                ln_dve(P0, i, 1, Y, 64, ("g0", "b0", CT))
                ln_dve(P0, i, 2, Y, 64)
                rows_out(P0, i, J * D, 1)

            handed_on("agg0")
            for l in range(L):
                d.wait_ge(P0.store[l], P0.stored)
            d.wait_ge(noe_dma, 16)
            link(d.tensor_scalar(NOEBUF[0:MP, :], MAPBUF[0:MP, :].rearrange("p (n k) -> p n k", k=2)[:, :, 0],
                                 float(N), None, ALU.is_lt))
            d.sem_inc(noe_ready, 1)

            def elu(P, i, rs, pool, o, res):
                stage(P, i, "proj", lambda l: d.tensor_scalar(SQ[l][rs, :], pool[l][rs, 0:W], v["bproj"][rs, :], 0.0,
                                                              ALU.add, ALU.min))
                stage(P, i, "elu_e", lambda l: d.tensor_scalar(o[l][rs, :], pool[l][rs, 0:W], v["bproj"][rs, :], 0.0,
                                                               ALU.add, ALU.max))
                stage(P, i, "elu_p", lambda l: d.scalar_tensor_tensor(out=o[l][rs, :], in0=SQ[l][rs, :], scalar=-1.0,
                                                                      in1=o[l][rs, :], op0=ALU.add, op1=ALU.add))
                stage(P, i, "elu", lambda l: d.tensor_tensor(o[l][rs, :], o[l][rs, :], res[l][rs, :], ALU.add))

            full, lo, hi = slice(0, 128), slice(0, 64), slice(64, 128)

            def zclip(P, i, rs, pool):
                stage(P, i, "z", lambda l: d.tensor_scalar(SQ[l][rs, :], pool[l][rs, 0:W], -1.0, 40.0, ALU.mult, ALU.min))

            with d.Fori(0, IT) as i:
                ln_dve(PD, i, 1, Y, 128, ("g0", "b0", CT))
                ln_dve(PD, i, 2, Y, 128)
                elu(PD, i, full, PA, H, Y)
                ln_dve(PD, i, 3, H, 128, ("g1", "b1", Y))
                ln_dve(PD, i, 4, H, 128)
                zclip(PD, i, full, PB)
                stage(PD, i, "zg", lambda l: d.tensor_tensor(Y[l][:, :], SQ[l][:, :], CO[l][:, :], ALU.mult))
                stage(PD, i, "rows3", lambda l: d.tensor_tensor(SQ[l][:, :], Y[l][:, :], MA[l][:, :], ALU.mult))

            with d.Fori(0, IT) as i:
                cat(P1, i)
                stage(P1, i, "cat", lambda l: d.tensor_tensor(H[l][lo, :], CT[l][lo, :], MB[l][lo, :], ALU.mult))
                for l in range(L):
                    d.wait_ge(P1.s[l], P1.at(i, "own"))
                    d.wait_ge(CARRY["hold1"], i * L + (l + 1))
                    d.tensor_tensor_scan(CT[l][lo, ::-1], MA[l][lo, ::-1], H[l][lo, ::-1], CAR[lo, 1:2],
                                         ALU.mult, ALU.add).then_inc(P1.s[l], 1)
                    d.wait_ge(P1.s[l], P1.at(i, "hold"))
                    d.tensor_copy(CAR[lo, 1:2], CT[l][lo, 0:1]).then_inc(CARRY["hold1"], 1)
                h4 = slice(0, 4)
                stage(P1, i, "lg", lambda l: d.scalar_tensor_tensor(out=Y[l][h4, :], in0=Y[l][h4, :], scalar=0.2,
                                                                    in1=Y[l][h4, :], op0=ALU.mult, op1=ALU.max))
                for l in range(L):
                    d.wait_ge(P1.s[l], P1.at(i, "leaky"))
                    d.wait_ge(CARRY["mx1"], i * L + (l + 1))
                    d.tensor_copy(MX[l][h4, W:W + 1], CAR[h4, 2:3]).then_inc(P1.s[l], 1)
                    d.wait_ge(P1.s[l], P1.at(i, "mcar"))
                    d.tensor_tensor_scan(MX[l][h4, W - 1::-1], MC[l][h4, ::-1], Y[l][h4, ::-1], MX[l][h4, W:W + 1],
                                         ALU.add, ALU.max).then_inc(P1.s[l], 1)
                    d.wait_ge(P1.s[l], P1.at(i, "mx"))
                    d.tensor_copy(CAR[h4, 2:3], MX[l][h4, 0:1]).then_inc(CARRY["mx1"], 1)
                stage(P1, i, "mx", lambda l: d.tensor_tensor(RW[l][h4, 0:W], MX[l][h4, 1:W + 1], MX[l][h4, 0:W],
                                                             ALU.subtract))
                stage(P1, i, "dr", lambda l: d.tensor_tensor(RW[l][h4, 0:W], RW[l][h4, 0:W], MC[l][h4, :], ALU.add))
                stage(P1, i, "drn", lambda l: d.tensor_tensor(RW[l][h4, W:2 * W], Y[l][h4, :], MX[l][h4, 0:W],
                                                              ALU.subtract))
                for l in range(L):
                    d.wait_ge(P1.s[l], P1.at(i, "exp"))
                    d.wait_ge(CARRY["den1"], i * L + (l + 1))
                    d.tensor_tensor_scan(H[l][h4, ::-1], RW[l][h4, W - 1::-1], RW[l][h4, 2 * W - 1:W - 1:-1],
                                         CAR[h4, 3:4], ALU.mult, ALU.add).then_inc(P1.s[l], 1)
                    d.wait_ge(P1.s[l], P1.at(i, "den"))
                    d.tensor_copy(CAR[h4, 3:4], H[l][h4, 0:1]).then_inc(CARRY["den1"], 1)
                e17 = slice(0, 17)
                for l in range(L):
                    d.wait_ge(P1.s[l], P1.at(i, "den"))
                    d.wait_ge(CARRY["eas1"], i * L + (l + 1))
                    d.tensor_tensor_scan(EAS[l][e17, ::-1], MA[l][e17, ::-1], EA[l][e17, ::-1], CAR[e17, 4:5],
                                         ALU.mult, ALU.add).then_inc(P1.s[l], 1)
                    d.wait_ge(P1.s[l], P1.at(i, "eas"))
                    d.tensor_copy(CAR[e17, 4:5], EAS[l][e17, 0:1]).then_inc(CARRY["eas1"], 1)
                for hp, S in ((0, S0), (1, S1)):
                    stage(P1, i, f"bw{hp}", lambda l: d.tensor_tensor(WD[l][:, :], PB[l][:, 0:W], CO[l][:, :],
                                                                      ALU.mult))
                    for l in range(L):
                        d.wait_ge(P1.s[l], P1.at(i, f"br{hp}"))
                        d.wait_ge(CARRY[f"s1{hp}"], i * L + (l + 1))
                        d.tensor_tensor_scan(S[l][:, ::-1], PA[l][:, W - 1::-1], WD[l][:, ::-1],
                                             CAR[:, 5 + hp:6 + hp], ALU.mult, ALU.add).then_inc(P1.s[l], 1)
                        d.wait_ge(P1.s[l], P1.at(i, f"s{hp}"))
                        d.tensor_copy(CAR[:, 5 + hp:6 + hp], S[l][:, 0:1]).then_inc(CARRY[f"s1{hp}"], 1)
                stage(P1, i, "rcnt", lambda l: d.tensor_tensor(SQ[l][h4, :], PA[l][h4, 0:W], SQ[l][h4, :], ALU.mult))
                stage(P1, i, "sself", lambda l: d.tensor_tensor(SQ[l][h4, :], PA[l][h4, 0:W], SQ[l][h4, :], ALU.add))
                stage(P1, i, "sadd", lambda l: d.scalar_tensor_tensor(out=SQ[l][h4, :], in0=SQ[l][h4, :], scalar=0.2,
                                                                      in1=SQ[l][h4, :], op0=ALU.mult, op1=ALU.max))
                stage(P1, i, "sleaky", lambda l: d.tensor_tensor(Y[l][h4, :], MX[l][h4, 0:W], SQ[l][h4, :], ALU.max))
                stage(P1, i, "mfin", lambda l: d.tensor_tensor(RW[l][h4, 0:W], MX[l][h4, 0:W], Y[l][h4, :],
                                                               ALU.subtract))
                stage(P1, i, "g1", lambda l: d.tensor_tensor(RW[l][h4, W:2 * W], SQ[l][h4, :], Y[l][h4, :],
                                                             ALU.subtract))
                stage(P1, i, "gexp", lambda l: d.tensor_tensor(Y[l][h4, :], H[l][h4, :], RW[l][h4, 0:W], ALU.mult))
                stage(P1, i, "dfac", lambda l: d.tensor_tensor(Y[l][h4, :], Y[l][h4, :], RW[l][h4, W:2 * W], ALU.add))
                stage(P1, i, "drec", lambda l: d.tensor_tensor(Y[l][h4, :], Y[l][h4, :], RW[l][h4, 0:W], ALU.mult))
                stage(P1, i, "bf0", lambda l: d.tensor_tensor(S0[l][:, :], S0[l][:, :], PB[l][:, 0:W], ALU.mult))
                stage(P1, i, "bf1", lambda l: d.tensor_tensor(S1[l][:, :], S1[l][:, :], PB[l][:, 0:W], ALU.mult))
                elu(P1, i, lo, PA, H, CT)
                ln_dve(P1, i, 3, H, 64, ("g1", "b1", CT))
                ln_dve(P1, i, 4, H, 64)
                rows_out(P1, i, J * D, 1)

            handed_on("hold1", "mx1", "den1", "eas1", "s10", "s11")
            with d.Fori(0, IT) as i:
                cat(P2, i)
                stage(P2, i, "cat", lambda l: d.tensor_tensor(H[l][lo, :], CT[l][lo, :], MB[l][lo, :], ALU.mult))
                for l in range(L):
                    d.wait_ge(P2.s[l], P2.at(i, "own"))
                    d.wait_ge(CARRY["hold2"], i * L + (l + 1))
                    d.tensor_tensor_scan(CT[l][lo, :], MA[l][lo, :], H[l][lo, :], CAR[lo, 1:2],
                                         ALU.mult, ALU.add).then_inc(P2.s[l], 1)
                    d.wait_ge(P2.s[l], P2.at(i, "hold"))
                    d.tensor_copy(CAR[lo, 1:2], CT[l][lo, W - 1:W]).then_inc(CARRY["hold2"], 1)
                h8 = slice(0, 8)
                stage(P2, i, "kv", lambda l: d.tensor_tensor(H[l][lo, :], PB[l][lo, 0:W], Y[l][lo, :], ALU.mult))
                for l in range(L):
                    d.wait_ge(P2.s[l], P2.at(i, "lg"))
                    d.wait_ge(CARRY["mx2"], i * L + (l + 1))
                    d.tensor_copy(MX[l][h8, 0:1], CAR[h8, 2:3]).then_inc(P2.s[l], 1)
                    d.wait_ge(P2.s[l], P2.at(i, "mcar"))
                    d.tensor_tensor_scan(MX[l][h8, 1:W + 1], MC[l][h8, :], SQ[l][h8, :], MX[l][h8, 0:1],
                                         ALU.add, ALU.max).then_inc(P2.s[l], 1)
                    d.wait_ge(P2.s[l], P2.at(i, "mx"))
                    d.tensor_copy(CAR[h8, 2:3], MX[l][h8, W:W + 1]).then_inc(CARRY["mx2"], 1)
                stage(P2, i, "mx", lambda l: d.tensor_tensor(RW[l][h8, 0:W], MX[l][h8, 0:W], MX[l][h8, 1:W + 1],
                                                             ALU.subtract))
                stage(P2, i, "dr", lambda l: d.tensor_tensor(RW[l][h8, 0:W], RW[l][h8, 0:W], MC[l][h8, :], ALU.add))
                stage(P2, i, "drn", lambda l: d.tensor_tensor(RW[l][h8, W:2 * W], SQ[l][h8, :], MX[l][h8, 1:W + 1],
                                                              ALU.subtract))
                for l in range(L):
                    d.wait_ge(P2.s[l], P2.at(i, "exp"))
                    d.wait_ge(CARRY["den2"], i * L + (l + 1))
                    d.tensor_tensor_scan(Y[l][h8, :], RW[l][h8, 0:W], RW[l][h8, W:2 * W], CAR[h8, 3:4],
                                         ALU.mult, ALU.add).then_inc(P2.s[l], 1)
                    d.wait_ge(P2.s[l], P2.at(i, "den"))
                    d.tensor_copy(CAR[h8, 3:4], Y[l][h8, W - 1:W]).then_inc(CARRY["den2"], 1)
                stage(P2, i, "bw", lambda l: d.tensor_tensor(WD[l][hi, :], WD[l][hi, :], PA[l][hi, 0:W], ALU.mult))
                for l in range(L):
                    d.wait_ge(P2.s[l], P2.at(i, "br"))
                    d.wait_ge(CARRY["s2"], i * L + (l + 1))
                    d.tensor_tensor_scan(S0[l][hi, :], PA[l][hi, 0:W], WD[l][hi, :], CAR[hi, 5:6],
                                         ALU.mult, ALU.add).then_inc(P2.s[l], 1)
                    d.wait_ge(P2.s[l], P2.at(i, "s"))
                    d.tensor_copy(CAR[hi, 5:6], S0[l][hi, W - 1:W]).then_inc(CARRY["s2"], 1)
                stage(P2, i, "bd", lambda l: d.tensor_tensor(CO[l][hi, :], S0[l][hi, :], PA[l][hi, 0:W], ALU.mult))
                zclip(P2, i, hi, PA)
                stage(P2, i, "zg", lambda l: d.tensor_tensor(S1[l][hi, :], SQ[l][hi, :], PB[l][hi, 0:W], ALU.mult))
                stage(P2, i, "gd", lambda l: d.tensor_tensor(CT[l][hi, :], CO[l][hi, :], S1[l][hi, :], ALU.add))
                stage(P2, i, "u", lambda l: d.tensor_tensor(SQ[l][hi, :], CT[l][hi, :], MD[l][hi, :], ALU.mult))
                rows_out(P2, i, J * 128, 1)

            handed_on("hold2", "mx2", "den2", "s2")
            for l in range(L):
                d.wait_ge(P2.s[l], P2.end())
            link(d.tensor_reduce(SUMS[:, 0:2], STAT[:, 0:2, :], AX.X, ALU.add))
            link(d.tensor_reduce(SUMS[hi, 2:4], STAT[hi, 2:4, :], AX.X, ALU.add))
            d.sem_inc(fin, 1)
            d.wait_ge(bn_done, 1)
            link(d.tensor_tensor(SUMS[hi, 2:4], SUMS[hi, 2:4], PA[0][hi, 0:2], ALU.add))
            link(d.tensor_scalar(v["mean"][hi, :], SUMS[hi, 2:3], 1.0 / N, None, ALU.mult))
            link(d.tensor_scalar(v["var"][hi, :], SUMS[hi, 3:4], 1.0 / N, None, ALU.mult))
            link(d.tensor_tensor(v["t0"][hi, :], v["mean"][hi, :], v["mean"][hi, :], ALU.mult))
            link(d.tensor_tensor(v["var"][hi, :], v["var"][hi, :], v["t0"][hi, :], ALU.subtract))
            d.sem_inc(fin, 3)
            d.wait_ge(fin, 6)
            link(d.tensor_tensor(v["bs"][hi, :], v["bs"][hi, :], v["g2"][hi, :], ALU.mult))
            link(d.tensor_tensor(v["t0"][hi, :], v["mean"][hi, :], v["bs"][hi, :], ALU.mult))
            link(d.tensor_tensor(v["bt"][hi, :], v["b2"][hi, :], v["t0"][hi, :], ALU.subtract))

            def x3_dve(P, i):
                cat(P, i)
                stage(P, i, "oT", lambda l: d.tensor_copy(CO[l][:, :], PB[l][:, 0:W]))
                for t_, a_, b_ in ((CT, "ocat", "aff"), (CO, "lrelu", "oaff")):
                    stage(P, i, a_, lambda l: d.tensor_scalar(t_[l][hi, :], t_[l][hi, :], v["bs"][hi, :],
                                                              v["bt"][hi, :], ALU.mult, ALU.add))
                    stage(P, i, b_, lambda l: d.scalar_tensor_tensor(out=t_[l][hi, :], in0=t_[l][hi, :], scalar=0.01,
                                                                     in1=t_[l][hi, :], op0=ALU.mult, op1=ALU.max))
                ln_dve(P, i, 1, Y, 128)

            with d.Fori(0, IT) as i:
                x3_dve(P4, i)
                stage(P4, i, "rstd2", lambda l: d.tensor_tensor(Y[l][:, :], H[l][:, :], SQ[l][:, :], ALU.mult))
                rows_out(P4, i, J * 128, 2)

            def ssp_dve(i, k, pool, bias, o):
                stage(P3, i, f"{k}l", lambda l: d.tensor_scalar(o[l][lo, :], pool[l][lo, 0:W], v[bias][lo, :], 0.0,
                                                                ALU.add, ALU.max))
                stage(P3, i, f"{k}r", lambda l: d.tensor_tensor(o[l][lo, :], o[l][lo, :], SQ[l][lo, :], ALU.add))

            with d.Fori(0, IT) as i:
                x3_dve(P3, i)
                ssp_dve(i, "f1", PA, "be1", H)
                ssp_dve(i, "f2", PB, "be2", H)
                stage(P3, i, "hb", lambda l: d.scalar_tensor_tensor(out=WD[l][lo, :], in0=H[l][lo, :], scalar=-LN2,
                                                                    in1=WD[l][lo, :], op0=ALU.add, op1=ALU.mult))
                for l in range(L):
                    d.wait_ge(P3.s[l], P3.at(i, "msg"))
                    d.wait_ge(CARRY["agg3"], i * L + (l + 1))
                    d.tensor_tensor_scan(S0[l][lo, :], MA[l][lo, :], WD[l][lo, :], CAR[lo, 1:2],
                                         ALU.mult, ALU.add).then_inc(P3.s[l], 1)
                    d.wait_ge(P3.s[l], P3.at(i, "agg"))
                    d.tensor_copy(CAR[lo, 1:2], S0[l][lo, W - 1:W]).then_inc(CARRY["agg3"], 1)
                ssp_dve(i, "c", PB, "bc", Y)
                stage(P3, i, "rstd2", lambda l: d.tensor_tensor(Y[l][lo, :], H[l][lo, :], SQ[l][lo, :], ALU.mult))
                rows_out(P3, i, J * D, 0)


_WEIGHTS = ['L0_gnn_W_msg', 'L0_gnn_b_msg', 'L0_gnn_W_upd', 'L0_gnn_b_upd', 'L0_gnn_gamma', 'L0_gnn_beta',
            'L1_gnn_bias', 'L1_gnn_Wp', 'L1_gnn_bp', 'L1_gnn_gamma', 'L1_gnn_beta', 'L2_gnn_Wq', 'L2_gnn_bq',
            'L2_gnn_Wk', 'L2_gnn_bk', 'L2_gnn_Wv', 'L2_gnn_bv', 'L2_gnn_We', 'L2_gnn_be', 'L2_gnn_Wskip',
            'L2_gnn_bskip', 'L2_gnn_Wbeta', 'L2_gnn_gamma', 'L2_gnn_beta_bn', 'L3_gnn_We1', 'L3_gnn_be1',
            'L3_gnn_We2', 'L3_gnn_be2', 'L3_gnn_Wn', 'L3_gnn_bn', 'L3_gnn_Wc', 'L3_gnn_bc', 'L3_gnn_Wo',
            'L3_gnn_bo']
_TURNED = {'WT': 'L1_gnn_W', 'WeT': 'L1_gnn_W_edge', 'att_srcT': 'L1_gnn_att_src', 'att_dstT': 'L1_gnn_att_dst',
           'att_edgeT': 'L1_gnn_att_edge', 'WoT': 'L3_gnn_Wo'}


def kernel(**inputs):
    import numpy as _np
    import concourse.bacc as _bacc
    from concourse import mybir as _mybir
    from concourse.bass_utils import run_bass_kernel_spmd as _run

    nc = _bacc.Bacc("TRN2", target_bir_lowering=False, num_devices=1)
    arrays, aps = {}, {}

    def give(name, a):
        a = _np.ascontiguousarray(a)
        arrays[name] = a
        aps[name] = nc.dram_tensor(name, a.shape, _mybir.dt.from_np(a.dtype), kind="ExternalInput").ap()

    for name in ("x", "src", "dst"):
        give(name, _np.asarray(inputs[name]))
    give("xT", _np.asarray(inputs["x"]).T)
    give("ea16T", _np.asarray(inputs["edge_attr_16"]).T)
    give("ea64T", _np.asarray(inputs["edge_attr_64"]).T)
    for name in _WEIGHTS:
        give(name, _np.asarray(inputs[name]))
    for name, of in _TURNED.items():
        give(name, _np.asarray(inputs[of]).T)
    out = nc.dram_tensor("out", (N, D), F32, kind="ExternalOutput").ap()
    program(nc, aps["x"], aps["xT"], aps["src"], aps["dst"], aps["ea16T"], aps["ea64T"], aps, out)
    r = _run(nc, [arrays], core_ids=[0])
    return r.results[0]["out"]
```

```python
from contextlib import ExitStack

import numpy as np
import concourse.bass as bass
from concourse import mybir
from concourse.alu_op_type import AluOpType as ALU

F32 = mybir.dt.float32
I32 = mybir.dt.int32
ACT = mybir.ActivationFunctionType
AX = mybir.AxisListType

N, E, D = 100000, 50000, 64
W = 500
TE = 125
J = W // TE
L = 4
NB = E // W
NQ = NB // 2
H1, H2 = 4, 8
EPS = 1e-5
LN2 = float(np.log(2.0))
NEG = -1.0e30
FAR = float(1 << 23)
MP, MN = 80, N // 80


FIRST_COUNT = [1 + 1000 * l for l in range(L)]
CARRY_COUNT = 128


class Chain:

    def __init__(self, *stages):
        self.stages = stages
        self.k = len(stages)

    def at(self, i, lane, stage=None):
        return i * self.k + (FIRST_COUNT[lane] + (self.stages.index(stage) + 1 if stage else 0))


LN_STEPS = ("cen", "sq", "var", "ln", "rstd", "norm")


def ln_names(k):
    return tuple(f"{s}{k}" for s in LN_STEPS)


def program(nc, x, xT, src, dst, ea16T, ea64T, w, out):
    ctx = ExitStack()
    with ctx:
        def sb(name, shape, dt=F32):
            return ctx.enter_context(nc.sbuf_tensor(name, shape, dt))

        def sem(name):
            return ctx.enter_context(nc.semaphore(name))

        T1 = nc.dram_tensor("T1", (N + E, D), F32).ap()
        T2 = nc.dram_tensor("T2", (N + E, D), F32).ap()
        T3 = nc.dram_tensor("T3", (N + E, 2 * D), F32).ap()
        MAP = nc.dram_tensor("MAP", (N, 2), I32).ap()
        MASKS = nc.dram_tensor("MASKS", (6, E), F32).ap()
        SAME, FIRST, SAMEN, LAST, NEGP, NEGN = range(6)
        NOE = nc.dram_tensor("NOE", (N,), F32).ap()

        def lanes(name, cols, dt=F32):
            return [sb(f"{name}{l}", [128, cols], dt) for l in range(L)]

        XD, XS, WD, Y, H, SQ = (lanes(n, W) for n in ("XD", "XS", "WD", "Y", "H", "SQ"))
        BIG1, BIG2 = lanes("BIG1", 1024), lanes("BIG2", 1024)
        S = [[b[:, c:c + W] for b in (BIG1[l], BIG2[l]) for c in (0, 512)] for l in range(L)]
        MX = lanes("MX", W + 1)
        RW = lanes("RW", 2 * W)
        MA, MB, MC = (lanes(n, W) for n in ("MA", "MB", "MC"))
        EA, EAS = (lanes(n, W) for n in ("EA", "EAS"))
        TILE, TILEO = (lanes(n, J * 128) for n in ("TILE", "TILEO"))
        ROWS = lanes("ROWS", 2 * J * 128)
        PA = [ctx.enter_context(nc.psum_tensor(f"PA{l}", [128, 512], F32)) for l in range(L)]
        PB = [ctx.enter_context(nc.psum_tensor(f"PB{l}", [128, 512], F32)) for l in range(L)]

        WALL = sb("WALL", [128, 3072])
        used = [0]

        def mat(cols, of=WALL, count=used):
            count[0] += cols
            return of[:, count[0] - cols:count[0]]

        w_msgs, w_msgd, w_updx, w_upda = mat(128), mat(128), mat(128), mat(128)
        g_h = [mat(128) for _ in range(H1)]
        g_sum = mat(128)
        a_src, a_dst, a_self = mat(36), mat(36), mat(36)
        a_edge, a_cnt = mat(36), mat(36)
        w_q, w_k, w_v, w_skip, w_ek, w_ev = (mat(128) for _ in range(6))
        w_zo, w_zx = mat(128), mat(128)
        w_e1, w_e2, w_n, w_c, w_oc = (mat(128) for _ in range(5))
        assert used[0] <= 3072, used[0]
        tmp = [0]
        wT, weT, wp, att, w_o, w_oT, w_e2t = (mat(c, BIG1[1], tmp) for c in (256, 64, 256, 12, 64, 64, 64))
        vec_names = ["bmsg", "bupd", "g0", "b0", "bp", "g1", "b1", "bq", "bskip", "g2", "b2", "be1", "be2", "bn",
                     "bc", "bo", "wb1", "wb2", "wb3", "bk", "bv", "be", "hb0", "hb1", "hb2", "hb3", "bproj", "wcol", "wb",
                     "cb", "sp0", "cvec", "mean", "var", "bs", "bt", "m64", "t0", "t1", "eps", "tiny"]
        VEC = sb("VEC", [128, len(vec_names)])
        v = {n: VEC[:, k:k + 1] for k, n in enumerate(vec_names)}
        STATD = sb("STATD", [128, 2, NB])
        STATE = sb("STATE", [128, 2, NQ])
        SUMS = sb("SUMS", [128, 4])
        IDN = sb("IDN", [128, 128])
        AVG = sb("AVG", [128, 128])
        CEN = sb("CEN", [128, 128])
        ADD2 = BIG2[1][:, 0:128]
        ONES = BIG2[1][:, 128:256]
        B4 = sb("B4", [64, H1 * 128])
        B8 = sb("B8", [64, 128])
        HSEL = sb("HSEL", [128, 40])
        CAR = sb("CAR", [128, 10])

        NT = E // TE
        SRCI, DSTI, SCATI = (sb(n, [TE, NT], I32) for n in ("SRCI", "DSTI", "SCATI"))
        MAPV = sb("MAPV", [TE, NT, 2], I32)
        RINGI = sb("RINGI", [TE, L, 2, 2 * J], I32)
        RINGV = sb("RINGV", [TE, L, J, 2], I32)

        MAPBUF = [b[0:MP, 0:W].bitcast(I32) for b in (WD[0], WD[1], WD[2], WD[3], RW[0])]
        MC5 = len(MAPBUF)
        NOEBUF = [SQ[0], SQ[1], SQ[2], SQ[3], RW[1]]
        PREP = [BIG2[2][:, 0:W], BIG2[2][:, 512:512 + W], BIG2[3][:, 0:W], BIG2[3][:, 512:512 + W]]
        wsem, built, pdma = sem("weights_in"), sem("constants_built"), sem("prep_dma")
        masks_ready, starts, indices_ready = sem("masks_ready"), sem("starts"), sem("indices_ready")
        built_pool, dve_link, derived = sem("pool_link"), sem("dve_link"), sem("derived")
        rows_free = [sem(f"rows_free{l}") for l in range(L)]
        bc_steps, bias_row, bias_row_in = sem("bc_steps"), sem("bias_row"), sem("bias_row_in")
        CARRY = {n: sem("carry_" + n) for n in ("agg0", "hold1", "mx1", "den1", "eas1", "s10", "s11", "s12", "s13", "hold2",
                                                "mx2", "den2", "s2", "agg3")}
        wdone, ptr = sem("weights_ready"), sem("prep_transposed")
        idx_ready, map_moved, map_done = sem("idx_ready"), [sem(f"map_moved{l}") for l in range(L)], sem("map_done")
        noe_dma, noe_ready, bn_done = sem("noe_dma"), sem("noe_ready"), sem("bn_done")
        map_got, map_copied = sem("map_got"), sem("map_copied")
        fin = sem("stat_done")

        class Phase:
            def __init__(self, tag, full, tail, *stages):
                self.chain = Chain(*stages)
                self.at, self.k = self.chain.at, self.chain.k
                self.lag = [l * self.k // L for l in range(L)]
                self.full, self.tail = full, tail
                self.s = [sem(f"{tag}_chain{l}") for l in range(L)]
                self.load = [sem(f"{tag}_load{l}") for l in range(L)]
                self.got = [sem(f"{tag}_gather{l}") for l in range(L)]
                self.store = [sem(f"{tag}_store{l}") for l in range(L)]

            def n(self, l):
                return self.full + (l < self.tail)

            def end(self, l):
                return self.at(self.n(l), l)

            def place(self, prev):
                return self.chain.stages.index(prev) + 1

            def weave(self, body, parts):
                runs = [[0, l, late, body(i, l)] for i, l, late in parts]
                for run in runs:
                    run[0] = next(run[3])
                while runs:
                    run = min(runs, key=lambda r: r[0] + self.lag[r[1]] - self.k * r[2])
                    try:
                        run[0] = run[3].send((run[0] + self.lag[run[1]] >= self.k) == run[2])
                    except StopIteration:
                        runs.remove(run)

            def loop(self, eng, body, whole=None):
                self.weave(body, [(0, l, False) for l in range(L)])
                whole = whole or self.full
                with eng.Fori(0, whole - 1) as i:
                    self.weave(body, [(i, l, True) for l in range(L)] + [(i + 1, l, False) for l in range(L)])
                for n in range(whole, self.full + 2):
                    self.weave(body, [(n - 1, l, True) for l in range(L) if n - 1 < self.n(l)] +
                               [(n, l, False) for l in range(L) if n < self.n(l)])

        out_steps = ("outT", "rows")
        elu_steps = ("proj", "elu_n", "elu_e", "elu_p", "elu", "elu_res")
        gate_steps = ("z", "zc", "ze", "zl", "zg")
        edges, nodes = (NQ // L, NQ % L), (NB // L, NB % L)

        def ssp_names(k):
            return tuple(k + e for e in ("", "a", "e", "l", "r", "s"))

        P0 = Phase("l0", *edges, "tT", "cat", "cato", "msg", "relu", "agg0", "agg1", "upd", "updrelu", *ln_names(1),
                   "aff1", "res1", *ln_names(2), *out_steps)
        PD = Phase("d1", *nodes, "upd", "updrelu", *ln_names(1), "aff1", "res1", *ln_names(2), "outT1", "rows1",
                   *elu_steps, *ln_names(3), "aff3", "res3", *ln_names(4), "outT2", "rows2", "xr", "xrb",
                   *gate_steps, "u", "outT3", "rows3", "um", "us", "uq")
        P1 = Phase("l1", *edges, "tT", "cat", "own", "hold0", "hold1", "logit", "lg", "leaky", "mc0", "mx0", "mc1",
                   "mx1", "dr", "drn", "dw", "exp", "den0", "den1", "eas0", "eas1", "dx",
                   *(n + str(h) for h in range(H1) for n in ("b", "wd", "sa", "sb")),
                   "esum", "lcnt", "rcnt", "emean", "sself", "sadd", "sleaky", "mfin", "g1", "g2", "gexp",
                   "dfac", "dsum", "dln", "drec", "fac", "bf0", "sf0", "sf1", "bf2", "sf2", "sf3",
                   *elu_steps, *ln_names(3), "aff3", "res3", *ln_names(4), *out_steps)
        P2 = Phase("l2", *edges, "tT", "cat", "own", "hold0", "hold1", "q", "qb", "kv", "qk", "vc", "logit", "lg",
                   "mc0", "mx0", "mc1", "mx1", "dr", "drn", "dw", "exp", "den0", "den1", "b", "wv", "s0", "s1",
                   "dln", "drec", "bd", "o", "xr", "xrb", *gate_steps, "df", "gd", "u", "um", "us", "uq", "outT",
                   "rows", "rowsu")
        P3 = Phase("l3", *edges, "tT", "cat0", "cat1", "catu0", "catu1", "lrelu", "oT", "ocat", "ocatu", "olrelu", *ln_names(1),
                   *ln_names(3), *ssp_names("f1"), *ssp_names("f2"), "h", "hb", "msg", "agg0", "agg1",
                   *ssp_names("c"), "cen2", "cb2", "sq2", "var2", "ln2", "rstd2", "norm2", *out_steps)
        P4 = Phase("d3", *nodes, "tT", "cat", "catu", "lrelu", *ln_names(1),
                   "cen2", "cb2", "sq2", "var2", "ln2", "rstd2", "norm2", *out_steps)
        for P_, n_ in ((P0, 2), (P1, 2), (P2, 2), (PD, 6), (P4, 2)):
            P_.stores, P_.credit = n_, n_
        P3.stores, P3.credit = 2 * J, 0

        block = ctx.enter_context(nc.Block())
        NWDMA_TOTAL = 3 + 4 + 3 * H1 + 3 + H1 + 6 + 6 + 4 + 2 * 16 + 2 * 3

        def pair(i, lane, back=False):
            return (NQ - 1 - lane) - i * L if back else i * L + lane

        def rows_at(table, row, c0=0, c1=None):
            c1 = table.shape[1] if c1 is None else c1
            return table[bass.ds(row, W), c0:c1].rearrange("(j p) c -> p j c", p=TE)

        def edge_at(q, half):
            return q * (2 * W) + half * W

        def node_at(b, half):
            return b * W + half * (N // 2)

        def spread(a, rows):
            return a.to_broadcast([rows, W])

        def mask_of(k, rows, q, half):
            return spread(MASKS[k:k + 1, bass.ds(edge_at(q, half), W)], rows)

        HALF = (slice(0, 64), slice(64, 128))

        def by_half(buf, cols):
            return buf[0:TE, 0:2 * J * cols].rearrange("p (j h c) -> p h j c", j=J, h=2)

        def by_part(buf, half):
            return buf[0:TE, :].rearrange("p (j k h c) -> p h j k c", j=J, k=2, h=2)[:, half]

        def wait_phase_done(eng, P, stores=True):
            for l in range(L):
                eng.wait_ge(P.s[l], P.end(l))
                if stores:
                    eng.wait_ge(P.store[l], 16 * (P.credit + P.stores * P.n(l)))

        NWDMA_TOTAL = 12 * 2 + 3 * H1 + 3 + H1 + 4 + 3 + 4 + 2 * 16 + 2 * 3

        @block.sync
        def _(sp):
            sp.wait_ge(built, 1)

            loaded = [0]

            def ld(o, i):
                sp.dma_start(o, i).then_inc(wsem, 16)
                loaded[0] += 1

            for m, a in ((w_msgs, w["L0_gnn_W_msg"][0:64, :]), (w_msgd, w["L0_gnn_W_msg"][64:128, :]),
                         (w_updx, w["L0_gnn_W_upd"][0:64, :]), (w_upda, w["L0_gnn_W_upd"][64:128, :]),
                         (w_q, w["L2_gnn_Wq"]), (w_k, w["L2_gnn_Wk"]), (w_v, w["L2_gnn_Wv"]),
                         (w_skip, w["L2_gnn_Wskip"]), (w_e1, w["L3_gnn_We1"]), (w_e2, w["L3_gnn_We2"]),
                         (w_n, w["L3_gnn_Wn"]), (w_c, w["L3_gnn_Wc"])):
                for hs in HALF:
                    ld(m[hs, hs], a)
            for h in range(H1):
                ld(wT[0:64, 64 * h:64 * h + 64], w["WT"][64 * h:64 * h + 64, :])
                ld(weT[0:64, 16 * h:16 * h + 16], w["WeT"][64 * h:64 * h + 64, :])
                ld(wp[0:64, 64 * h:64 * h + 64], w["L1_gnn_Wp"][64 * h:64 * h + 64, :])
            for k, n in enumerate(("att_src", "att_dst", "att_edge")):
                ld(att[0:64, 4 * k:4 * k + 4], w[n + "T"])
            for h in range(H1):
                ld(v[f"hb{h}"][0:64, :], w["L1_gnn_bias"][64 * h:64 * h + 64].unsqueeze(1))
            for m in (w_ek, w_ev):
                for half in range(2):
                    ld(m[64 * half:64 * half + 16, HALF[half]], w["L2_gnn_We"])
            ld(w_o[0:64, :], w["L3_gnn_Wo"])
            ld(w_oT[0:64, :], w["WoT"])
            ld(w_e2t[0:64, :], w["L3_gnn_We2"])
            sp_rows = (("L2_gnn_bk", 0), ("L2_gnn_bv", 64))
            for n, c in sp_rows:
                ld(ROWS[0][0:1, c:c + 64], w[n].unsqueeze(0))
                ld(ROWS[1][0:1, c:c + 64], w["L2_gnn_be"].unsqueeze(0))
            for name, a in (("bmsg", "L0_gnn_b_msg"), ("bupd", "L0_gnn_b_upd"), ("g0", "L0_gnn_gamma"),
                            ("b0", "L0_gnn_beta"), ("bp", "L1_gnn_bp"), ("g1", "L1_gnn_gamma"),
                            ("b1", "L1_gnn_beta"), ("bq", "L2_gnn_bq"), ("bskip", "L2_gnn_bskip"),
                            ("g2", "L2_gnn_gamma"), ("b2", "L2_gnn_beta_bn"), ("be1", "L3_gnn_be1"),
                            ("be2", "L3_gnn_be2"), ("bn", "L3_gnn_bn"), ("bc", "L3_gnn_bc"), ("bo", "L3_gnn_bo")):
                ld(v[name][0:64, :], w[a].unsqueeze(1))
                ld(v[name][64:128, :], w[a].unsqueeze(1))
            wb = w["L2_gnn_Wbeta"]
            for k, name in enumerate(("wb1", "wb2", "wb3")):
                ld(v[name][0:64, :], wb[64 * k:64 * k + 64, :])
                ld(v[name][64:128, :], wb[64 * k:64 * k + 64, :])

            assert loaded[0] == NWDMA_TOTAL, loaded
            d2, s2 = dst.rearrange("(r c) -> r c", c=W), src.rearrange("(r c) -> r c", c=W)
            DI, DP, DN, SI = (t[0:NB, 0:W].bitcast(I32) for t in (XD[0], XD[1], XD[2], XD[3]))
            sp.wait_ge(built, 2)
            sp.dma_start(DI, d2).then_inc(pdma, 16)
            sp.dma_start(SI, s2).then_inc(pdma, 16)
            sp.dma_start(DP[:, 1:W], d2[:, 0:W - 1]).then_inc(pdma, 16)
            sp.dma_start(DP[1:NB, 0:1], d2[0:NB - 1, W - 1:W], allow_slow_non_contiguous=True).then_inc(pdma, 16)
            sp.dma_start(DN[:, 0:W - 1], d2[:, 1:W]).then_inc(pdma, 16)
            sp.dma_start(DN[0:NB - 1, W - 1:W], d2[1:NB, 0:1], allow_slow_non_contiguous=True).then_inc(pdma, 16)
            sp.wait_ge(built, 3)
            map_v = MAP.rearrange("(p n) k -> p (n k)", p=MP)
            for k, b in enumerate(MAPBUF):
                sp.dma_start(map_v[:, k * W:(k + 1) * W], b).then_inc(pdma, 16)
            sp.wait_ge(masks_ready, 1)
            for k, t in enumerate((Y[0], Y[1], Y[2], Y[3], H[0], H[1])):
                sp.dma_start(MASKS[k, :].rearrange("(r c) -> r c", c=W), t[0:NB, 0:W]).then_inc(pdma, 16)
            sp.wait_ge(pdma, 16 * 17)
            sp.wait_ge(bias_row, 1)
            for k, m in enumerate((w_ek, w_ev)):
                for half in range(2):
                    sp.dma_start(m[64 * half + 16:64 * half + 17, HALF[half]],
                                 ROWS[0][0:1, 64 * k:64 * k + 64]).then_inc(bias_row_in, 16)
            sp.wait_ge(bias_row_in, 16 * 4)

            def first_credit(P):
                for l in range(L):
                    sp.sem_inc(P.s[l], FIRST_COUNT[l])
                    if P.credit:
                        sp.sem_inc(P.store[l], 16 * P.credit)

            def waited(P, i, l, stage):
                sp.wait_ge(P.s[l], P.at(i, l, stage))
                sp.nop(nofuse=True)

            def run(P, loads, used, *stores):
                def more(i, l):
                    if not isinstance(i, int) or i + 1 < P.n(l):
                        loads(i + 1, l)

                def body(i, l):
                    for stage, act in sorted([(used, more), *stores], key=lambda e: P.place(e[0])):
                        if (yield P.place(stage)):
                            waited(P, i, l, stage)
                            act(i, l)

                for l in range(L):
                    loads(0, l)
                P.loop(sp, body, whole=P.full - 1)

            def load(P, l, o, a):
                sp.dma_start(o, a).then_inc(P.load[l], 16)

            def store(P, l, o, a):
                sp.dma_start(o, a).then_inc(P.store[l], 16)

            def store_rows(P, table, i, l, cols, back=False):
                for half in range(2):
                    store(P, l, rows_at(table, N + edge_at(pair(i, l, back), half)), by_half(ROWS[l], cols)[:, half])

            sp.wait_ge(wdone, 1)
            first_credit(P0)

            def loads0(i, l):
                for half, hs in enumerate(HALF):
                    load(P0, l, MA[l][hs, :], mask_of(SAME, 64, pair(i, l), half))

            run(P0, loads0, "agg1", ("rows", lambda i, l: store_rows(P0, T1, i, l, D)))

            wait_phase_done(sp, P0)
            sp.wait_ge(map_done, 1)
            for k, b in enumerate(MAPBUF):
                sp.dma_start(b, map_v[:, k * W:(k + 1) * W]).then_inc(noe_dma, 16)
            sp.wait_ge(noe_ready, 1)
            for k, b in enumerate(NOEBUF):
                sp.dma_start(NOE.rearrange("(p n) -> p n", p=MP)[:, k * (W // 2):(k + 1) * (W // 2)],
                             b[0:MP, 0:W // 2]).then_inc(noe_dma, 16)
            sp.wait_ge(noe_dma, 16 * 10)
            first_credit(PD)

            def loadsD(i, l):
                b = pair(i, l)
                for half, hs in enumerate(HALF):
                    load(PD, l, XD[l][hs, :], xT[:, bass.ds(node_at(b, half), W)])
                    load(PD, l, MA[l][hs, :], spread(NOE[bass.ds(node_at(b, half), W)].unsqueeze(0), 64))

            def stores1(i, l):
                for half in range(2):
                    store(PD, l, rows_at(T1, node_at(pair(i, l), half)), by_half(TILE[l], D)[:, half])

            def stores3(i, l):
                for half in range(2):
                    b = node_at(pair(i, l), half)
                    store(PD, l, rows_at(T2, b), by_half(ROWS[l], 2 * D)[:, half, :, 0:D])
                    store(PD, l, rows_at(T3, b), by_half(ROWS[l], 2 * D)[:, half])

            run(PD, loadsD, "um", ("rows1", stores1), ("rows3", stores3))

            wait_phase_done(sp, PD)
            first_credit(P1)

            def loads12(P, i, l, q, T, same, own, neg):
                for half, hs in enumerate(HALF):
                    load(P, l, by_half(TILEO[l], D)[:, half], rows_at(T, N + edge_at(q, half)))
                    load(P, l, MA[l][hs, :], mask_of(same, 64, q, half))
                    load(P, l, MB[l][hs, :], mask_of(own, 64, q, half))
                    load(P, l, MC[l][32 * half:32 * half + 32, :], mask_of(neg, 32, q, half))
                    load(P, l, EA[l][64 * half:64 * half + 16, :], ea16T[:, bass.ds(edge_at(q, half), W)])

            run(P1, lambda i, l: loads12(P1, i, l, pair(i, l, True), T1, SAMEN, LAST, NEGN), "eas1",
                ("rows", lambda i, l: store_rows(P1, T2, i, l, D, True)))

            wait_phase_done(sp, P1)
            first_credit(P2)

            def loads2(i, l):
                q = pair(i, l)
                loads12(P2, i, l, q, T2, SAME, FIRST, NEGP)
                for half, hs in enumerate(HALF):
                    load(P2, l, S[l][3][hs, :], mask_of(LAST, 64, q, half))

            run(P2, loads2, "um", ("rowsu", lambda i, l: store_rows(P2, T3, i, l, 2 * D)))

            wait_phase_done(sp, P2)
            first_credit(P4)

            def loads4(i, l):
                for half in range(2):
                    for k in range(2):
                        load(P4, l, by_part(BIG1[l], half)[:, :, k],
                             rows_at(T3, node_at(pair(i, l), half), k * D, k * D + D))

            def stores4(i, l):
                for half in range(2):
                    store(P4, l, rows_at(out, node_at(pair(i, l), half)), by_half(ROWS[l], D)[:, half])

            run(P4, loads4, "tT", ("rows", stores4))

            wait_phase_done(sp, P4)
            first_credit(P3)

            def loads3(i, l):
                q = pair(i, l)
                for half, hs in enumerate(HALF):
                    for k in range(2):
                        load(P3, l, by_part(BIG2[l], half)[:, :, k],
                             rows_at(T3, N + edge_at(q, half), k * D, k * D + D))
                    load(P3, l, MA[l][hs, :], mask_of(SAME, 64, q, half))
                    load(P3, l, MB[l][hs, :], ea64T[:, bass.ds(edge_at(q, half), W)])

            run(P3, loads3, "agg1")
            wait_phase_done(sp, P3)

        @block.gpsimd
        def _(g):
            n = [0]

            def step(ins):
                n[0] += 1
                ins.then_inc(built_pool, 1)
                g.wait_ge(built_pool, n[0])

            step(g.memset(WALL[:, :], 0.0))
            step(g.memset(VEC[:, :], 0.0))
            step(g.memset(v["m64"], -LN2))
            step(g.memset(v["eps"], EPS))
            step(g.memset(v["tiny"], 1e-16))
            for l in range(L):
                step(g.memset(EA[l][:, :], 1.0))
            g.sem_inc(built, 1)
            step(g.memset(XD[1][0:NB, 0:W].bitcast(I32), -1))
            step(g.memset(XD[2][0:NB, 0:W].bitcast(I32), -1))
            g.sem_inc(built, 1)
            for k, b in enumerate(MAPBUF):
                step(g.iota(b.rearrange("p (n k) -> p n k", k=2), pattern=[[1, W // 2], [0, 2]], base=k * (W // 2),
                            channel_multiplier=MN))
            g.sem_inc(built, 1)
            step(g.iota(MAPV[:, :, 0], pattern=[[TE, NT]], base=N, channel_multiplier=1))
            step(g.iota(XS[0][0:NB, 0:W].bitcast(I32), pattern=[[1, W]], base=0, channel_multiplier=W))
            step(g.memset(IDN[:, :], 0.0))
            step(g.affine_select(out=IDN[:, :], in_=IDN[:, :], compare_op=ALU.not_equal, fill=1.0, base=0,
                                 pattern=[[-1, 128]], channel_multiplier=1))
            step(g.memset(AVG[:, :], 0.0))
            step(g.memset(AVG[0:64, 0:64], 1.0 / D))
            step(g.memset(AVG[64:128, 64:128], 1.0 / D))
            step(g.memset(ONES[:, :], 1.0))
            step(g.memset(CAR[:, :], 0.0))

            def where_zero(t, pattern, base=0):
                step(g.memset(t, 0.0))
                k = {2: "p (a b) -> p a b", 3: "p (a b c) -> p a b c"}[len(pattern)]
                o = t.rearrange(k, **{n: p[1] for n, p in zip("abc", pattern)})
                step(g.affine_select(out=o, in_=o, compare_op=ALU.not_equal, fill=1.0, base=base, pattern=pattern,
                                     channel_multiplier=1))

            where_zero(B4[:, :], [[-1, H1], [-32, 2], [0, 64]])
            where_zero(B8[:, :], [[-32, 2], [-1, 8], [0, 8]])
            step(g.memset(HSEL[:, :], 0.0))
            for half in range(2):
                t = HSEL[HALF[half], 32 * half:32 * half + 8]
                step(g.memset(t, 1.0))
                for pat, mult, base in (([[-8, 8]], 1, 0), ([[8, 8]], -1, 7)):
                    step(g.affine_select(out=t, in_=t, compare_op=ALU.is_ge, fill=0.0, base=base, pattern=pat,
                                         channel_multiplier=mult))
            for c0, c1, row in ((0, 32, 16), (32, 36, 80)):
                t = a_cnt[:, c0:c1]
                step(g.affine_select(out=t, in_=t, compare_op=ALU.not_equal, fill=1.0, base=-row,
                                     pattern=[[0, c1 - c0]], channel_multiplier=1))
            g.sem_inc(built, 1)

            def free(P, i, l, stage):
                g.wait_ge(P.s[l], P.at(i, l, stage))
                g.nop(nofuse=True)

            g.wait_ge(indices_ready, 1)
            g.wait_ge(pdma, 16 * 17)
            cnt = [0]

            def scat_map(i, l, value):
                b = pair(i, l)
                g.tensor_copy(RINGI[:, l, 0, 0:J], SCATI[:, bass.ds(b * J, J)]).then_inc(idx_ready, 1)
                g.tensor_copy(RINGV[:, l, :, :], MAPV[:, bass.ds(b * J, J), :]).then_inc(idx_ready, 1)
                g.wait_ge(idx_ready, value)
                g.nop(nofuse=True)
                for j in range(J):
                    g.indirect_dma_start(MAP, bass.IndirectOffsetOnAxis(RINGI[:, l, 0, j:j + 1], 0),
                                         RINGV[:, l, j, :], None, bounds_check=N - 1, oob_is_err=False)\
                        .then_inc(map_moved[l], 16)

            for l in range(L):
                scat_map(0, l, 2 * (l + 1))
            with g.Fori(0, NB // L - 1) as i:
                for l in range(L):
                    g.wait_ge(map_moved[l], i * (16 * J) + 16 * J)
                    g.nop(nofuse=True)
                    scat_map(i + 1, l, i * (2 * L) + 2 * L + 2 * (l + 1))
            for l in range(L):
                g.wait_ge(map_moved[l], 16 * J * (NB // L))
            g.sem_inc(map_done, 1)
            done = 2 * NB

            J2 = 2 * J

            def gather(P, tile, cols, table, l, k):
                for h in range(2):
                    for j in range(J):
                        c = (2 * j + h) * cols
                        g.indirect_dma_start(tile[l][0:TE, c:c + cols], None, table,
                                             bass.IndirectOffsetOnAxis(RINGI[:, l, k, h * J + j:h * J + j + 1], 0))\
                            .then_inc(P.got[l], 16)

            def indices(l, k, idx, value):
                g.tensor_copy(RINGI[:, l, k, :], idx).then_inc(idx_ready, 1)
                g.wait_ge(idx_ready, value)
                g.nop(nofuse=True)

            def gathers(P, base, used, sets, back=False):
                m = len(sets)

                def one(i, l, value):
                    q = pair(i, l, back)
                    for k, (idx, tile, cols, table) in enumerate(sets):
                        indices(l, k, idx(q), value + k + 1)
                        gather(P, tile, cols, table, l, k)

                for l in range(L):
                    one(0, l, base + m * l)
                with g.Fori(0, P.full - 1) as i:
                    for l in range(L):
                        free(P, i, l, used)
                        one(i + 1, l, i * (m * L) + (base + m * L + m * l))
                for l in range(P.tail):
                    free(P, P.full - 1, l, used)
                    one(P.full, l, base + m * L * P.full + m * l)
                return base + m * NQ

            done = gathers(P0, done, "tT", [
                (lambda q: DSTI[:, bass.ds(q * J2, J2)], TILEO, D, x),
                (lambda q: SRCI[:, bass.ds(q * J2, J2)], TILE, D, x)])

            GR = L * J

            def map_gather(i, value, got):
                g.tensor_copy(RINGI[:, :, 0, 0:J], SRCI[:, bass.ds(i * GR, GR)].rearrange("p (l j) -> p l j", l=L))\
                    .then_inc(idx_ready, 1)
                g.wait_ge(idx_ready, value)
                g.nop(nofuse=True)
                for l in range(L):
                    for j in range(J):
                        g.indirect_dma_start(RINGV[:, l, j, :], None, MAP,
                                             bass.IndirectOffsetOnAxis(RINGI[:, l, 0, j:j + 1], 0))\
                            .then_inc(map_got, 16)
                g.wait_ge(map_got, got)
                g.tensor_copy(MAPV[:, bass.ds(i * GR, GR), :].rearrange("p (l j) k -> p l j k", l=L), RINGV[:, :, :, :])\
                    .then_inc(map_copied, 1)

            for l in range(L):
                g.wait_ge(P0.got[l], 16 * 2 * J2 * P0.n(l))
            with g.Fori(0, NB // L) as i:
                map_gather(i, i + (done + 1), i * (16 * GR) + 16 * GR)
                g.wait_ge(map_copied, i + 1)
                g.nop(nofuse=True)
            done += NB // L

            wait_phase_done(g, PD)
            done = gathers(P1, done, "tT", [(lambda q: MAPV[:, bass.ds(q * J2, J2), 0], TILE, D, T1)], back=True)
            wait_phase_done(g, P1)
            done = gathers(P2, done, "tT", [(lambda q: MAPV[:, bass.ds(q * J2, J2), 1], TILE, D, T2)])
            wait_phase_done(g, P4)

            def one3(i, l, value):
                indices(l, 0, MAPV[:, bass.ds(pair(i, l) * J2, J2), 0], value)
                gather(P3, BIG1, 2 * D, T3, l, 0)

            def scatter3(i, l, value):
                indices(l, 1, SCATI[:, bass.ds(pair(i, l) * J2, J2)], value)
                g.wait_ge(P3.s[l], P3.at(i, l, "rows"))
                g.nop(nofuse=True)
                for h in range(2):
                    for j in range(J):
                        c = (2 * j + h) * D
                        g.indirect_dma_start(out, bass.IndirectOffsetOnAxis(RINGI[:, l, 1, h * J + j:h * J + j + 1], 0),
                                             ROWS[l][0:TE, c:c + D], None, bounds_check=N - 1, oob_is_err=False)\
                            .then_inc(P3.store[l], 16)

            def scattered(l, value):
                g.wait_ge(P3.store[l], value)
                g.nop(nofuse=True)
                g.sem_inc(rows_free[l], 1)

            for l in range(L):
                g.sem_inc(rows_free[l], 1)
                one3(0, l, done + l + 1)
            base = done + L
            for l in range(L):
                free(P3, 0, l, "tT")
                one3(1, l, base + l + 1)
            base += L

            def lane3(i, l, value, more=True):
                if more:
                    free(P3, i + 1, l, "tT")
                    one3(i + 2, l, value)
                scatter3(i, l, value + more)
                if l:
                    scattered(l - 1, i * (16 * J2) + 16 * J2)
                elif not isinstance(i, int) or i > 0:
                    scattered(L - 1, i * (16 * J2))

            for l in range(L):
                lane3(0, l, base + 2 * l + 1)
            base += 2 * L
            with g.Fori(0, P3.full - 3) as i:
                for l in range(L):
                    lane3(i + 1, l, i * (2 * L) + (base + 2 * l + 1))
            base += 2 * L * (P3.full - 3)
            for n in range(P3.full - 2, P3.full + 1):
                for l in range(L):
                    if n < P3.n(l):
                        more = n + 2 < P3.n(l)
                        lane3(n, l, base + 1, more)
                        base += 1 + more

        @block.tensor
        def _(t):
            t.wait_ge(built, 4)

            def after(P, i, l, stage, odd=False):
                t.wait_ge(P.s[l], P.at(i, l, stage))
                if odd:
                    t.nop(nofuse=True)

            def mm(o, a, b, start=True, stop=True):
                return t.matmul(o, a, b, start=start, stop=stop)

            t.wait_ge(starts, 1)
            t.transpose(PA[0][0:1, 0:NB], XS[1][0:NB, W - 1:W], IDN[0:NB, 0:NB]).then_inc(ptr, 1)
            t.wait_ge(starts, 2)
            mm(PA[1][0:NB, 0:1], XS[2][0:1, 0:NB], ONES[0:1, 0:1]).then_inc(ptr, 1)
            t.wait_ge(starts, 3)
            for a, t_in in enumerate(PREP):
                for j in range(J):
                    t.transpose(PB[a][0:TE, j * NB:(j + 1) * NB], t_in[0:NB, j * TE:(j + 1) * TE], IDN[0:NB, 0:NB])\
                        .then_inc(ptr, 1)

            t.wait_ge(wsem, 16 * NWDMA_TOTAL)
            t.wait_ge(derived, 1)
            for h in range(H1):
                a_, b_ = wT[0:64, 64 * h:64 * h + 64], wp[0:64, 64 * h:64 * h + 64]
                for hs in HALF:
                    mm(PA[0][hs, 64 * h:64 * h + 64], a_, b_)
            for hs in HALF:
                for h in range(H1):
                    mm(PB[0][hs, 0:64], wT[0:64, 64 * h:64 * h + 64], wp[0:64, 64 * h:64 * h + 64],
                       start=h == 0, stop=h == H1 - 1)
            for h in range(H1):
                a_ = wT[0:64, 64 * h:64 * h + 64]
                for hs in HALF:
                    mm(PB[1][hs, h:h + 1], a_, att[0:64, h:h + 1])
                    mm(PB[1][hs, 4 + h:5 + h], a_, att[0:64, 4 + h:5 + h])
                    mm(PB[1][hs, 8 + h:9 + h], a_, att[0:64, h:h + 1], stop=False)
                    mm(PB[1][hs, 8 + h:9 + h], a_, att[0:64, 4 + h:5 + h], start=False)
                for b_ in (0, 64):
                    mm(PA[1][b_:b_ + 16, h:h + 1], weT[0:64, 16 * h:16 * h + 16], att[0:64, 8 + h:9 + h])
            for hs in HALF:
                for h in range(H1):
                    mm(PA[2][hs, 0:1], wp[0:64, 64 * h:64 * h + 64], v[f"hb{h}"][0:64, :], start=h == 0,
                       stop=h == H1 - 1)
                mm(PA[2][hs, 1:2], w_e2t[0:64, :], v["m64"][0:64, :])
                mm(PA[2][hs, 2:3], w_o[0:64, :], v["m64"][0:64, :])
                last = mm(PA[3][hs, 0:64], w_oT[0:64, :], CEN[0:64, 0:64])
            last.then_inc(ptr, 1)
            t.wait_ge(derived, 2)
            mm(PB[2][:, 0:1], CEN[:, :], v["t0"])
            mm(PB[3][:, 0:1], w_oc, v["sp0"]).then_inc(ptr, 1)

            def pe(P, i, l, prev, f):
                if (yield P.place(prev)):
                    after(P, i, l, prev)
                    f(l).then_inc(P.s[l], 1)

            def fresh(P, i, l, loads, gathers):
                if loads:
                    t.wait_ge(P.load[l], i * (16 * loads) + 16 * loads)
                if gathers:
                    t.wait_ge(P.got[l], i * (16 * gathers) + 16 * gathers)
                t.wait_ge(P.s[l], P.at(i, l))

            def turn(o, cols_in):
                for j in range(J):
                    last = t.transpose(o[:, j * TE:(j + 1) * TE], cols_in(j), IDN[0:TE, 0:TE])
                return last

            def sum_mm(o, *pairs):
                for k, (a_, b_) in enumerate(pairs):
                    last = mm(o, a_, b_, start=k == 0, stop=k == len(pairs) - 1)
                return last

            def ln_pe(P, i, l, k, prev, ys, cpool=PB, vpool=PA):
                yield from pe(P, i, l, prev, lambda l: sum_mm(cpool[l][:, 0:W], *((CEN[:, :], y[l][:, :]) for y in ys)))
                yield from pe(P, i, l, f"sq{k}", lambda l: mm(vpool[l][:, 0:W], AVG[:, :], SQ[l][:, :]))

            def back_turn(o, y):
                for j in range(J):
                    last = t.transpose(o[0:TE, j * 128:(j + 1) * 128], y[:, j * TE:(j + 1) * TE], IDN[:, :])
                return last

            def outT(P, i, l, prev, y, pool=PA):
                if (yield P.place(prev)):
                    after(P, i, l, prev, True)
                    back_turn(pool[l], y[l]).then_inc(P.s[l], 1)

            def both_tiles(P, i, l, loads, gathers):
                if (yield 0):
                    fresh(P, i, l, loads, gathers)
                    turn(PA[l], lambda j: TILE[l][0:TE, j * 128:(j + 1) * 128])
                    turn(PB[l], lambda j: TILEO[l][0:TE, j * 128:(j + 1) * 128]).then_inc(P.s[l], 1)

            def layer0(i, l):
                P = P0
                yield from both_tiles(P, i, l, 0, 4 * J)
                yield from pe(P, i, l, "cato", lambda l: sum_mm(PA[l][:, 0:W], (w_msgs, XS[l][:, :]), (w_msgd, XD[l][:, :])))
                yield from pe(P, i, l, "agg1", lambda l: sum_mm(PA[l][:, 0:W], (w_updx, XD[l][:, :]), (w_upda, H[l][:, :])))
                yield from ln_pe(P, i, l, 1, "updrelu", (Y,))
                yield from ln_pe(P, i, l, 2, "res1", (Y,))
                yield from outT(P, i, l, "norm2", Y)

            P0.loop(t, layer0)

            def dense(i, l):
                P = PD
                if (yield 0):
                    fresh(P, i, l, 4, 0)
                    mm(PA[l][:, 0:W], w_updx, XD[l][:, :]).then_inc(P.s[l], 1)
                yield from ln_pe(P, i, l, 1, "updrelu", (Y,))
                yield from ln_pe(P, i, l, 2, "res1", (Y,))
                yield from outT(P, i, l, "norm2", Y)
                yield from pe(P, i, l, "rows1", lambda l: mm(PA[l][:, 0:W], g_sum, Y[l][:, :]))
                yield from ln_pe(P, i, l, 3, "elu_res", (H,))
                yield from ln_pe(P, i, l, 4, "res3", (H,))
                yield from outT(P, i, l, "norm4", H)
                yield from pe(P, i, l, "rows2", lambda l: mm(PA[l][:, 0:W], w_skip, H[l][:, :]))
                yield from pe(P, i, l, "xrb", lambda l: mm(PB[l][:, 0:W], w_zx, XS[l][:, :]))
                yield from outT(P, i, l, "u", Y)

            PD.loop(t, dense)

            def head(h):
                return B4[0:36, 128 * h:128 * h + 128]

            def layer1(i, l):
                P = P1
                yield from both_tiles(P, i, l, 10, 2 * J)
                yield from pe(P, i, l, "hold1", lambda l: sum_mm(PB[l][0:36, 0:W], (a_src, XS[l][:, :]), (a_dst, XD[l][:, :]),
                                                         (a_edge, EA[l][:, :])))
                for h in range(H1):
                    def weights(l):
                        mm(PB[l][:, 0:W], head(h), RW[l][0:36, W:2 * W])
                        return mm(PA[l][:, 0:W], head(h), RW[l][0:36, 0:W])
                    yield from pe(P, i, l, "dx" if h == 0 else f"sb{h - 1}", weights)

                def loop_edge(l):
                    mm(PA[l][0:36, 0:W], a_edge, EAS[l][:, :])
                    return mm(PB[l][0:36, 0:W], a_cnt, EAS[l][:, :])
                yield from pe(P, i, l, "sb3", loop_edge)
                yield from pe(P, i, l, "emean", lambda l: mm(PA[l][0:36, 0:W], a_self, XD[l][:, :]))
                for h, prev in ((0, "fac"), (2, "sf1")):
                    def factors(l):
                        mm(PA[l][:, 0:W], head(h), Y[l][0:36, :])
                        return mm(PB[l][:, 0:W], head(h + 1), Y[l][0:36, :])
                    yield from pe(P, i, l, prev, factors)
                yield from pe(P, i, l, "sf3", lambda l: sum_mm(PA[l][:, 0:W], *((g_h[h], S[l][h]) for h in range(H1)),
                                                        (g_sum, XD[l][:, :])))
                yield from ln_pe(P, i, l, 3, "elu_res", (H,))
                yield from ln_pe(P, i, l, 4, "res3", (H,))
                yield from outT(P, i, l, "norm4", H)

            P1.loop(t, layer1)

            def layer2(i, l):
                P = P2
                yield from both_tiles(P, i, l, 12, 2 * J)
                yield from pe(P, i, l, "hold1", lambda l: mm(PA[l][:, 0:W], w_q, XD[l][:, :]))

                def kv(l):
                    sum_mm(PB[l][:, 0:W], (w_k, XS[l][:, :]), (w_ek, EA[l][:, :]))
                    return sum_mm(PA[l][:, 0:W], (w_v, XS[l][:, :]), (w_ev, EA[l][:, :]))
                yield from pe(P, i, l, "qb", kv)
                yield from pe(P, i, l, "vc", lambda l: mm(PA[l][0:40, 0:W], HSEL[:, :], H[l][:, :]))

                def weights(l):
                    mm(PA[l][:, 0:W], B8[0:40, :], RW[l][0:40, W:2 * W])
                    return mm(PB[l][:, 0:W], B8[0:40, :], RW[l][0:40, 0:W])
                yield from pe(P, i, l, "den1", weights)
                yield from pe(P, i, l, "drec", lambda l: mm(PA[l][:, 0:W], B8[0:40, :], SQ[l][0:40, :]))
                yield from pe(P, i, l, "o", lambda l: mm(PB[l][:, 0:W], w_skip, XD[l][:, :]))
                yield from pe(P, i, l, "xrb", lambda l: sum_mm(PA[l][:, 0:W], (w_zx, XS[l][:, :]), (w_zo, S[l][0])))
                if (yield P.place("uq")):
                    after(P, i, l, "uq", True)
                    back_turn(PA[l], XD[l])
                    back_turn(PB[l], Y[l]).then_inc(P.s[l], 1)

            P2.loop(t, layer2)

            def x_and_u(l, tile):
                turn(PA[l], lambda j: tile[l][0:TE, j * 256:j * 256 + 128])
                return turn(PB[l], lambda j: tile[l][0:TE, j * 256 + 128:j * 256 + 256])

            t.wait_ge(fin, 1)
            mm(PA[0][:, 0:2], ADD2, SUMS[:, 0:2]).then_inc(bn_done, 1)
            t.wait_ge(fin, 4)

            def dense3(i, l):
                P = P4
                if (yield 0):
                    fresh(P, i, l, 4, 0)
                    x_and_u(l, BIG1).then_inc(P.s[l], 1)
                yield from ln_pe(P, i, l, 1, "lrelu", (XD, XS), PA, PB)
                yield from pe(P, i, l, "norm1", lambda l: mm(PA[l][:, 0:W], CEN[:, :], Y[l][:, :]))
                yield from pe(P, i, l, "sq2", lambda l: mm(PB[l][:, 0:W], AVG[:, :], SQ[l][:, :]))
                yield from outT(P, i, l, "norm2", Y)

            P4.loop(t, dense3)

            def layer3(i, l):
                P = P3

                def linear(prev, pool, weight, y):
                    yield from pe(P, i, l, prev, lambda l: mm(pool[l][:, 0:W], weight, y[l][:, :]))

                if (yield 0):
                    fresh(P, i, l, 8, 2 * J)
                    for h, pool in enumerate((PA, PB)):
                        last = turn(pool[l], lambda j: BIG1[l][0:TE, (2 * j + h) * 2 * D:(2 * j + h + 1) * 2 * D])
                    last.then_inc(P.s[l], 1)
                yield from pe(P, i, l, "lrelu", lambda l: x_and_u(l, BIG2))
                yield from ln_pe(P, i, l, 1, "olrelu", (XD, XS), PA, PB)
                yield from ln_pe(P, i, l, 3, "norm1", (Y, H), PA, PB)
                yield from linear("norm3", PA, w_e1, MB)
                yield from linear("f1s", PB, w_e2, H)
                yield from linear("f2s", PA, w_n, XD)
                yield from linear("agg1", PB, w_c, XD)
                yield from pe(P, i, l, "cs", lambda l: sum_mm(PA[l][:, 0:W], (w_oc, H[l][:, :]), (CEN[:, :], Y[l][:, :])))
                yield from linear("sq2", PB, AVG[:, :], SQ)
                yield from outT(P, i, l, "norm2", Y)

            P3.loop(t, layer3)

        @block.scalar
        def _(a):
            a.preload_act_table_set("natural_log_exp_and_others")

            def each(P, i, l, prev, o, in_, f, **kw):
                if (yield P.place(prev)):
                    a.wait_ge(P.s[l], P.at(i, l, prev))
                    a.activation(o(l), in_(l), f, **kw).then_inc(P.s[l], 1)

            a.wait_ge(wsem, 16 * NWDMA_TOTAL)
            a.activation(v["sp0"], v["bc"], ACT.Abs).then_inc(bc_steps, 1)
            a.wait_ge(bc_steps, 1)
            a.activation(v["sp0"], v["sp0"], ACT.Exp, scale=-1.0).then_inc(bc_steps, 1)
            a.wait_ge(bc_steps, 2)
            a.activation(v["sp0"], v["sp0"], ACT.Ln, bias=1.0).then_inc(bc_steps, 1)

            a.wait_ge(built, 4)

            def on(buf, rows=128):
                return lambda l: buf[l][0:rows, 0:W]

            def ln_act(P, i, l, k, cpool=PB, vpool=PA):
                yield from each(P, i, l, f"cen{k}", on(SQ), on(cpool), ACT.Square)
                yield from each(P, i, l, f"var{k}", on(SQ), on(vpool), ACT.Ln, bias=v["eps"])
                yield from each(P, i, l, f"ln{k}", on(SQ), on(SQ), ACT.Exp, scale=-0.5)

            def layer0(i, l):
                P = P0
                yield from each(P, i, l, "cat", on(XD), on(PB), ACT.Copy)
                yield from each(P, i, l, "msg", on(WD), on(PA), ACT.Relu, bias=v["bmsg"])
                yield from each(P, i, l, "upd", on(Y), on(PA), ACT.Relu, bias=v["bupd"])
                yield from ln_act(P, i, l, 1)
                yield from ln_act(P, i, l, 2)

            P0.loop(a, layer0)

            def gate(P, i, l):
                yield from each(P, i, l, "zc", on(SQ), on(SQ), ACT.Exp)
                yield from each(P, i, l, "ze", on(SQ), on(SQ), ACT.Ln, bias=1.0)
                yield from each(P, i, l, "zl", on(SQ), on(SQ), ACT.Exp, scale=-1.0)

            def sums(P, i, l, st):
                for k, prev, f in ((0, "um", ACT.Copy), (1, "us", ACT.Square)):
                    if (yield P.place(prev)):
                        a.wait_ge(P.s[l], P.at(i, l, prev))
                        a.activation(WD[l][:, :], SQ[l][:, :], f, accum_out=st[:, k, bass.ds(pair(i, l), 1)])\
                            .then_inc(P.s[l], 1)

            def xu_rows(l, k):
                return ROWS[l][0:TE, :].rearrange("p (jh k c) -> p jh k c", k=2, c=D)[:, :, k, :]

            def tile_rows(pool, l):
                return pool[l][0:TE, 0:J * 128].rearrange("p (jh c) -> p jh c", c=D)

            def dense(i, l):
                P = PD
                yield from each(P, i, l, "upd", on(Y), on(PA), ACT.Relu, bias=v["bupd"])
                yield from ln_act(P, i, l, 1)
                yield from ln_act(P, i, l, 2)
                if (yield P.place("outT1")):
                    a.wait_ge(P.store[l], i * (16 * P.stores) + 16 * P.stores)
                    a.wait_ge(P.s[l], P.at(i, l, "outT1"))
                    a.activation(TILE[l][0:TE, :], PA[l][0:TE, 0:J * 128], ACT.Copy).then_inc(P.s[l], 1)
                yield from each(P, i, l, "elu_n", on(SQ), on(SQ), ACT.Exp)
                yield from ln_act(P, i, l, 3)
                yield from ln_act(P, i, l, 4)
                yield from each(P, i, l, "outT2", lambda l: xu_rows(l, 0), lambda l: tile_rows(PA, l), ACT.Copy)
                yield from each(P, i, l, "xr", on(XS), on(PA), ACT.Identity, bias=v["bskip"])
                yield from gate(P, i, l)
                yield from each(P, i, l, "outT3", lambda l: xu_rows(l, 1), lambda l: tile_rows(PA, l), ACT.Copy)
                yield from sums(P, i, l, STATD)

            PD.loop(a, dense)

            def layer1(i, l):
                P = P1
                yield from each(P, i, l, "logit", on(Y, 36), on(PB, 36), ACT.Copy)
                yield from each(P, i, l, "dw", lambda l: RW[l][0:36, :], lambda l: RW[l][0:36, :], ACT.Exp)
                yield from each(P, i, l, "esum", on(SQ, 36), on(PB, 36), ACT.Ln)
                yield from each(P, i, l, "lcnt", on(SQ, 36), on(SQ, 36), ACT.Exp, scale=-1.0)
                yield from each(P, i, l, "g2", lambda l: RW[l][0:36, :], lambda l: RW[l][0:36, :], ACT.Exp)
                yield from each(P, i, l, "dsum", on(Y, 36), on(Y, 36), ACT.Ln)
                yield from each(P, i, l, "dln", on(Y, 36), on(Y, 36), ACT.Exp, scale=-1.0)
                yield from each(P, i, l, "elu_n", on(SQ), on(SQ), ACT.Exp)
                yield from ln_act(P, i, l, 3)
                yield from ln_act(P, i, l, 4)

            P1.loop(a, layer1)

            def layer2(i, l):
                P = P2
                yield from each(P, i, l, "q", on(Y), on(PA), ACT.Identity, bias=v["bq"])
                yield from each(P, i, l, "qk", on(WD), on(PA), ACT.Copy)
                yield from each(P, i, l, "logit", on(SQ, 40), on(PA, 40), ACT.Copy, scale=float(H2) ** -0.5)
                yield from each(P, i, l, "dw", lambda l: RW[l][0:40, :], lambda l: RW[l][0:40, :], ACT.Exp)
                yield from each(P, i, l, "s1", on(SQ, 40), on(Y, 40), ACT.Ln, bias=v["tiny"][0:40, :])
                yield from each(P, i, l, "dln", on(SQ, 40), on(SQ, 40), ACT.Exp, scale=-1.0)
                yield from each(P, i, l, "xr", on(XS), on(PB), ACT.Identity, bias=v["bskip"])
                yield from gate(P, i, l)
                yield from sums(P, i, l, STATE)
                yield from each(P, i, l, "rows", lambda l: xu_rows(l, 1), lambda l: tile_rows(PB, l), ACT.Copy)

            P2.loop(a, layer2)

            a.wait_ge(fin, 4)
            a.activation(v["bs"], v["var"], ACT.Ln, bias=v["eps"]).then_inc(fin, 1)
            a.wait_ge(fin, 5)
            a.activation(v["bs"], v["bs"], ACT.Exp, scale=-0.5).then_inc(fin, 1)

            def last_ln(P, i, l, bias):
                yield from each(P, i, l, "cen2", on(H), on(PA), ACT.Identity, bias=bias)
                yield from each(P, i, l, "cb2", on(SQ), on(H), ACT.Square)
                yield from each(P, i, l, "var2", on(SQ), on(PB), ACT.Ln, bias=v["eps"])
                yield from each(P, i, l, "ln2", on(SQ), on(SQ), ACT.Exp, scale=-0.5)

            def dense3(i, l):
                yield from ln_act(P4, i, l, 1, PA, PB)
                yield from last_ln(P4, i, l, v["cvec"])

            P4.loop(a, dense3)

            def layer3(i, l):
                P = P3

                def ssp(k, pool, bias):
                    yield from each(P, i, l, k, on(SQ), on(pool), ACT.Abs, bias=bias)
                    yield from each(P, i, l, f"{k}a", on(SQ), on(SQ), ACT.Exp, scale=-1.0)
                    yield from each(P, i, l, f"{k}e", on(SQ), on(SQ), ACT.Ln, bias=1.0)

                yield from ln_act(P, i, l, 1, PA, PB)
                yield from ln_act(P, i, l, 3, PA, PB)
                yield from ssp("f1", PA, v["be1"])
                yield from ssp("f2", PB, v["be2"])
                yield from each(P, i, l, "h", on(XS), on(PA), ACT.Identity, bias=v["bn"])
                yield from ssp("c", PB, v["bc"])
                yield from last_ln(P, i, l, v["cb"])

            P3.loop(a, layer3)

        @block.vector
        def _(d):
            chain = [0]

            def link(ins):
                chain[0] += 1
                ins.then_inc(dve_link, 1)
                d.wait_ge(dve_link, chain[0])

            R_ = slice(0, NB)
            i32 = lambda t: t[R_, 0:W].bitcast(I32)
            d.wait_ge(pdma, 16 * 11)
            link(d.tensor_tensor(Y[0][R_, :], i32(XD[0]), i32(XD[1]), ALU.is_equal))
            link(d.tensor_tensor(Y[2][R_, :], i32(XD[0]), i32(XD[2]), ALU.is_equal))
            link(d.tensor_scalar(Y[1][R_, :], Y[0][R_, :], -1.0, 1.0, ALU.mult, ALU.add))
            link(d.tensor_scalar(Y[3][R_, :], Y[2][R_, :], -1.0, 1.0, ALU.mult, ALU.add))
            link(d.tensor_scalar(H[0][R_, :], Y[1][R_, :], NEG, None, ALU.mult))
            link(d.tensor_scalar(H[1][R_, :], Y[3][R_, :], NEG, None, ALU.mult))
            d.sem_inc(masks_ready, 1)
            d.wait_ge(built, 4)
            link(d.tensor_copy(H[2][R_, :], i32(XS[0])))
            link(d.tensor_tensor(H[2][R_, :], H[2][R_, :], Y[1][R_, :], ALU.mult))
            link(d.tensor_tensor_scan(XS[1][R_, :], H[2][R_, :], H[2][R_, :], 0.0, ALU.max, ALU.max))
            d.sem_inc(starts, 1)
            d.wait_ge(ptr, 1)
            link(d.memset(XS[2][0:1, 0:1], 0.0))
            link(d.tensor_copy(XS[3][0:1, 0:NB], PA[0][0:1, 0:NB]))
            link(d.tensor_tensor_scan(XS[2][0:1, 1:NB + 1], XS[3][0:1, 0:NB], XS[3][0:1, 0:NB], 0.0, ALU.max, ALU.max))
            d.sem_inc(starts, 1)
            d.wait_ge(ptr, 2)
            link(d.tensor_copy(CAR[R_, 9:10], PA[1][R_, 0:1]))
            link(d.tensor_scalar(PREP[3][R_, :], XS[1][R_, :], CAR[R_, 9:10], float(N), ALU.max, ALU.add))
            link(d.tensor_copy(PREP[0][R_, :], i32(XD[3])))
            link(d.tensor_copy(PREP[1][R_, :], i32(XD[0])))
            link(d.tensor_scalar(H[3][R_, :], Y[2][R_, :], FAR, None, ALU.mult))
            link(d.tensor_tensor(PREP[2][R_, :], PREP[1][R_, :], H[3][R_, :], ALU.add))
            d.sem_inc(starts, 1)
            for k, o in enumerate((SRCI[:, :], DSTI[:, :], SCATI[:, :], MAPV[:, :, 1])):
                d.wait_ge(ptr, 2 + J * (k + 1))
                link(d.tensor_copy(o.rearrange("p (b j) -> p j b", j=J),
                                   PB[k][0:TE, 0:J * NB].rearrange("p (j b) -> p j b", j=J)))
            d.sem_inc(indices_ready, 1)
            link(d.tensor_tensor(CEN[:, :], IDN[:, :], AVG[:, :], ALU.subtract))
            d.wait_ge(wsem, 16 * NWDMA_TOTAL)
            d.sem_inc(derived, 1)
            link(d.tensor_tensor(v["wb"], v["wb2"], v["wb3"], ALU.subtract))
            link(d.tensor_tensor(v["wcol"], v["wb1"], v["wb3"], ALU.add))
            link(d.tensor_scalar(w_zx, AVG[:, :], v["wb"], float(D), ALU.mult, ALU.mult))
            link(d.tensor_scalar(w_zo, AVG[:, :], v["wcol"], float(D), ALU.mult, ALU.mult))
            link(d.tensor_tensor(ROWS[0][0:1, 0:128], ROWS[0][0:1, 0:128], ROWS[1][0:1, 0:128], ALU.add))
            d.sem_inc(bias_row, 1)
            d.wait_ge(ptr, 2 + 4 * J + 1)
            for hs in HALF:
                for h in range(H1):
                    link(d.tensor_copy(g_h[h][hs, hs], PA[0][hs, 64 * h:64 * h + 64]))
                link(d.tensor_copy(g_sum[hs, hs], PB[0][hs, 0:64]))
                c = 0 if hs.start == 0 else 32
                for k, m in enumerate((a_src, a_dst, a_self)):
                    link(d.tensor_copy(m[hs, c:c + 4], PB[1][hs, 4 * k:4 * k + 4]))
                link(d.tensor_copy(a_edge[hs.start:hs.start + 16, c:c + 4], PA[1][hs.start:hs.start + 16, 0:4]))
                link(d.tensor_copy(w_oc[hs, hs], PA[3][hs, 0:64]))
            link(d.tensor_tensor(v["bproj"], v["bp"], PA[2][:, 0:1], ALU.add))
            link(d.tensor_tensor(v["be2"], v["be2"], PA[2][:, 1:2], ALU.add))
            link(d.tensor_tensor(v["t0"], v["bo"], PA[2][:, 2:3], ALU.add))
            d.wait_ge(bc_steps, 3)
            link(d.tensor_scalar(v["t1"], v["bc"], 0.0, None, ALU.max))
            link(d.tensor_tensor(v["sp0"], v["sp0"], v["t1"], ALU.add))
            d.sem_inc(derived, 1)
            d.wait_ge(ptr, 2 + 4 * J + 2)
            link(d.tensor_copy(v["cb"], PB[2][:, 0:1]))
            link(d.tensor_tensor(v["cvec"], v["cb"], PB[3][:, 0:1], ALU.add))
            d.sem_inc(wdone, 1)

            def stage(P, i, l, prev, f):
                if (yield P.place(prev)):
                    d.wait_ge(P.s[l], P.at(i, l, prev))
                    f(l).then_inc(P.s[l], 1)

            def scans(P, i, l, prev, me, carry, col, out_, data0, data1, rows, real, op0=ALU.mult, op1=ALU.add,
                      back=False, before=None):
                order = (1, 0) if back else (0, 1)
                step = -1 if back else 1
                for k, b in enumerate(order):
                    rs = rows[b]
                    before_scan = prev if k == 0 else me[0]
                    if not (yield P.place(before_scan)):
                        continue
                    d.wait_ge(P.s[l], P.at(i, l, before_scan))
                    d.wait_ge(CARRY[carry], i * (2 * L) + (carried[carry] + 2 * l + k))
                    if before:
                        c0 = before(l)
                        d.tensor_copy(c0[rs, :], CAR[rs, col:col + 1]).then_inc(P.s[l], 1)
                        d.wait_ge(P.s[l], P.at(i, l, before_names[k]))
                    d.tensor_tensor_scan(out_(l)[rs, ::step], data0(l)[rs, ::step], data1(l)[rs, ::step],
                                         CAR[rs, col:col + 1], op0, op1).then_inc(P.s[l], 1)
                    d.wait_ge(P.s[l], P.at(i, l, me[k]))
                    e = 0 if back else W - 1
                    d.tensor_copy(CAR[real[1 - b], col:col + 1], out_(l)[real[b], e:e + 1]).then_inc(CARRY[carry], 1)
                    if k == 1:
                        d.wait_ge(CARRY[carry], i * (2 * L) + (carried[carry] + 2 * l + 2))

            before_names = ("mc0", "mc1")
            R64 = (slice(0, 64), slice(64, 128))
            R4, R4R = (slice(0, 32), slice(32, 36)), (slice(0, 4), slice(32, 36))
            R8, R8R = (slice(0, 32), slice(32, 40)), (slice(0, 8), slice(32, 40))

            def handed_on(*names):
                for n_ in names:
                    d.wait_ge(CARRY[n_], carried[n_] + NB)

            carried = {n_: 1 + CARRY_COUNT * k for k, n_ in enumerate(CARRY)}
            for n_, s_ in CARRY.items():
                d.sem_inc(s_, carried[n_])

            def on(buf, rows=128, c0=0):
                return lambda l: buf[l][0:rows, c0:c0 + W]

            def tt(P, i, l, prev, o, a_, b_, op):
                yield from stage(P, i, l, prev, lambda l: d.tensor_tensor(o(l), a_(l), b_(l), op))

            def ln_dve(P, i, l, k, y, aff=None, pool=PB):
                yield from tt(P, i, l, f"rstd{k}", on(y), on(pool), on(SQ), ALU.mult)
                if aff:
                    g_, b_, res = aff
                    yield from stage(P, i, l, f"norm{k}", lambda l: d.tensor_scalar(y[l][:, :], y[l][:, :], v[g_], v[b_],
                                                                             ALU.mult, ALU.add))
                    yield from tt(P, i, l, f"aff{k}", on(y), on(y), on(res), ALU.add)

            def rows_out(P, i, l):
                if (yield P.place("outT")):
                    if P.credit:
                        d.wait_ge(P.store[l], i * (16 * P.stores) + 16 * P.stores)
                    else:
                        d.wait_ge(rows_free[l], i + 1)
                    d.wait_ge(P.s[l], P.at(i, l, "outT"))
                    d.tensor_copy(ROWS[l][0:TE, 0:J * 128], PA[l][0:TE, 0:J * 128]).then_inc(P.s[l], 1)

            def cat(P, i, l, prev="tT", o=XS):
                yield from stage(P, i, l, prev, lambda l: d.tensor_copy(o[l][:, :], PA[l][:, 0:W]))

            def loaded(P, i, l, prev, n):
                if (yield P.place(prev)):
                    d.wait_ge(P.load[l], i * (16 * n) + 16 * n)

            def layer0(i, l):
                P = P0
                yield from cat(P, i, l)
                yield from loaded(P, i, l, "relu", 2)
                yield from scans(P, i, l, "relu", ("agg0", "agg1"), "agg0", 0, on(H), on(MA), on(WD), R64, R64)
                yield from ln_dve(P, i, l, 1, Y, ("g0", "b0", XD))
                yield from ln_dve(P, i, l, 2, Y)
                yield from rows_out(P, i, l)

            P0.loop(d, layer0)

            handed_on("agg0")
            wait_phase_done(d, P0)
            d.wait_ge(noe_dma, 16 * MC5)
            for b, o in zip(MAPBUF, NOEBUF):
                link(d.tensor_scalar(o[0:MP, 0:W // 2], b.rearrange("p (n k) -> p n k", k=2)[:, :, 0],
                                     float(N), None, ALU.is_lt))
            d.sem_inc(noe_ready, 1)

            def elu(P, i, l, o, res):
                yield from stage(P, i, l, "proj", lambda l: d.tensor_scalar(SQ[l][:, :], PA[l][:, 0:W], v["bproj"], 0.0,
                                                                     ALU.add, ALU.min))
                yield from stage(P, i, l, "elu_e", lambda l: d.tensor_scalar(o[l][:, :], PA[l][:, 0:W], v["bproj"], 0.0,
                                                                      ALU.add, ALU.max))
                yield from stage(P, i, l, "elu_p", lambda l: d.scalar_tensor_tensor(
                    out=o[l][:, :], in0=SQ[l][:, :], scalar=-1.0, in1=o[l][:, :], op0=ALU.add, op1=ALU.add))
                yield from tt(P, i, l, "elu", on(o), on(o), on(res), ALU.add)

            def zclip(P, i, l, pool):
                yield from stage(P, i, l, "z", lambda l: d.tensor_scalar(SQ[l][:, :], pool[l][:, 0:W], -1.0, 40.0, ALU.mult,
                                                                  ALU.min))

            def leaky(P, i, l, prev, buf, slope, rows=128):
                yield from stage(P, i, l, prev, lambda l: d.scalar_tensor_tensor(
                    out=buf[l][0:rows, 0:W], in0=buf[l][0:rows, 0:W], scalar=slope, in1=buf[l][0:rows, 0:W],
                    op0=ALU.mult, op1=ALU.max))

            def dense(i, l):
                P = PD
                yield from ln_dve(P, i, l, 1, Y, ("g0", "b0", XD))
                yield from ln_dve(P, i, l, 2, Y)
                yield from elu(P, i, l, H, Y)
                yield from ln_dve(P, i, l, 3, H, ("g1", "b1", Y))
                yield from ln_dve(P, i, l, 4, H)
                yield from zclip(P, i, l, PB)
                yield from tt(P, i, l, "zg", on(Y), on(SQ), on(XS), ALU.mult)
                yield from tt(P, i, l, "rows3", on(SQ), on(Y), on(MA), ALU.mult)

            PD.loop(d, dense)

            def held(P, i, l, back):
                yield from cat(P, i, l)
                yield from tt(P, i, l, "cat", on(H), on(PB), on(MB), ALU.mult)
                yield from scans(P, i, l, "own", ("hold0", "hold1"), "hold1" if back else "hold2", 1, on(XD), on(MA), on(H),
                      R64, R64, back=back)

            def layer1(i, l):
                P = P1
                yield from held(P, i, l, True)
                n = 36
                yield from leaky(P, i, l, "lg", Y, 0.2, n)
                yield from scans(P, i, l, "leaky", ("mx0", "mx1"), "mx1", 2, on(MX), on(MC), on(Y), R4, R4R, ALU.add, ALU.max,
                      back=True, before=lambda l: MX[l][:, W:W + 1])
                yield from tt(P, i, l, "mx1", on(RW, n), on(MX, n, 1), on(MX, n), ALU.subtract)
                yield from tt(P, i, l, "dr", on(RW, n), on(RW, n), on(MC, n), ALU.add)
                yield from tt(P, i, l, "drn", on(RW, n, W), on(Y, n), on(MX, n), ALU.subtract)
                yield from scans(P, i, l, "exp", ("den0", "den1"), "den1", 3, on(H), on(RW), on(RW, 128, W), R4, R4R, back=True)
                yield from scans(P, i, l, "den1", ("eas0", "eas1"), "eas1", 4, on(EAS), on(MA), on(EA), R64, R64, back=True)
                yield from tt(P, i, l, "eas1", on(XS), on(XS), on(XD), ALU.subtract)
                for h in range(H1):
                    yield from tt(P, i, l, f"b{h}", on(WD), on(PB), on(XS), ALU.mult)
                    yield from scans(P, i, l, f"wd{h}", (f"sa{h}", f"sb{h}"), f"s1{h}", 5 + h, lambda l: S[l][h],
                          on(PA), on(WD), R64, R64, back=True)
                yield from tt(P, i, l, "rcnt", on(SQ, n), on(PA, n), on(SQ, n), ALU.mult)
                yield from tt(P, i, l, "sself", on(SQ, n), on(PA, n), on(SQ, n), ALU.add)
                yield from leaky(P, i, l, "sadd", SQ, 0.2, n)
                yield from tt(P, i, l, "sleaky", on(Y, n), on(MX, n), on(SQ, n), ALU.max)
                yield from tt(P, i, l, "mfin", on(RW, n), on(MX, n), on(Y, n), ALU.subtract)
                yield from tt(P, i, l, "g1", on(RW, n, W), on(SQ, n), on(Y, n), ALU.subtract)
                yield from tt(P, i, l, "gexp", on(Y, n), on(H, n), on(RW, n), ALU.mult)
                yield from tt(P, i, l, "dfac", on(Y, n), on(Y, n), on(RW, n, W), ALU.add)
                yield from tt(P, i, l, "drec", on(Y, n), on(Y, n), on(RW, n), ALU.mult)
                for h, prev, pool in ((0, "bf0", PA), (1, "sf0", PB), (2, "bf2", PA), (3, "sf2", PB)):
                    yield from tt(P, i, l, prev, lambda l: S[l][h], lambda l: S[l][h], on(pool), ALU.mult)
                yield from elu(P, i, l, H, XD)
                yield from ln_dve(P, i, l, 3, H, ("g1", "b1", XD))
                yield from ln_dve(P, i, l, 4, H)
                yield from rows_out(P, i, l)

            P1.loop(d, layer1)
            handed_on("hold1", "mx1", "den1", "eas1", "s10", "s11", "s12", "s13")

            def layer2(i, l):
                P = P2
                yield from held(P, i, l, False)
                n = 40
                yield from tt(P, i, l, "kv", on(H), on(PB), on(Y), ALU.mult)
                yield from scans(P, i, l, "lg", ("mx0", "mx1"), "mx2", 2, on(MX, 128, 1), on(MC), on(SQ), R8, R8R, ALU.add,
                      ALU.max, before=lambda l: MX[l][:, 0:1])
                yield from tt(P, i, l, "mx1", on(RW, n), on(MX, n), on(MX, n, 1), ALU.subtract)
                yield from tt(P, i, l, "dr", on(RW, n), on(RW, n), on(MC, n), ALU.add)
                yield from tt(P, i, l, "drn", on(RW, n, W), on(SQ, n), on(MX, n, 1), ALU.subtract)
                yield from scans(P, i, l, "exp", ("den0", "den1"), "den2", 3, on(Y), on(RW), on(RW, 128, W), R8, R8R)
                yield from tt(P, i, l, "b", on(WD), on(WD), on(PA), ALU.mult)
                yield from scans(P, i, l, "wv", ("s0", "s1"), "s2", 5, lambda l: S[l][0], on(PB), on(WD), R64, R64)
                yield from tt(P, i, l, "bd", lambda l: S[l][0], lambda l: S[l][0], on(PA), ALU.mult)
                yield from zclip(P, i, l, PA)
                yield from tt(P, i, l, "zg", on(WD), on(XS), lambda l: S[l][0], ALU.subtract)
                yield from tt(P, i, l, "df", on(WD), on(WD), on(SQ), ALU.mult)
                yield from tt(P, i, l, "gd", on(Y), lambda l: S[l][0], on(WD), ALU.add)
                yield from tt(P, i, l, "u", on(SQ), on(Y), lambda l: S[l][3], ALU.mult)
                if (yield P.place("outT")):
                    d.wait_ge(P.store[l], i * (16 * P.stores) + 16 * P.stores)
                    d.wait_ge(P.s[l], P.at(i, l, "outT"))
                    d.tensor_copy(ROWS[l][0:TE, :].rearrange("p (jh k c) -> p jh k c", k=2, c=D)[:, :, 0, :],
                                  PA[l][0:TE, 0:J * 128].rearrange("p (jh c) -> p jh c", c=D)).then_inc(P.s[l], 1)

            P2.loop(d, layer2)
            handed_on("hold2", "mx2", "den2", "s2")

            for l in range(L):
                d.wait_ge(P2.s[l], P2.end(l))
            link(d.tensor_tensor(ADD2[:, 0:64], IDN[:, 0:64], IDN[:, 64:128], ALU.add))
            link(d.tensor_copy(ADD2[:, 64:128], ADD2[:, 0:64]))
            link(d.tensor_reduce(SUMS[:, 0:2], STATD[:, :, :], AX.X, ALU.add))
            link(d.tensor_reduce(SUMS[:, 2:4], STATE[:, :, :], AX.X, ALU.add))
            link(d.tensor_tensor(SUMS[:, 0:2], SUMS[:, 0:2], SUMS[:, 2:4], ALU.add))
            d.sem_inc(fin, 1)
            d.wait_ge(bn_done, 1)
            link(d.tensor_scalar(v["mean"], PA[0][:, 0:1], 1.0 / N, None, ALU.mult))
            link(d.tensor_scalar(v["var"], PA[0][:, 1:2], 1.0 / N, None, ALU.mult))
            link(d.tensor_tensor(v["t0"], v["mean"], v["mean"], ALU.mult))
            link(d.tensor_tensor(v["var"], v["var"], v["t0"], ALU.subtract))
            d.sem_inc(fin, 3)
            d.wait_ge(fin, 6)
            link(d.tensor_tensor(v["bs"], v["bs"], v["g2"], ALU.mult))
            link(d.tensor_tensor(v["t0"], v["mean"], v["bs"], ALU.mult))
            link(d.tensor_tensor(v["bt"], v["b2"], v["t0"], ALU.subtract))

            def x_and_u(P, i, l, turned, copied, scaled, x_, u_):
                yield from cat(P, i, l, turned, x_)
                yield from stage(P, i, l, copied, lambda l: d.tensor_scalar(u_[l][:, :], PB[l][:, 0:W], v["bs"], v["bt"],
                                                                     ALU.mult, ALU.add))
                yield from leaky(P, i, l, scaled, u_, 0.01)

            def dense3(i, l):
                P = P4
                yield from x_and_u(P, i, l, "tT", "cat", "catu", XD, XS)
                yield from ln_dve(P, i, l, 1, Y, pool=PA)
                yield from tt(P, i, l, "rstd2", on(Y), on(H), on(SQ), ALU.mult)
                yield from rows_out(P, i, l)

            P4.loop(d, dense3)

            def layer3(i, l):
                P = P3

                def ssp(k, pool, bias, o):
                    yield from stage(P, i, l, f"{k}l", lambda l: d.tensor_scalar(o[l][:, :], pool[l][:, 0:W], v[bias], 0.0,
                                                                          ALU.add, ALU.max))
                    yield from tt(P, i, l, f"{k}r", on(o), on(o), on(SQ), ALU.add)

                for h, prev, pool in ((0, "tT", PA), (1, "cat0", PB)):
                    yield from stage(P, i, l, prev, lambda l: d.tensor_copy(XD[l][R64[h], :], pool[l][0:64, 0:W]))
                for h, prev, pool in ((0, "cat1", PA), (1, "catu0", PB)):
                    yield from stage(P, i, l, prev, lambda l: d.tensor_scalar(
                        XS[l][R64[h], :], pool[l][64:128, 0:W], v["bs"][64:128, :], v["bt"][64:128, :], ALU.mult, ALU.add))
                yield from leaky(P, i, l, "catu1", XS, 0.01)
                yield from x_and_u(P, i, l, "oT", "ocat", "ocatu", Y, H)
                yield from ln_dve(P, i, l, 1, XD, pool=PA)
                yield from ln_dve(P, i, l, 3, Y, pool=PA)
                yield from ssp("f1", PA, "be1", H)
                yield from ssp("f2", PB, "be2", H)
                yield from stage(P, i, l, "hb", lambda l: d.scalar_tensor_tensor(
                    out=XS[l][:, :], in0=H[l][:, :], scalar=-LN2, in1=XS[l][:, :], op0=ALU.add, op1=ALU.mult))
                yield from scans(P, i, l, "msg", ("agg0", "agg1"), "agg3", 1, on(XD), on(MA), on(XS), R64, R64)
                yield from ssp("c", PB, "bc", H)
                yield from tt(P, i, l, "rstd2", on(Y), on(H), on(SQ), ALU.mult)
                yield from rows_out(P, i, l)

            P3.loop(d, layer3)


_WEIGHTS = ['L0_gnn_W_msg', 'L0_gnn_b_msg', 'L0_gnn_W_upd', 'L0_gnn_b_upd', 'L0_gnn_gamma', 'L0_gnn_beta',
            'L1_gnn_bias', 'L1_gnn_Wp', 'L1_gnn_bp', 'L1_gnn_gamma', 'L1_gnn_beta', 'L2_gnn_Wq', 'L2_gnn_bq',
            'L2_gnn_Wk', 'L2_gnn_bk', 'L2_gnn_Wv', 'L2_gnn_bv', 'L2_gnn_We', 'L2_gnn_be', 'L2_gnn_Wskip',
            'L2_gnn_bskip', 'L2_gnn_Wbeta', 'L2_gnn_gamma', 'L2_gnn_beta_bn', 'L3_gnn_We1', 'L3_gnn_be1',
            'L3_gnn_We2', 'L3_gnn_be2', 'L3_gnn_Wn', 'L3_gnn_bn', 'L3_gnn_Wc', 'L3_gnn_bc', 'L3_gnn_Wo',
            'L3_gnn_bo']
_TURNED = {'WT': 'L1_gnn_W', 'WeT': 'L1_gnn_W_edge', 'att_srcT': 'L1_gnn_att_src', 'att_dstT': 'L1_gnn_att_dst',
           'att_edgeT': 'L1_gnn_att_edge', 'WoT': 'L3_gnn_Wo'}


def kernel(**inputs):
    import numpy as _np
    import concourse.bacc as _bacc
    from concourse import mybir as _mybir
    from concourse.bass_utils import run_bass_kernel_spmd as _run

    nc = _bacc.Bacc("TRN2", target_bir_lowering=False, num_devices=1)
    arrays, aps = {}, {}

    def give(name, a):
        a = _np.ascontiguousarray(a)
        arrays[name] = a
        aps[name] = nc.dram_tensor(name, a.shape, _mybir.dt.from_np(a.dtype), kind="ExternalInput").ap()

    for name in ("x", "src", "dst"):
        give(name, _np.asarray(inputs[name]))
    give("xT", _np.asarray(inputs["x"]).T)
    give("ea16T", _np.asarray(inputs["edge_attr_16"]).T)
    give("ea64T", _np.asarray(inputs["edge_attr_64"]).T)
    for name in _WEIGHTS:
        give(name, _np.asarray(inputs[name]))
    for name, of in _TURNED.items():
        give(name, _np.asarray(inputs[of]).T)
    out = nc.dram_tensor("out", (N, D), F32, kind="ExternalOutput").ap()
    program(nc, aps["x"], aps["xT"], aps["src"], aps["dst"], aps["ea16T"], aps["ea64T"], aps, out)
    r = _run(nc, [arrays], core_ids=[0])
    return r.results[0]["out"]
```

```python
from contextlib import ExitStack

import numpy as np
import concourse.bass as bass
from concourse import mybir
from concourse.alu_op_type import AluOpType as ALU

F32 = mybir.dt.float32
I32 = mybir.dt.int32
ACT = mybir.ActivationFunctionType
AX = mybir.AxisListType

N, E, D = 100000, 50000, 64
W = 500
TE = 125
J = W // TE
L = 4
NB = E // W
NQ = NB // 2
H1, H2 = 4, 8
EPS = 1e-5
LN2 = float(np.log(2.0))
NEG = -1.0e30
FAR = float(1 << 23)
MP, MN = 80, N // 80


FIRST_COUNT = [1 + 1000 * l for l in range(L)]
CARRY_COUNT = 128


PACE = {
    "l0": ((0, 77, 208, 338),
           (10, 11, 1, 30, 19, 13, 3, 54, 15, 16, 5, 1, 15, 1, 7, 19, 45, 44, 7, 24, 1, 19, 18, 17)),
    "d1": ((0, 34, 239, 321),
           (12, 9, 12, 7, 12, 11, 7, 3, 3, 16, 11, 12, 7, 7, 7, 10, 12, 7, 7, 5, 7, 7, 8, 7, 12, 11, 7, 5, 7,
               12, 7, 12, 7, 7, 7, 12, 16, 1, 7, 12, 7, 7, 9, 7, 7, 12, 7, 7, 7)),
    "l1": ((0, 186, 373, 558),
           (30, 7, 11, 1, 7, 32, 7, 7, 7, 7, 5, 7, 7, 7, 7, 14, 7, 9, 9, 5, 9, 12, 1, 7, 7, 7, 1, 5, 1, 7, 7,
               12, 1, 7, 7, 7, 12, 2, 7, 7, 9, 22, 7, 7, 7, 12, 7, 7, 15, 9, 7, 7, 5, 15, 7, 3, 7, 12, 2, 7, 7, 8,
               1, 7, 7, 52, 5, 5, 7, 10, 1, 20, 5, 9, 7, 7, 12, 22, 12, 9, 7, 15, 12, 5)),
    "l2": ((0, 170, 338, 503),
           (54, 5, 31, 10, 23, 1, 5, 5, 15, 28, 11, 42, 17, 1, 1, 19, 9, 29, 1, 7, 9, 5, 25, 22, 13, 9, 16, 1,
               5, 1, 11, 4, 12, 15, 7, 23, 24, 15, 30, 1, 15, 1, 15, 3, 22, 19, 18, 13, 1, 1)),
    "d3": ((0, 306, 451, 614),
           (58, 58, 42, 52, 60, 60, 56, 6, 36, 34, 50, 43, 18, 60, 15, 56, 30, 27, 32)),
    "l3": ((0, 176, 345, 521),
           (22, 5, 13, 1, 1, 5, 24, 3, 7, 7, 12, 23, 14, 1, 33, 23, 28, 5, 18, 13, 9, 5, 16, 25, 19, 3, 23, 13,
               1, 7, 19, 1, 9, 13, 1, 19, 23, 3, 23, 20, 11, 1, 11, 7, 13, 27, 3, 19, 12, 1, 31, 3, 22, 23)),
}


class Chain:

    def __init__(self, *stages):
        self.stages = stages
        self.k = len(stages)

    def at(self, i, lane, stage=None):
        return i * self.k + (FIRST_COUNT[lane] + (self.stages.index(stage) + 1 if stage else 0))


LN_STEPS = ("cen", "sq", "var", "ln", "rstd", "norm")


def ln_names(k):
    return tuple(f"{s}{k}" for s in LN_STEPS)


def program(nc, x, xT, src, dst, ea16T, ea64T, w, out):
    ctx = ExitStack()
    with ctx:
        def sb(name, shape, dt=F32):
            return ctx.enter_context(nc.sbuf_tensor(name, shape, dt))

        def sem(name):
            return ctx.enter_context(nc.semaphore(name))

        T1 = nc.dram_tensor("T1", (N + E, D), F32).ap()
        T2 = nc.dram_tensor("T2", (N + E, D), F32).ap()
        T3 = nc.dram_tensor("T3", (N + E, 2 * D), F32).ap()
        TU = nc.dram_tensor("TU", (N, D), F32).ap()
        MAP = nc.dram_tensor("MAP", (N, 2), I32).ap()
        MASKS = nc.dram_tensor("MASKS", (6, E), F32).ap()
        SAME, FIRST, SAMEN, LAST, NEGP, NEGN = range(6)

        def lanes(name, cols, dt=F32):
            return [sb(f"{name}{l}", [128, cols], dt) for l in range(L)]

        XD, XS, WD, Y, H, SQ = (lanes(n, W) for n in ("XD", "XS", "WD", "Y", "H", "SQ"))
        BIG1, BIG2 = lanes("BIG1", 1024), lanes("BIG2", 1024)
        S = [[b[:, c:c + W] for b in (BIG1[l], BIG2[l]) for c in (0, 512)] for l in range(L)]
        MX = lanes("MX", W + 1)
        RW = lanes("RW", 2 * W)
        MA, MB, MC = (lanes(n, W) for n in ("MA", "MB", "MC"))
        EA, EAS = (lanes(n, W) for n in ("EA", "EAS"))
        TILE, TILEO = (lanes(n, J * 128) for n in ("TILE", "TILEO"))
        ROWS = lanes("ROWS", 2 * J * 128)
        PA = [ctx.enter_context(nc.psum_tensor(f"PA{l}", [128, 512], F32)) for l in range(L)]
        PB = [ctx.enter_context(nc.psum_tensor(f"PB{l}", [128, 512], F32)) for l in range(L)]

        WALL = sb("WALL", [128, 3072])
        used = [0]

        def mat(cols, of=WALL, count=used):
            count[0] += cols
            return of[:, count[0] - cols:count[0]]

        w_msgs, w_msgd, w_updx, w_upda = mat(128), mat(128), mat(128), mat(128)
        g_h = [mat(128) for _ in range(H1)]
        g_sum = mat(128)
        a_src, a_dst, a_self = mat(36), mat(36), mat(36)
        a_edge, a_cnt = mat(36), mat(36)
        w_q, w_k, w_v, w_skip, w_ek, w_ev = (mat(128) for _ in range(6))
        w_zo, w_zx = mat(128), mat(128)
        w_e1, w_e2, w_n, w_c, w_oc = (mat(128) for _ in range(5))
        assert used[0] <= 3072, used[0]
        tmp = [0]
        wT, weT, wp, att, w_o, w_oT, w_e2t = (mat(c, BIG1[1], tmp) for c in (256, 64, 256, 12, 64, 64, 64))
        vec_names = ["bmsg", "bupd", "g0", "b0", "bp", "g1", "b1", "bq", "bskip", "g2", "b2", "be1", "be2", "bn",
                     "bc", "bo", "wb1", "wb2", "wb3", "bk", "bv", "be", "hb0", "hb1", "hb2", "hb3", "bproj", "wcol", "wb",
                     "cb", "sp0", "cvec", "mean", "var", "bs", "bt", "m64", "t0", "t1", "eps", "tiny", "cb0", "cb1", "bproj1"]
        VEC = sb("VEC", [128, len(vec_names)])
        v = {n: VEC[:, k:k + 1] for k, n in enumerate(vec_names)}
        STATD = sb("STATD", [128, 2, NB])
        STATE = sb("STATE", [128, 2, NQ])
        STATF = sb("STATF", [128, 2, NQ])
        SUMS = sb("SUMS", [128, 4])
        IDN = sb("IDN", [128, 128])
        AVG = sb("AVG", [128, 128])
        CEN = sb("CEN", [128, 128])
        ADD2 = BIG2[1][:, 0:128]
        ONES = BIG2[1][:, 128:256]
        B4 = sb("B4", [64, H1 * 128])
        B8 = sb("B8", [64, 128])
        HSEL = sb("HSEL", [128, 40])
        CAR = sb("CAR", [128, 10])

        NT = E // TE
        SRCI, DSTI, SCATI = (sb(n, [TE, NT], I32) for n in ("SRCI", "DSTI", "SCATI"))
        MAPV = sb("MAPV", [TE, NT, 2], I32)
        RINGI = sb("RINGI", [TE, L, 2, 2 * J], I32)
        RINGV = sb("RINGV", [TE, L, J, 2], I32)

        MAPBUF = [b[0:MP, 0:W].bitcast(I32) for b in (WD[0], WD[1], WD[2], WD[3], RW[0])]
        DTILE = [b[:, 512:1024] for b in BIG1]
        PREP = [BIG2[2][:, 0:W], BIG2[2][:, 512:512 + W], BIG2[3][:, 0:W], BIG2[3][:, 512:512 + W]]
        wsem, built, pdma = sem("weights_in"), sem("constants_built"), sem("prep_dma")
        masks_ready, starts, indices_ready = sem("masks_ready"), sem("starts"), sem("indices_ready")
        built_pool, dve_link, derived = sem("pool_link"), sem("dve_link"), sem("derived")
        rows_free = [sem(f"rows_free{l}") for l in range(L)]
        bc_steps, bias_row, bias_row_in = sem("bc_steps"), sem("bias_row"), sem("bias_row_in")
        CARRY = {n: sem("carry_" + n) for n in ("agg0", "hold1", "mx1", "den1", "eas1", "s10", "s11", "s12", "s13", "hold2",
                                                "mx2", "den2", "s2", "agg3")}
        wdone, ptr = sem("weights_ready"), sem("prep_transposed")
        idx_ready, map_moved, stats_added = sem("idx_ready"), [sem(f"map_moved{l}") for l in range(L)], sem("stats_added")
        late_mask = [sem(f"late_mask{l}") for l in range(L)]
        map_got, map_copied = sem("map_got"), sem("map_copied")
        stats = sem("stats")

        class Phase:
            def __init__(self, tag, full, tail, *stages):
                self.chain = Chain(*stages)
                self.at, self.k = self.chain.at, self.chain.k
                self.lag, lengths = PACE[tag]
                assert len(lengths) == len(stages)
                self.begins = [sum(lengths[:k]) for k in range(len(lengths) + 1)]
                self.window = self.begins[-1]
                self.full, self.tail = full, tail
                self.s = [sem(f"{tag}_chain{l}") for l in range(L)]
                self.load = [sem(f"{tag}_load{l}") for l in range(L)]
                self.got = [sem(f"{tag}_gather{l}") for l in range(L)]
                self.store = [sem(f"{tag}_store{l}") for l in range(L)]

            def n(self, l):
                return self.full + (l < self.tail)

            def end(self, l):
                return self.at(self.n(l), l)

            def place(self, prev):
                return self.begins[self.chain.stages.index(prev) + 1]

            def weave(self, body, parts):
                runs = [[0, l, late, body(i, l)] for i, l, late in parts]
                for run in runs:
                    run[0] = next(run[3])
                while runs:
                    run = min(runs, key=lambda r: r[0] + self.lag[r[1]] - self.window * r[2])
                    try:
                        run[0] = run[3].send((run[0] + self.lag[run[1]] >= self.window) == run[2])
                    except StopIteration:
                        runs.remove(run)

            def loop(self, eng, body, whole=None):
                self.weave(body, [(0, l, False) for l in range(L)])
                whole = whole or self.full
                with eng.Fori(0, whole - 1) as i:
                    self.weave(body, [(i, l, True) for l in range(L)] + [(i + 1, l, False) for l in range(L)])
                for n in range(whole, self.full + 2):
                    self.weave(body, [(n - 1, l, True) for l in range(L) if n - 1 < self.n(l)] +
                               [(n, l, False) for l in range(L) if n < self.n(l)])

        out_steps = ("outT", "rows")
        elu_steps = ("proj", "elu_e", "elu_l", "elu", "elu_res")
        gate_steps = ("z", "zc", "ze", "zl", "zg")
        edges, nodes = (NQ // L, NQ % L), (NB // L, NB % L)

        def ssp_names(k):
            return tuple(k + e for e in ("", "a", "r", "e", "l", "s"))

        P0 = Phase("l0", *edges, "tT", "cat", "cato", "msg", "relu", "agg0", "agg1", "upd", "updrelu", *ln_names(1),
                   "res1", *ln_names(2), *out_steps)
        PD = Phase("d1", *nodes, "upd", "updrelu", *ln_names(1), "res1", *ln_names(2), "outT1", "proj", "rows1",
                   *elu_steps[1:], *ln_names(3), "res3", *ln_names(4), "outT2", "xr", "rows2", "xrb",
                   *gate_steps, "u", "outT3", "us", "rows3", "uq")
        P1 = Phase("l1", *edges, "tT", "cat", "own", "hold0", "hold1", "logit", "lg", "leaky", "mc0", "mx0", "mc1",
                   "mx1", "dr", "drn", "dw", "exp", "den0", "den1", "eas0", "eas1", "dx",
                   *(n + str(h) for h in range(H1) for n in ("b", "a", "wd", "sa", "sb")),
                   "esum", "lcnt", "rcnt", "emean", "sself", "sadd", "sleaky", "mfin", "g1", "g2", "gexp",
                   "dfac", "dsum", "dln", "drec", "fac", "bf0", "bf1", "sf0", "sf1", "bf2", "bf3", "sf2", "sf3",
                   *elu_steps[:-1], *ln_names(3), "res3", *ln_names(4), *out_steps)
        P2 = Phase("l2", *edges, "tT", "cat", "own", "dT", "dm", "ds", "hold0", "dq", "hold1", "q", "qb", "kv", "qk", "vc", "logit", "lg",
                   "mc0", "mx0", "mc1", "mx1", "dr", "drn", "dw", "exp", "den0", "den1", "b", "wv", "s0", "s1",
                   "dln", "drec", "bd", "o", "xr", "xrb", *gate_steps, "df", "gd", "u", "um", "us", "outT",
                   "rows", "rowsu", "uq")
        P3 = Phase("l3", *edges, "tT", "cat0", "cat1", "catu0", "catu1", "lrelu", "oT", "ocat", "ocatu", "olrelu", *ln_names(1),
                   *ln_names(3), *ssp_names("f1"), *ssp_names("f2"), "h", "hb", "msg", "agg0", "agg1",
                   *ssp_names("c"), "cen2", "cb2", "sq2", "var2", "ln2", "rstd2", "norm2", *out_steps)
        P4 = Phase("d3", *nodes, "tT", "cat", "catu", "lrelu", *ln_names(1),
                   "cen2", "cb2", "sq2", "var2", "ln2", "rstd2", "norm2", *out_steps)
        for P_, n_ in ((P0, 2), (P1, 2), (P2, 2), (PD, 8), (P4, 2)):
            P_.stores, P_.credit = n_, n_
        P3.stores, P3.credit = 2 * J, 0

        block = ctx.enter_context(nc.Block())
        weight_loads = 12 * 2 + 3 * H1 + 3 + H1 + 4 + 3 + 4 + 2 * 16 + 2 * 3

        def pair(i, lane, back=False):
            return (NQ - 1 - lane) - i * L if back else i * L + lane

        def rows_at(table, row, c0=0, c1=None):
            c1 = table.shape[1] if c1 is None else c1
            return table[bass.ds(row, W), c0:c1].rearrange("(j p) c -> p j c", p=TE)

        def edge_at(q, half):
            return q * (2 * W) + half * W

        def node_at(b, half):
            return b * W + half * (N // 2)

        def spread(a, rows):
            return a.to_broadcast([rows, W])

        def mask_of(k, rows, q, half):
            return spread(MASKS[k:k + 1, bass.ds(edge_at(q, half), W)], rows)

        HALF = (slice(0, 64), slice(64, 128))

        def by_half(buf, cols):
            return buf[0:TE, 0:2 * J * cols].rearrange("p (j h c) -> p h j c", j=J, h=2)

        def by_part(buf, half):
            return buf[0:TE, :].rearrange("p (j k h c) -> p h j k c", j=J, k=2, h=2)[:, half]

        def wait_phase_done(eng, P, stores=True):
            for l in range(L):
                eng.wait_ge(P.s[l], P.end(l))
                if stores:
                    eng.wait_ge(P.store[l], 16 * (P.credit + P.stores * P.n(l)))

        @block.sync
        def _(sp):
            sp.wait_ge(built, 1)

            issued = [0]

            def ld(o, i):
                sp.dma_start(o, i).then_inc(wsem, 16)
                issued[0] += 1

            for m, a in ((w_msgs, w["L0_gnn_W_msg"][0:64, :]), (w_msgd, w["L0_gnn_W_msg"][64:128, :]),
                         (w_updx, w["L0_gnn_W_upd"][0:64, :]), (w_upda, w["L0_gnn_W_upd"][64:128, :]),
                         (w_q, w["L2_gnn_Wq"]), (w_k, w["L2_gnn_Wk"]), (w_v, w["L2_gnn_Wv"]),
                         (w_skip, w["L2_gnn_Wskip"]), (w_e1, w["L3_gnn_We1"]), (w_e2, w["L3_gnn_We2"]),
                         (w_n, w["L3_gnn_Wn"]), (w_c, w["L3_gnn_Wc"])):
                for hs in HALF:
                    ld(m[hs, hs], a)
            for h in range(H1):
                ld(wT[0:64, 64 * h:64 * h + 64], w["WT"][64 * h:64 * h + 64, :])
                ld(weT[0:64, 16 * h:16 * h + 16], w["WeT"][64 * h:64 * h + 64, :])
                ld(wp[0:64, 64 * h:64 * h + 64], w["L1_gnn_Wp"][64 * h:64 * h + 64, :])
            for k, n in enumerate(("att_src", "att_dst", "att_edge")):
                ld(att[0:64, 4 * k:4 * k + 4], w[n + "T"])
            for h in range(H1):
                ld(v[f"hb{h}"][0:64, :], w["L1_gnn_bias"][64 * h:64 * h + 64].unsqueeze(1))
            for m in (w_ek, w_ev):
                for half in range(2):
                    ld(m[64 * half:64 * half + 16, HALF[half]], w["L2_gnn_We"])
            ld(w_o[0:64, :], w["L3_gnn_Wo"])
            ld(w_oT[0:64, :], w["WoT"])
            ld(w_e2t[0:64, :], w["L3_gnn_We2"])
            for n, c in (("L2_gnn_bk", 0), ("L2_gnn_bv", 64)):
                ld(ROWS[0][0:1, c:c + 64], w[n].unsqueeze(0))
                ld(ROWS[1][0:1, c:c + 64], w["L2_gnn_be"].unsqueeze(0))
            for name, a in (("bmsg", "L0_gnn_b_msg"), ("bupd", "L0_gnn_b_upd"), ("g0", "L0_gnn_gamma"),
                            ("b0", "L0_gnn_beta"), ("bp", "L1_gnn_bp"), ("g1", "L1_gnn_gamma"),
                            ("b1", "L1_gnn_beta"), ("bq", "L2_gnn_bq"), ("bskip", "L2_gnn_bskip"),
                            ("g2", "L2_gnn_gamma"), ("b2", "L2_gnn_beta_bn"), ("be1", "L3_gnn_be1"),
                            ("be2", "L3_gnn_be2"), ("bn", "L3_gnn_bn"), ("bc", "L3_gnn_bc"), ("bo", "L3_gnn_bo")):
                ld(v[name][0:64, :], w[a].unsqueeze(1))
                ld(v[name][64:128, :], w[a].unsqueeze(1))
            wb = w["L2_gnn_Wbeta"]
            for k, name in enumerate(("wb1", "wb2", "wb3")):
                ld(v[name][0:64, :], wb[64 * k:64 * k + 64, :])
                ld(v[name][64:128, :], wb[64 * k:64 * k + 64, :])

            assert issued[0] == weight_loads, issued
            d2, s2 = dst.rearrange("(r c) -> r c", c=W), src.rearrange("(r c) -> r c", c=W)
            DI, DP, DN, SI = (t[0:NB, 0:W].bitcast(I32) for t in (XD[0], XD[1], XD[2], XD[3]))
            sp.wait_ge(built, 2)
            sp.dma_start(DI, d2).then_inc(pdma, 16)
            sp.dma_start(SI, s2).then_inc(pdma, 16)
            sp.dma_start(DP[:, 1:W], d2[:, 0:W - 1]).then_inc(pdma, 16)
            sp.dma_start(DP[1:NB, 0:1], d2[0:NB - 1, W - 1:W], allow_slow_non_contiguous=True).then_inc(pdma, 16)
            sp.dma_start(DN[:, 0:W - 1], d2[:, 1:W]).then_inc(pdma, 16)
            sp.dma_start(DN[0:NB - 1, W - 1:W], d2[1:NB, 0:1], allow_slow_non_contiguous=True).then_inc(pdma, 16)
            sp.wait_ge(built, 3)
            map_v = MAP.rearrange("(p n) k -> p (n k)", p=MP)
            for k, b in enumerate(MAPBUF):
                sp.dma_start(map_v[:, k * W:(k + 1) * W], b).then_inc(pdma, 16)
            sp.wait_ge(masks_ready, 1)
            for k, t in enumerate((Y[0], Y[1], Y[2], Y[3], H[0], H[1])):
                sp.dma_start(MASKS[k, :].rearrange("(r c) -> r c", c=W), t[0:NB, 0:W]).then_inc(pdma, 16)
            sp.wait_ge(pdma, 16 * 17)
            sp.wait_ge(bias_row, 1)
            for k, m in enumerate((w_ek, w_ev)):
                for half in range(2):
                    sp.dma_start(m[64 * half + 16:64 * half + 17, HALF[half]],
                                 ROWS[0][0:1, 64 * k:64 * k + 64]).then_inc(bias_row_in, 16)
            sp.wait_ge(bias_row_in, 16 * 4)

            def first_credit(P):
                for l in range(L):
                    sp.sem_inc(P.s[l], FIRST_COUNT[l])
                    if P.credit:
                        sp.sem_inc(P.store[l], 16 * P.credit)

            def waited(P, i, l, stage):
                sp.wait_ge(P.s[l], P.at(i, l, stage))
                sp.nop(nofuse=True)

            def run(P, loads, used, *stores):
                def more(i, l):
                    if not isinstance(i, int) or i + 1 < P.n(l):
                        loads(i + 1, l)

                def body(i, l):
                    for stage, act in sorted([(used, more), *stores], key=lambda e: P.place(e[0])):
                        if (yield P.place(stage)):
                            waited(P, i, l, stage)
                            act(i, l)

                for l in range(L):
                    loads(0, l)
                P.loop(sp, body, whole=P.full - 1)

            def load(P, l, o, a):
                sp.dma_start(o, a).then_inc(P.load[l], 16)

            def store(P, l, o, a):
                sp.dma_start(o, a).then_inc(P.store[l], 16)

            def store_rows(P, table, i, l, cols, back=False):
                for half in range(2):
                    store(P, l, rows_at(table, N + edge_at(pair(i, l, back), half)), by_half(ROWS[l], cols)[:, half])

            sp.wait_ge(wdone, 1)
            first_credit(P0)

            def loads0(i, l):
                for half, hs in enumerate(HALF):
                    load(P0, l, MA[l][hs, :], mask_of(SAME, 64, pair(i, l), half))

            run(P0, loads0, "agg1", ("rows", lambda i, l: store_rows(P0, T1, i, l, D)))

            wait_phase_done(sp, P0)
            first_credit(PD)

            def loadsD(i, l):
                b = pair(i, l)
                for half, hs in enumerate(HALF):
                    load(PD, l, XD[l][hs, :], xT[:, bass.ds(node_at(b, half), W)])

            def stores1(i, l):
                for half in range(2):
                    store(PD, l, rows_at(T1, node_at(pair(i, l), half)), by_half(TILE[l], D)[:, half])

            def stores3(i, l):
                for half in range(2):
                    b = node_at(pair(i, l), half)
                    store(PD, l, rows_at(T2, b), by_half(ROWS[l], 2 * D)[:, half, :, D:2 * D])
                    store(PD, l, rows_at(T3, b), by_half(ROWS[l], 2 * D)[:, half])
                    store(PD, l, rows_at(TU, b), by_half(ROWS[l], 2 * D)[:, half, :, 0:D])

            run(PD, loadsD, "res1", ("rows1", stores1), ("uq", stores3))

            wait_phase_done(sp, PD)
            first_credit(P1)

            def loads12(P, i, l, q, T, same, own, neg):
                for half, hs in enumerate(HALF):
                    load(P, l, by_half(TILEO[l], D)[:, half], rows_at(T, N + edge_at(q, half)))
                    load(P, l, MA[l][hs, :], mask_of(same, 64, q, half))
                    load(P, l, MB[l][hs, :], mask_of(own, 64, q, half))
                    load(P, l, MC[l][32 * half:32 * half + 32, :], mask_of(neg, 32, q, half))
                    load(P, l, EA[l][64 * half:64 * half + 16, :], ea16T[:, bass.ds(edge_at(q, half), W)])

            run(P1, lambda i, l: loads12(P1, i, l, pair(i, l, True), T1, SAMEN, LAST, NEGN), "eas1",
                ("rows", lambda i, l: store_rows(P1, T2, i, l, D, True)))

            wait_phase_done(sp, P1)
            first_credit(P2)

            def loads2(i, l):
                q = pair(i, l)
                loads12(P2, i, l, q, T2, SAME, FIRST, NEGP)
                for half, hs in enumerate(HALF):
                    load(P2, l, S[l][2][hs, :], mask_of(LAST, 64, q, half))

            def late2(i, l):
                for half, hs in enumerate(HALF):
                    sp.dma_start(S[l][3][hs, :], mask_of(LAST, 64, pair(i, l), half)).then_inc(late_mask[l], 16)

            def more2(i, l):
                if not isinstance(i, int) or i + 1 < P2.n(l):
                    late2(i + 1, l)

            for l in range(L):
                late2(0, l)
            run(P2, loads2, "drn", ("um", more2), ("rowsu", lambda i, l: store_rows(P2, T3, i, l, 2 * D)))

            wait_phase_done(sp, P2)
            first_credit(P4)

            def loads4(i, l):
                for half in range(2):
                    for k in range(2):
                        load(P4, l, by_part(BIG1[l], half)[:, :, k],
                             rows_at(T3, node_at(pair(i, l), half), k * D, k * D + D))

            def stores4(i, l):
                for half in range(2):
                    store(P4, l, rows_at(out, node_at(pair(i, l), half)), by_half(ROWS[l], D)[:, half])

            run(P4, loads4, "tT", ("rows", stores4))

            wait_phase_done(sp, P4)
            first_credit(P3)

            def loads3(i, l):
                q = pair(i, l)
                for half, hs in enumerate(HALF):
                    for k in range(2):
                        load(P3, l, by_part(BIG2[l], half)[:, :, k],
                             rows_at(T3, N + edge_at(q, half), k * D, k * D + D))
                    load(P3, l, MA[l][hs, :], mask_of(SAME, 64, q, half))
                    load(P3, l, MB[l][hs, :], ea64T[:, bass.ds(edge_at(q, half), W)])

            run(P3, loads3, "agg1")
            wait_phase_done(sp, P3)

        @block.gpsimd
        def _(g):
            n = [0]

            def step(ins):
                n[0] += 1
                ins.then_inc(built_pool, 1)
                g.wait_ge(built_pool, n[0])

            step(g.memset(WALL[:, :], 0.0))
            step(g.memset(VEC[:, :], 0.0))
            step(g.memset(v["m64"], -LN2))
            step(g.memset(v["eps"], EPS))
            step(g.memset(v["tiny"], 1e-16))
            for l in range(L):
                step(g.memset(EA[l][:, :], 1.0))
            g.sem_inc(built, 1)
            step(g.memset(XD[1][0:NB, 0:W].bitcast(I32), -1))
            step(g.memset(XD[2][0:NB, 0:W].bitcast(I32), -1))
            g.sem_inc(built, 1)
            for k, b in enumerate(MAPBUF):
                step(g.iota(b.rearrange("p (n k) -> p n k", k=2), pattern=[[1, W // 2], [0, 2]], base=k * (W // 2),
                            channel_multiplier=MN))
            g.sem_inc(built, 1)
            step(g.iota(MAPV[:, :, 0], pattern=[[TE, NT]], base=N, channel_multiplier=1))
            step(g.iota(XS[0][0:NB, 0:W].bitcast(I32), pattern=[[1, W]], base=0, channel_multiplier=W))
            step(g.memset(IDN[:, :], 0.0))
            step(g.affine_select(out=IDN[:, :], in_=IDN[:, :], compare_op=ALU.not_equal, fill=1.0, base=0,
                                 pattern=[[-1, 128]], channel_multiplier=1))
            step(g.memset(AVG[:, :], 0.0))
            step(g.memset(AVG[0:64, 0:64], 1.0 / D))
            step(g.memset(AVG[64:128, 64:128], 1.0 / D))
            step(g.memset(ONES[:, :], 1.0))
            step(g.memset(CAR[:, :], 0.0))

            def where_zero(t, pattern, base=0):
                step(g.memset(t, 0.0))
                k = {2: "p (a b) -> p a b", 3: "p (a b c) -> p a b c"}[len(pattern)]
                o = t.rearrange(k, **{n: p[1] for n, p in zip("abc", pattern)})
                step(g.affine_select(out=o, in_=o, compare_op=ALU.not_equal, fill=1.0, base=base, pattern=pattern,
                                     channel_multiplier=1))

            where_zero(B4[:, :], [[-1, H1], [-32, 2], [0, 64]])
            where_zero(B8[:, :], [[-32, 2], [-1, 8], [0, 8]])
            step(g.memset(HSEL[:, :], 0.0))
            for half in range(2):
                t = HSEL[HALF[half], 32 * half:32 * half + 8]
                step(g.memset(t, 1.0))
                for pat, mult, base in (([[-8, 8]], 1, 0), ([[8, 8]], -1, 7)):
                    step(g.affine_select(out=t, in_=t, compare_op=ALU.is_ge, fill=0.0, base=base, pattern=pat,
                                         channel_multiplier=mult))
            for c0, c1, row in ((0, 32, 16), (32, 36, 80)):
                t = a_cnt[:, c0:c1]
                step(g.affine_select(out=t, in_=t, compare_op=ALU.not_equal, fill=1.0, base=-row,
                                     pattern=[[0, c1 - c0]], channel_multiplier=1))
            g.sem_inc(built, 1)

            def free(P, i, l, stage):
                g.wait_ge(P.s[l], P.at(i, l, stage))
                g.nop(nofuse=True)

            g.wait_ge(indices_ready, 1)
            J2 = 2 * J

            def gather(P, tile, cols, table, l, k):
                for h in range(2):
                    for j in range(J):
                        c = (2 * j + h) * cols
                        g.indirect_dma_start(tile[l][0:TE, c:c + cols], None, table,
                                             bass.IndirectOffsetOnAxis(RINGI[:, l, k, h * J + j:h * J + j + 1], 0))\
                            .then_inc(P.got[l], 16)

            def indices(l, k, idx, value):
                g.tensor_copy(RINGI[:, l, k, :], idx).then_inc(idx_ready, 1)
                g.wait_ge(idx_ready, value)
                g.nop(nofuse=True)

            def gathers(P, base, used, sets, back=False):
                m = len(sets)

                def one(i, l, value):
                    q = pair(i, l, back)
                    for k, (idx, tile, cols, table) in enumerate(sets):
                        indices(l, k, idx(q), value + k + 1)
                        gather(P, tile, cols, table, l, k)

                for l in range(L):
                    one(0, l, base + m * l)
                with g.Fori(0, P.full - 1) as i:
                    for l in range(L):
                        free(P, i, l, used)
                        one(i + 1, l, i * (m * L) + (base + m * L + m * l))
                for l in range(P.tail):
                    free(P, P.full - 1, l, used)
                    one(P.full, l, base + m * L * P.full + m * l)
                return base + m * NQ

            done = gathers(P0, 0, "tT", [
                (lambda q: DSTI[:, bass.ds(q * J2, J2)], TILEO, D, x),
                (lambda q: SRCI[:, bass.ds(q * J2, J2)], TILE, D, x)])

            for l in range(L):
                g.wait_ge(P0.got[l], 16 * 2 * J2 * P0.n(l))
            g.wait_ge(pdma, 16 * 17)

            def scat_map(i, l, value):
                b = pair(i, l)
                g.tensor_copy(RINGI[:, l, 0, 0:J], SCATI[:, bass.ds(b * J, J)]).then_inc(idx_ready, 1)
                g.tensor_copy(RINGV[:, l, :, :], MAPV[:, bass.ds(b * J, J), :]).then_inc(idx_ready, 1)
                g.wait_ge(idx_ready, value)
                g.nop(nofuse=True)
                for j in range(J):
                    g.indirect_dma_start(MAP, bass.IndirectOffsetOnAxis(RINGI[:, l, 0, j:j + 1], 0),
                                         RINGV[:, l, j, :], None, bounds_check=N - 1, oob_is_err=False)\
                        .then_inc(map_moved[l], 16)

            for l in range(L):
                scat_map(0, l, done + 2 * (l + 1))
            with g.Fori(0, NB // L - 1) as i:
                for l in range(L):
                    g.wait_ge(map_moved[l], i * (16 * J) + 16 * J)
                    g.nop(nofuse=True)
                    scat_map(i + 1, l, i * (2 * L) + (done + 2 * L + 2 * (l + 1)))
            for l in range(L):
                g.wait_ge(map_moved[l], 16 * J * (NB // L))
            done += 2 * NB

            GR = L * J

            def map_gather(i, value, got):
                g.tensor_copy(RINGI[:, :, 0, 0:J], SRCI[:, bass.ds(i * GR, GR)].rearrange("p (l j) -> p l j", l=L))\
                    .then_inc(idx_ready, 1)
                g.wait_ge(idx_ready, value)
                g.nop(nofuse=True)
                for l in range(L):
                    for j in range(J):
                        g.indirect_dma_start(RINGV[:, l, j, :], None, MAP,
                                             bass.IndirectOffsetOnAxis(RINGI[:, l, 0, j:j + 1], 0))\
                            .then_inc(map_got, 16)
                g.wait_ge(map_got, got)
                g.tensor_copy(MAPV[:, bass.ds(i * GR, GR), :].rearrange("p (l j) k -> p l j k", l=L), RINGV[:, :, :, :])\
                    .then_inc(map_copied, 1)

            with g.Fori(0, NB // L) as i:
                map_gather(i, i + (done + 1), i * (16 * GR) + 16 * GR)
                g.wait_ge(map_copied, i + 1)
                g.nop(nofuse=True)
            done += NB // L

            wait_phase_done(g, PD)
            done = gathers(P1, done, "tT", [(lambda q: MAPV[:, bass.ds(q * J2, J2), 0], TILE, D, T1)], back=True)
            wait_phase_done(g, P1)
            done = gathers(P2, done, "dT", [
                (lambda q: MAPV[:, bass.ds(q * J2, J2), 1], TILE, D, T2),
                (lambda q: DSTI[:, bass.ds(q * J2, J2)], DTILE, D, TU)])
            wait_phase_done(g, P4)

            def one3(i, l, value):
                indices(l, 0, MAPV[:, bass.ds(pair(i, l) * J2, J2), 0], value)
                gather(P3, BIG1, 2 * D, T3, l, 0)

            def scatter3(i, l, value):
                indices(l, 1, SCATI[:, bass.ds(pair(i, l) * J2, J2)], value)
                g.wait_ge(P3.s[l], P3.at(i, l, "rows"))
                g.nop(nofuse=True)
                for h in range(2):
                    for j in range(J):
                        c = (2 * j + h) * D
                        g.indirect_dma_start(out, bass.IndirectOffsetOnAxis(RINGI[:, l, 1, h * J + j:h * J + j + 1], 0),
                                             ROWS[l][0:TE, c:c + D], None, bounds_check=N - 1, oob_is_err=False)\
                            .then_inc(P3.store[l], 16)

            def scattered(l, value):
                g.wait_ge(P3.store[l], value)
                g.nop(nofuse=True)
                g.sem_inc(rows_free[l], 1)

            for l in range(L):
                g.sem_inc(rows_free[l], 1)
                one3(0, l, done + l + 1)
            base = done + L
            for l in range(L):
                free(P3, 0, l, "tT")
                one3(1, l, base + l + 1)
            base += L

            def lane3(i, l, value, more=True):
                if more:
                    free(P3, i + 1, l, "tT")
                    one3(i + 2, l, value)
                scatter3(i, l, value + more)
                if l:
                    scattered(l - 1, i * (16 * J2) + 16 * J2)
                elif not isinstance(i, int) or i > 0:
                    scattered(L - 1, i * (16 * J2))

            for l in range(L):
                lane3(0, l, base + 2 * l + 1)
            base += 2 * L
            with g.Fori(0, P3.full - 3) as i:
                for l in range(L):
                    lane3(i + 1, l, i * (2 * L) + (base + 2 * l + 1))
            base += 2 * L * (P3.full - 3)
            for n in range(P3.full - 2, P3.full + 1):
                for l in range(L):
                    if n < P3.n(l):
                        more = n + 2 < P3.n(l)
                        lane3(n, l, base + 1, more)
                        base += 1 + more

        @block.tensor
        def _(t):
            t.wait_ge(built, 4)

            def after(P, i, l, stage, odd=False):
                t.wait_ge(P.s[l], P.at(i, l, stage))
                if odd:
                    t.nop(nofuse=True)

            def mm(o, a, b, start=True, stop=True):
                return t.matmul(o, a, b, start=start, stop=stop)

            t.wait_ge(starts, 1)
            t.transpose(PA[0][0:1, 0:NB], XS[1][0:NB, W - 1:W], IDN[0:NB, 0:NB]).then_inc(ptr, 1)
            t.wait_ge(starts, 2)
            mm(PA[1][0:NB, 0:1], XS[2][0:1, 0:NB], ONES[0:1, 0:1]).then_inc(ptr, 1)
            t.wait_ge(starts, 3)
            for a, t_in in enumerate(PREP):
                for j in range(J):
                    t.transpose(PB[a][0:TE, j * NB:(j + 1) * NB], t_in[0:NB, j * TE:(j + 1) * TE], IDN[0:NB, 0:NB])\
                        .then_inc(ptr, 1)

            t.wait_ge(wsem, 16 * weight_loads)
            t.wait_ge(derived, 1)
            for h in range(H1):
                a_, b_ = wT[0:64, 64 * h:64 * h + 64], wp[0:64, 64 * h:64 * h + 64]
                for hs in HALF:
                    mm(PA[0][hs, 64 * h:64 * h + 64], a_, b_)
            for hs in HALF:
                for h in range(H1):
                    mm(PB[0][hs, 0:64], wT[0:64, 64 * h:64 * h + 64], wp[0:64, 64 * h:64 * h + 64],
                       start=h == 0, stop=h == H1 - 1)
            for h in range(H1):
                a_ = wT[0:64, 64 * h:64 * h + 64]
                for hs in HALF:
                    mm(PB[1][hs, h:h + 1], a_, att[0:64, h:h + 1])
                    mm(PB[1][hs, 4 + h:5 + h], a_, att[0:64, 4 + h:5 + h])
                    mm(PB[1][hs, 8 + h:9 + h], a_, att[0:64, h:h + 1], stop=False)
                    mm(PB[1][hs, 8 + h:9 + h], a_, att[0:64, 4 + h:5 + h], start=False)
                for b_ in (0, 64):
                    mm(PA[1][b_:b_ + 16, h:h + 1], weT[0:64, 16 * h:16 * h + 16], att[0:64, 8 + h:9 + h])
            for hs in HALF:
                for h in range(H1):
                    mm(PA[2][hs, 0:1], wp[0:64, 64 * h:64 * h + 64], v[f"hb{h}"][0:64, :], start=h == 0,
                       stop=h == H1 - 1)
                mm(PA[2][hs, 1:2], w_e2t[0:64, :], v["m64"][0:64, :])
                mm(PA[2][hs, 2:3], w_o[0:64, :], v["m64"][0:64, :])
                last = mm(PA[3][hs, 0:64], w_oT[0:64, :], CEN[0:64, 0:64])
            last.then_inc(ptr, 1)
            t.wait_ge(derived, 2)
            for k, n_ in enumerate(("t0", "b0", "b1")):
                mm(PB[2][:, k:k + 1], CEN[:, :], v[n_])
            mm(PB[3][:, 0:1], w_oc, v["sp0"]).then_inc(ptr, 1)

            def pe(P, i, l, prev, f):
                if (yield P.place(prev)):
                    after(P, i, l, prev)
                    f(l).then_inc(P.s[l], 1)

            def pe_next(P, i, l, prev, f):
                if (yield P.place(prev)):
                    f(l).then_inc(P.s[l], 1)

            def fresh(P, i, l, loads, gathers):
                if loads:
                    t.wait_ge(P.load[l], i * (16 * loads) + 16 * loads)
                if gathers:
                    t.wait_ge(P.got[l], i * (16 * gathers) + 16 * gathers)
                t.wait_ge(P.s[l], P.at(i, l))

            def turn(o, cols_in):
                for j in range(J):
                    last = t.transpose(o[:, j * TE:(j + 1) * TE], cols_in(j), IDN[0:TE, 0:TE])
                return last

            def sum_mm(o, *pairs):
                for k, (a_, b_) in enumerate(pairs):
                    last = mm(o, a_, b_, start=k == 0, stop=k == len(pairs) - 1)
                return last

            def ln_pe(P, i, l, k, prev, ys, cpool=PB, vpool=PA):
                yield from pe(P, i, l, prev, lambda l: sum_mm(cpool[l][:, 0:W], *((CEN[:, :], y[l][:, :]) for y in ys)))
                yield from pe(P, i, l, f"sq{k}", lambda l: mm(vpool[l][:, 0:W], AVG[:, :], SQ[l][:, :]))

            def back_turn(o, y):
                for j in range(J):
                    last = t.transpose(o[0:TE, j * 128:(j + 1) * 128], y[:, j * TE:(j + 1) * TE], IDN[:, :])
                return last

            def outT(P, i, l, prev, y, pool=PA):
                if (yield P.place(prev)):
                    after(P, i, l, prev, True)
                    back_turn(pool[l], y[l]).then_inc(P.s[l], 1)

            def both_tiles(P, i, l, loads, gathers):
                if (yield 0):
                    fresh(P, i, l, loads, gathers)
                    turn(PA[l], lambda j: TILE[l][0:TE, j * 128:(j + 1) * 128])
                    turn(PB[l], lambda j: TILEO[l][0:TE, j * 128:(j + 1) * 128]).then_inc(P.s[l], 1)

            def layer0(i, l):
                P = P0
                yield from both_tiles(P, i, l, 0, 4 * J)
                yield from pe(P, i, l, "cato", lambda l: sum_mm(PA[l][:, 0:W], (w_msgs, XS[l][:, :]), (w_msgd, XD[l][:, :])))
                yield from pe(P, i, l, "agg1", lambda l: sum_mm(PA[l][:, 0:W], (w_updx, XD[l][:, :]), (w_upda, H[l][:, :])))
                yield from ln_pe(P, i, l, 1, "updrelu", (Y,))
                yield from ln_pe(P, i, l, 2, "res1", (Y,))
                yield from outT(P, i, l, "norm2", Y)

            P0.loop(t, layer0)

            def dense(i, l):
                P = PD
                if (yield 0):
                    fresh(P, i, l, 2, 0)
                    mm(PA[l][:, 0:W], w_updx, XD[l][:, :]).then_inc(P.s[l], 1)
                yield from ln_pe(P, i, l, 1, "updrelu", (Y,))
                yield from ln_pe(P, i, l, 2, "res1", (Y,))
                yield from outT(P, i, l, "norm2", Y, PB)
                yield from pe_next(P, i, l, "outT1", lambda l: mm(PA[l][:, 0:W], g_sum, Y[l][:, :]))
                yield from ln_pe(P, i, l, 3, "elu_res", (H,))
                yield from ln_pe(P, i, l, 4, "res3", (H,))
                yield from outT(P, i, l, "norm4", H, PB)
                yield from pe_next(P, i, l, "outT2", lambda l: mm(PA[l][:, 0:W], w_skip, H[l][:, :]))
                yield from pe(P, i, l, "xrb", lambda l: mm(PB[l][:, 0:W], w_zx, XS[l][:, :]))
                yield from outT(P, i, l, "u", Y)

            PD.loop(t, dense)

            def head(h):
                return B4[0:36, 128 * h:128 * h + 128]

            def layer1(i, l):
                P = P1
                yield from both_tiles(P, i, l, 10, 2 * J)
                yield from pe(P, i, l, "hold1", lambda l: sum_mm(PB[l][0:36, 0:W], (a_src, XS[l][:, :]), (a_dst, XD[l][:, :]),
                                                         (a_edge, EA[l][:, :])))
                for h in range(H1):
                    yield from pe(P, i, l, "dx" if h == 0 else f"sb{h - 1}",
                                  lambda l: mm(PB[l][:, 0:W], head(h), RW[l][0:36, W:2 * W]))
                    yield from pe_next(P, i, l, f"b{h}", lambda l: mm(PA[l][:, 0:W], head(h), RW[l][0:36, 0:W]))

                def loop_edge(l):
                    mm(PA[l][0:36, 0:W], a_edge, EAS[l][:, :])
                    return mm(PB[l][0:36, 0:W], a_cnt, EAS[l][:, :])
                yield from pe(P, i, l, "sb3", loop_edge)
                yield from pe(P, i, l, "emean", lambda l: mm(PA[l][0:36, 0:W], a_self, XD[l][:, :]))
                for h, prev in ((0, "fac"), (2, "sf1")):
                    yield from pe(P, i, l, prev, lambda l: mm(PA[l][:, 0:W], head(h), Y[l][0:36, :]))
                    yield from pe_next(P, i, l, f"bf{h}", lambda l: mm(PB[l][:, 0:W], head(h + 1), Y[l][0:36, :]))
                yield from pe(P, i, l, "sf3", lambda l: sum_mm(PA[l][:, 0:W], *((g_h[h], S[l][h]) for h in range(H1)),
                                                        (g_sum, XD[l][:, :])))
                yield from ln_pe(P, i, l, 3, "elu", (H, XD))
                yield from ln_pe(P, i, l, 4, "res3", (H,))
                yield from outT(P, i, l, "norm4", H)

            P1.loop(t, layer1)

            def layer2(i, l):
                P = P2
                yield from both_tiles(P, i, l, 12, 4 * J)
                yield from pe(P, i, l, "own", lambda l: turn(PA[l], lambda j: DTILE[l][0:TE, j * 128:(j + 1) * 128]))
                yield from pe(P, i, l, "hold1", lambda l: mm(PA[l][:, 0:W], w_q, XD[l][:, :]))

                def kv(l):
                    sum_mm(PB[l][:, 0:W], (w_k, XS[l][:, :]), (w_ek, EA[l][:, :]))
                    return sum_mm(PA[l][:, 0:W], (w_v, XS[l][:, :]), (w_ev, EA[l][:, :]))
                yield from pe(P, i, l, "qb", kv)
                yield from pe(P, i, l, "vc", lambda l: mm(PA[l][0:40, 0:W], HSEL[:, :], H[l][:, :]))

                def weights(l):
                    mm(PA[l][:, 0:W], B8[0:40, :], RW[l][0:40, W:2 * W])
                    return mm(PB[l][:, 0:W], B8[0:40, :], RW[l][0:40, 0:W])
                yield from pe(P, i, l, "den1", weights)
                yield from pe(P, i, l, "drec", lambda l: mm(PA[l][:, 0:W], B8[0:40, :], SQ[l][0:40, :]))
                yield from pe(P, i, l, "o", lambda l: mm(PB[l][:, 0:W], w_skip, XD[l][:, :]))
                yield from pe(P, i, l, "xrb", lambda l: sum_mm(PA[l][:, 0:W], (w_zx, XS[l][:, :]), (w_zo, S[l][0])))
                if (yield P.place("um")):
                    after(P, i, l, "um", True)
                    back_turn(PA[l], XD[l])
                    back_turn(PB[l], Y[l]).then_inc(P.s[l], 1)

            P2.loop(t, layer2)

            def x_and_u(l, tile):
                turn(PB[l], lambda j: tile[l][0:TE, j * 256:j * 256 + 128])
                return turn(PA[l], lambda j: tile[l][0:TE, j * 256 + 128:j * 256 + 256])

            t.wait_ge(stats, 1)
            mm(PA[0][:, 0:2], ADD2, SUMS[:, 0:2]).then_inc(stats_added, 1)
            t.wait_ge(stats, 4)

            def dense3(i, l):
                P = P4
                if (yield 0):
                    fresh(P, i, l, 4, 0)
                    x_and_u(l, BIG1).then_inc(P.s[l], 1)
                yield from ln_pe(P, i, l, 1, "lrelu", (XD, XS), PA, PB)
                yield from pe(P, i, l, "norm1", lambda l: mm(PA[l][:, 0:W], CEN[:, :], Y[l][:, :]))
                yield from pe(P, i, l, "sq2", lambda l: mm(PB[l][:, 0:W], AVG[:, :], SQ[l][:, :]))
                yield from outT(P, i, l, "norm2", Y)

            P4.loop(t, dense3)

            def layer3(i, l):
                P = P3

                def linear(prev, pool, weight, y):
                    yield from pe(P, i, l, prev, lambda l: mm(pool[l][:, 0:W], weight, y[l][:, :]))

                if (yield 0):
                    fresh(P, i, l, 8, 2 * J)
                    for h, pool in enumerate((PA, PB)):
                        last = turn(pool[l], lambda j: BIG1[l][0:TE, (2 * j + h) * 2 * D:(2 * j + h + 1) * 2 * D])
                    last.then_inc(P.s[l], 1)
                yield from pe(P, i, l, "catu1", lambda l: x_and_u(l, BIG2))
                yield from ln_pe(P, i, l, 1, "olrelu", (XD, XS), PA, PB)
                yield from ln_pe(P, i, l, 3, "norm1", (Y, H), PA, PB)
                yield from linear("norm3", PA, w_e1, MB)
                yield from linear("f1s", PB, w_e2, H)
                yield from linear("f2s", PA, w_n, XD)
                yield from linear("agg1", PB, w_c, XD)
                yield from pe(P, i, l, "cs", lambda l: sum_mm(PA[l][:, 0:W], (w_oc, H[l][:, :]), (CEN[:, :], Y[l][:, :])))
                yield from linear("sq2", PB, AVG[:, :], SQ)
                yield from outT(P, i, l, "norm2", Y)

            P3.loop(t, layer3)

        @block.scalar
        def _(a):
            a.preload_act_table_set("natural_log_exp_and_others")

            def each(P, i, l, prev, o, in_, f, **kw):
                if (yield P.place(prev)):
                    a.wait_ge(P.s[l], P.at(i, l, prev))
                    a.activation(o(l), in_(l), f, **kw).then_inc(P.s[l], 1)

            a.wait_ge(wsem, 16 * weight_loads)
            a.activation(v["sp0"], v["bc"], ACT.Abs).then_inc(bc_steps, 1)
            a.wait_ge(bc_steps, 1)
            a.activation(v["sp0"], v["sp0"], ACT.Exp, scale=-1.0).then_inc(bc_steps, 1)
            a.wait_ge(bc_steps, 2)
            a.activation(v["sp0"], v["sp0"], ACT.Ln, bias=1.0).then_inc(bc_steps, 1)

            a.wait_ge(built, 4)

            def on(buf, rows=128):
                return lambda l: buf[l][0:rows, 0:W]

            def ln_act(P, i, l, k, cpool=PB, vpool=PA, bias=0.0):
                yield from each(P, i, l, f"cen{k}", on(SQ), on(cpool), ACT.Square, bias=bias)
                yield from each(P, i, l, f"var{k}", on(SQ), on(vpool), ACT.Ln, bias=v["eps"])
                yield from each(P, i, l, f"ln{k}", on(SQ), on(SQ), ACT.Exp, scale=-0.5)

            def layer0(i, l):
                P = P0
                yield from each(P, i, l, "tT", on(XD), on(PB), ACT.Copy)
                yield from each(P, i, l, "msg", on(WD), on(PA), ACT.Relu, bias=v["bmsg"])
                yield from each(P, i, l, "upd", on(Y), on(PA), ACT.Relu, bias=v["bupd"])
                yield from ln_act(P, i, l, 1)
                yield from ln_act(P, i, l, 2, bias=v["cb0"])

            P0.loop(a, layer0)

            def gate(P, i, l):
                yield from each(P, i, l, "zc", on(SQ), on(SQ), ACT.Exp)
                yield from each(P, i, l, "ze", on(SQ), on(SQ), ACT.Ln, bias=1.0)
                yield from each(P, i, l, "zl", on(SQ), on(SQ), ACT.Exp, scale=-1.0)

            def sum_of(P, i, l, st, k, buf, prev):
                if (yield P.place(prev)):
                    a.wait_ge(P.s[l], P.at(i, l, prev))
                    a.activation(WD[l][:, :], buf[l][:, :], (ACT.Copy, ACT.Square)[k],
                                 accum_out=st[:, k, bass.ds(pair(i, l), 1)]).then_inc(P.s[l], 1)

            def elu_exp(P, i, l, prev="proj"):
                yield from each(P, i, l, prev, on(SQ), on(PA), ACT.Exp, bias=v["bproj"])

            def xu_rows(l, k):
                return ROWS[l][0:TE, :].rearrange("p (jh k c) -> p jh k c", k=2, c=D)[:, :, k, :]

            def tile_rows(pool, l):
                return pool[l][0:TE, 0:J * 128].rearrange("p (jh c) -> p jh c", c=D)

            def dense(i, l):
                P = PD
                yield from each(P, i, l, "upd", on(Y), on(PA), ACT.Relu, bias=v["bupd"])
                yield from ln_act(P, i, l, 1)
                yield from ln_act(P, i, l, 2, bias=v["cb0"])
                yield from elu_exp(P, i, l, "rows1")
                yield from ln_act(P, i, l, 3)
                yield from ln_act(P, i, l, 4, bias=v["cb1"])
                yield from each(P, i, l, "rows2", on(XS), on(PA), ACT.Identity, bias=v["bskip"])
                yield from gate(P, i, l)
                yield from sum_of(P, i, l, STATD, 0, Y, "u")
                yield from sum_of(P, i, l, STATD, 1, Y, "us")

            PD.loop(a, dense)

            def layer1(i, l):
                P = P1
                yield from each(P, i, l, "tT", on(XS), on(PA), ACT.Copy)
                yield from each(P, i, l, "logit", on(Y, 36), on(PB, 36), ACT.Copy)
                yield from each(P, i, l, "dw", lambda l: RW[l][0:36, :], lambda l: RW[l][0:36, :], ACT.Exp)
                yield from each(P, i, l, "esum", on(SQ, 36), on(PB, 36), ACT.Ln)
                yield from each(P, i, l, "lcnt", on(SQ, 36), on(SQ, 36), ACT.Exp, scale=-1.0)
                yield from each(P, i, l, "g2", lambda l: RW[l][0:36, :], lambda l: RW[l][0:36, :], ACT.Exp)
                yield from each(P, i, l, "dsum", on(Y, 36), on(Y, 36), ACT.Ln)
                yield from each(P, i, l, "dln", on(Y, 36), on(Y, 36), ACT.Exp, scale=-1.0)
                yield from elu_exp(P, i, l)
                yield from each(P, i, l, "elu_e", on(H), on(PA), ACT.Identity, bias=v["bproj1"])
                yield from ln_act(P, i, l, 3)
                yield from ln_act(P, i, l, 4, bias=v["cb1"])
                if (yield P.place("outT")):
                    a.wait_ge(P.store[l], i * (16 * P.stores) + 16 * P.stores)
                yield from each(P, i, l, "outT", lambda l: ROWS[l][0:TE, 0:J * 128], lambda l: PA[l][0:TE, 0:J * 128],
                                ACT.Copy)

            P1.loop(a, layer1)

            def layer2(i, l):
                P = P2
                yield from each(P, i, l, "tT", on(XS), on(PA), ACT.Copy)
                yield from sum_of(P, i, l, STATF, 0, Y, "dm")
                yield from sum_of(P, i, l, STATF, 1, Y, "hold0")
                yield from each(P, i, l, "q", on(Y), on(PA), ACT.Identity, bias=v["bq"])
                yield from each(P, i, l, "qk", on(WD), on(PA), ACT.Copy)
                yield from each(P, i, l, "logit", on(SQ, 40), on(PA, 40), ACT.Copy, scale=float(H2) ** -0.5)
                yield from each(P, i, l, "dw", lambda l: RW[l][0:40, :], lambda l: RW[l][0:40, :], ACT.Exp)
                yield from each(P, i, l, "s1", on(SQ, 40), on(Y, 40), ACT.Ln, bias=v["tiny"][0:40, :])
                yield from each(P, i, l, "dln", on(SQ, 40), on(SQ, 40), ACT.Exp, scale=-1.0)
                yield from each(P, i, l, "xr", on(XS), on(PB), ACT.Identity, bias=v["bskip"])
                yield from gate(P, i, l)
                yield from sum_of(P, i, l, STATE, 0, SQ, "um")
                if (yield P.place("outT")):
                    a.wait_ge(P.store[l], i * (16 * P.stores) + 16 * P.stores)
                yield from each(P, i, l, "outT", lambda l: xu_rows(l, 0), lambda l: tile_rows(PB, l), ACT.Copy)
                yield from sum_of(P, i, l, STATE, 1, SQ, "rowsu")

            P2.loop(a, layer2)

            a.wait_ge(stats, 4)
            a.activation(v["bs"], v["var"], ACT.Ln, bias=v["eps"]).then_inc(stats, 1)
            a.wait_ge(stats, 5)
            a.activation(v["bs"], v["bs"], ACT.Exp, scale=-0.5).then_inc(stats, 1)

            def last_ln(P, i, l, bias):
                yield from each(P, i, l, "cen2", on(H), on(PA), ACT.Identity, bias=bias)
                yield from each(P, i, l, "cb2", on(SQ), on(H), ACT.Square)
                yield from each(P, i, l, "var2", on(SQ), on(PB), ACT.Ln, bias=v["eps"])
                yield from each(P, i, l, "ln2", on(SQ), on(SQ), ACT.Exp, scale=-0.5)

            def dense3(i, l):
                yield from ln_act(P4, i, l, 1, PA, PB)
                yield from last_ln(P4, i, l, v["cvec"])

            P4.loop(a, dense3)

            def layer3(i, l):
                P = P3

                def ssp(k, pool, bias):
                    yield from each(P, i, l, k, on(SQ), on(pool), ACT.Abs, bias=bias)
                    yield from each(P, i, l, f"{k}a", on(SQ), on(SQ), ACT.Exp, scale=-1.0)
                    yield from each(P, i, l, f"{k}e", on(SQ), on(SQ), ACT.Ln, bias=1.0)

                yield from ln_act(P, i, l, 1, PA, PB)
                yield from ln_act(P, i, l, 3, PA, PB)
                yield from ssp("f1", PA, v["be1"])
                yield from ssp("f2", PB, v["be2"])
                yield from each(P, i, l, "h", on(XS), on(PA), ACT.Identity, bias=v["bn"])
                yield from ssp("c", PB, v["bc"])
                yield from last_ln(P, i, l, v["cb"])

            P3.loop(a, layer3)

        @block.vector
        def _(d):
            chain = [0]

            def link(ins):
                chain[0] += 1
                ins.then_inc(dve_link, 1)
                d.wait_ge(dve_link, chain[0])

            R_ = slice(0, NB)
            i32 = lambda t: t[R_, 0:W].bitcast(I32)
            d.wait_ge(pdma, 16 * 11)
            link(d.tensor_tensor(Y[0][R_, :], i32(XD[0]), i32(XD[1]), ALU.is_equal))
            link(d.tensor_tensor(Y[2][R_, :], i32(XD[0]), i32(XD[2]), ALU.is_equal))
            link(d.tensor_scalar(Y[1][R_, :], Y[0][R_, :], -1.0, 1.0, ALU.mult, ALU.add))
            link(d.tensor_scalar(Y[3][R_, :], Y[2][R_, :], -1.0, 1.0, ALU.mult, ALU.add))
            link(d.tensor_scalar(H[0][R_, :], Y[1][R_, :], NEG, None, ALU.mult))
            link(d.tensor_scalar(H[1][R_, :], Y[3][R_, :], NEG, None, ALU.mult))
            d.sem_inc(masks_ready, 1)
            d.wait_ge(built, 4)
            link(d.tensor_copy(H[2][R_, :], i32(XS[0])))
            link(d.tensor_tensor(H[2][R_, :], H[2][R_, :], Y[1][R_, :], ALU.mult))
            link(d.tensor_tensor_scan(XS[1][R_, :], H[2][R_, :], H[2][R_, :], 0.0, ALU.max, ALU.max))
            d.sem_inc(starts, 1)
            d.wait_ge(ptr, 1)
            link(d.memset(XS[2][0:1, 0:1], 0.0))
            link(d.tensor_copy(XS[3][0:1, 0:NB], PA[0][0:1, 0:NB]))
            link(d.tensor_tensor_scan(XS[2][0:1, 1:NB + 1], XS[3][0:1, 0:NB], XS[3][0:1, 0:NB], 0.0, ALU.max, ALU.max))
            d.sem_inc(starts, 1)
            d.wait_ge(ptr, 2)
            link(d.tensor_copy(CAR[R_, 9:10], PA[1][R_, 0:1]))
            link(d.tensor_scalar(PREP[3][R_, :], XS[1][R_, :], CAR[R_, 9:10], float(N), ALU.max, ALU.add))
            link(d.tensor_copy(PREP[0][R_, :], i32(XD[3])))
            link(d.tensor_copy(PREP[1][R_, :], i32(XD[0])))
            link(d.tensor_scalar(H[3][R_, :], Y[2][R_, :], FAR, None, ALU.mult))
            link(d.tensor_tensor(PREP[2][R_, :], PREP[1][R_, :], H[3][R_, :], ALU.add))
            d.sem_inc(starts, 1)
            for k, o in enumerate((SRCI[:, :], DSTI[:, :], SCATI[:, :], MAPV[:, :, 1])):
                d.wait_ge(ptr, 2 + J * (k + 1))
                link(d.tensor_copy(o.rearrange("p (b j) -> p j b", j=J),
                                   PB[k][0:TE, 0:J * NB].rearrange("p (j b) -> p j b", j=J)))
            d.sem_inc(indices_ready, 1)
            link(d.tensor_tensor(CEN[:, :], IDN[:, :], AVG[:, :], ALU.subtract))
            d.wait_ge(wsem, 16 * weight_loads)
            d.sem_inc(derived, 1)
            link(d.tensor_tensor(v["wb"], v["wb2"], v["wb3"], ALU.subtract))
            link(d.tensor_tensor(v["wcol"], v["wb1"], v["wb3"], ALU.add))
            link(d.tensor_scalar(w_zx, AVG[:, :], v["wb"], float(D), ALU.mult, ALU.mult))
            link(d.tensor_scalar(w_zo, AVG[:, :], v["wcol"], float(D), ALU.mult, ALU.mult))
            link(d.tensor_tensor(ROWS[0][0:1, 0:128], ROWS[0][0:1, 0:128], ROWS[1][0:1, 0:128], ALU.add))
            d.sem_inc(bias_row, 1)
            d.wait_ge(ptr, 2 + 4 * J + 1)
            for hs in HALF:
                for h in range(H1):
                    link(d.tensor_copy(g_h[h][hs, hs], PA[0][hs, 64 * h:64 * h + 64]))
                link(d.tensor_copy(g_sum[hs, hs], PB[0][hs, 0:64]))
                c = 0 if hs.start == 0 else 32
                for k, m in enumerate((a_src, a_dst, a_self)):
                    link(d.tensor_copy(m[hs, c:c + 4], PB[1][hs, 4 * k:4 * k + 4]))
                link(d.tensor_copy(a_edge[hs.start:hs.start + 16, c:c + 4], PA[1][hs.start:hs.start + 16, 0:4]))
                link(d.tensor_copy(w_oc[hs, hs], PA[3][hs, 0:64]))
            link(d.tensor_tensor(v["bproj"], v["bp"], PA[2][:, 0:1], ALU.add))
            link(d.tensor_scalar(v["bproj1"], v["bproj"], 1.0, None, ALU.add))
            link(d.tensor_tensor(v["be2"], v["be2"], PA[2][:, 1:2], ALU.add))
            link(d.tensor_tensor(v["t0"], v["bo"], PA[2][:, 2:3], ALU.add))
            d.wait_ge(bc_steps, 3)
            link(d.tensor_scalar(v["t1"], v["bc"], 0.0, None, ALU.max))
            link(d.tensor_tensor(v["sp0"], v["sp0"], v["t1"], ALU.add))
            d.sem_inc(derived, 1)
            d.wait_ge(ptr, 2 + 4 * J + 2)
            for k, n_ in enumerate(("cb", "cb0", "cb1")):
                link(d.tensor_copy(v[n_], PB[2][:, k:k + 1]))
            link(d.tensor_tensor(v["cvec"], v["cb"], PB[3][:, 0:1], ALU.add))
            d.sem_inc(wdone, 1)

            def stage(P, i, l, prev, f):
                if (yield P.place(prev)):
                    d.wait_ge(P.s[l], P.at(i, l, prev))
                    f(l).then_inc(P.s[l], 1)

            def scans(P, i, l, prev, me, carry, col, out_, data0, data1, rows, real, op0=ALU.mult, op1=ALU.add,
                      back=False, before=None):
                order, step = ((1, 0), -1) if back else ((0, 1), 1)
                for k, b in enumerate(order):
                    rs = rows[b]
                    before_scan = prev if k == 0 else me[0]
                    if not (yield P.place(before_scan)):
                        continue
                    d.wait_ge(P.s[l], P.at(i, l, before_scan))
                    d.wait_ge(CARRY[carry], i * (2 * L) + (carried[carry] + 2 * l + k))
                    if before:
                        c0 = before(l)
                        d.tensor_copy(c0[rs, :], CAR[rs, col:col + 1]).then_inc(P.s[l], 1)
                        d.wait_ge(P.s[l], P.at(i, l, before_names[k]))
                    d.tensor_tensor_scan(out_(l)[rs, ::step], data0(l)[rs, ::step], data1(l)[rs, ::step],
                                         CAR[rs, col:col + 1], op0, op1).then_inc(P.s[l], 1)
                    d.wait_ge(P.s[l], P.at(i, l, me[k]))
                    e = 0 if back else W - 1
                    d.tensor_copy(CAR[real[1 - b], col:col + 1], out_(l)[real[b], e:e + 1]).then_inc(CARRY[carry], 1)
                    if k == 1:
                        d.wait_ge(CARRY[carry], i * (2 * L) + (carried[carry] + 2 * l + 2))

            before_names = ("mc0", "mc1")
            R64 = (slice(0, 64), slice(64, 128))
            R4, R4R = (slice(0, 32), slice(32, 36)), (slice(0, 4), slice(32, 36))
            R8, R8R = (slice(0, 32), slice(32, 40)), (slice(0, 8), slice(32, 40))

            def handed_on(*names):
                for n_ in names:
                    d.wait_ge(CARRY[n_], carried[n_] + NB)

            carried = {n_: 1 + CARRY_COUNT * k for k, n_ in enumerate(CARRY)}
            for n_, s_ in CARRY.items():
                d.sem_inc(s_, carried[n_])

            def on(buf, rows=128, c0=0):
                return lambda l: buf[l][0:rows, c0:c0 + W]

            def tt(P, i, l, prev, o, a_, b_, op):
                yield from stage(P, i, l, prev, lambda l: d.tensor_tensor(o(l), a_(l), b_(l), op))

            def ln_dve(P, i, l, k, y, aff=None, bias=None, pool=PB):
                if bias:
                    yield from stage(P, i, l, f"rstd{k}", lambda l: d.scalar_tensor_tensor(
                        out=y[l][:, :], in0=pool[l][:, 0:W], scalar=v[bias], in1=SQ[l][:, :], op0=ALU.add, op1=ALU.mult))
                else:
                    yield from tt(P, i, l, f"rstd{k}", on(y), on(pool), on(SQ), ALU.mult)
                if aff:
                    g_, res = aff
                    yield from stage(P, i, l, f"norm{k}", lambda l: d.scalar_tensor_tensor(
                        out=y[l][:, :], in0=y[l][:, :], scalar=v[g_], in1=res[l][:, :], op0=ALU.mult, op1=ALU.add))

            def rows_out(P, i, l):
                if (yield P.place("outT")):
                    if P.credit:
                        d.wait_ge(P.store[l], i * (16 * P.stores) + 16 * P.stores)
                    else:
                        d.wait_ge(rows_free[l], i + 1)
                    d.wait_ge(P.s[l], P.at(i, l, "outT"))
                    d.tensor_copy(ROWS[l][0:TE, 0:J * 128], PA[l][0:TE, 0:J * 128]).then_inc(P.s[l], 1)

            def cat(P, i, l, prev="tT", o=XS):
                yield from stage(P, i, l, prev, lambda l: d.tensor_copy(o[l][:, :], PA[l][:, 0:W]))

            def loaded(P, i, l, prev, n):
                if (yield P.place(prev)):
                    d.wait_ge(P.load[l], i * (16 * n) + 16 * n)

            def layer0(i, l):
                P = P0
                yield from cat(P, i, l)
                yield from loaded(P, i, l, "relu", 2)
                yield from scans(P, i, l, "relu", ("agg0", "agg1"), "agg0", 0, on(H), on(MA), on(WD), R64, R64)
                yield from ln_dve(P, i, l, 1, Y, ("g0", XD))
                yield from ln_dve(P, i, l, 2, Y, bias="cb0")
                yield from rows_out(P, i, l)

            P0.loop(d, layer0)

            handed_on("agg0")
            def elu(P, i, l, res, linear=True):
                if linear:
                    yield from stage(P, i, l, "elu_e", lambda l: d.tensor_scalar(H[l][:, :], PA[l][:, 0:W], v["bproj1"],
                                                                                 None, ALU.add))
                yield from stage(P, i, l, "elu_l", lambda l: d.scalar_tensor_tensor(
                    out=H[l][:, :], in0=SQ[l][:, :], scalar=1.0, in1=H[l][:, :], op0=ALU.min, op1=ALU.max))
                if res:
                    yield from tt(P, i, l, "elu", on(H), on(H), on(res), ALU.add)

            def zclip(P, i, l, pool):
                yield from stage(P, i, l, "z", lambda l: d.tensor_scalar(SQ[l][:, :], pool[l][:, 0:W], -1.0, 40.0, ALU.mult,
                                                                  ALU.min))

            def leaky(P, i, l, prev, buf, slope, rows=128):
                yield from stage(P, i, l, prev, lambda l: d.scalar_tensor_tensor(
                    out=buf[l][0:rows, 0:W], in0=buf[l][0:rows, 0:W], scalar=slope, in1=buf[l][0:rows, 0:W],
                    op0=ALU.mult, op1=ALU.max))

            def xu_rows(l, k):
                return ROWS[l][0:TE, :].rearrange("p (jh k c) -> p jh k c", k=2, c=D)[:, :, k, :]

            def tile_rows(pool, l):
                return pool[l][0:TE, 0:J * 128].rearrange("p (jh c) -> p jh c", c=D)

            def dense(i, l):
                P = PD
                yield from ln_dve(P, i, l, 1, Y, ("g0", XD))
                yield from ln_dve(P, i, l, 2, Y, bias="cb0")
                if (yield P.place("outT1")):
                    d.wait_ge(P.store[l], i * (16 * P.stores) + 16 * P.stores)
                    d.wait_ge(P.s[l], P.at(i, l, "outT1"))
                    d.tensor_copy(TILE[l][0:TE, :], PB[l][0:TE, 0:J * 128]).then_inc(P.s[l], 1)
                yield from elu(P, i, l, Y)
                yield from ln_dve(P, i, l, 3, H, ("g1", Y))
                yield from ln_dve(P, i, l, 4, H, bias="cb1")
                yield from stage(P, i, l, "outT2", lambda l: d.tensor_copy(xu_rows(l, 1), tile_rows(PB, l)))
                yield from zclip(P, i, l, PB)
                yield from tt(P, i, l, "zg", on(Y), on(SQ), on(XS), ALU.mult)
                yield from stage(P, i, l, "us", lambda l: d.tensor_copy(xu_rows(l, 0), tile_rows(PA, l)))

            PD.loop(d, dense)

            def held(P, i, l, back):
                yield from tt(P, i, l, "tT", on(H), on(PB), on(MB), ALU.mult)
                if not back:
                    yield from tt(P, i, l, "dT", on(Y), on(PA), lambda l: S[l][2], ALU.mult)
                yield from scans(P, i, l, "own" if back else "dm", ("hold0", "hold1"), "hold1" if back else "hold2", 1, on(XD), on(MA), on(H),
                      R64, R64, back=back)

            def layer1(i, l):
                P = P1
                yield from held(P, i, l, True)
                n = 36
                yield from leaky(P, i, l, "lg", Y, 0.2, n)
                yield from scans(P, i, l, "leaky", ("mx0", "mx1"), "mx1", 2, on(MX), on(MC), on(Y), R4, R4R, ALU.add, ALU.max,
                      back=True, before=lambda l: MX[l][:, W:W + 1])
                yield from tt(P, i, l, "mx1", on(RW, n), on(MX, n, 1), on(MX, n), ALU.subtract)
                yield from tt(P, i, l, "dr", on(RW, n), on(RW, n), on(MC, n), ALU.add)
                yield from tt(P, i, l, "drn", on(RW, n, W), on(Y, n), on(MX, n), ALU.subtract)
                yield from scans(P, i, l, "exp", ("den0", "den1"), "den1", 3, on(H), on(RW), on(RW, 128, W), R4, R4R, back=True)
                yield from scans(P, i, l, "den1", ("eas0", "eas1"), "eas1", 4, on(EAS), on(MA), on(EA), R64, R64, back=True)
                yield from tt(P, i, l, "eas1", on(XS), on(XS), on(XD), ALU.subtract)
                for h in range(H1):
                    yield from tt(P, i, l, f"b{h}", on(WD), on(PB), on(XS), ALU.mult)
                    yield from scans(P, i, l, f"wd{h}", (f"sa{h}", f"sb{h}"), f"s1{h}", 5 + h, lambda l: S[l][h],
                          on(PA), on(WD), R64, R64, back=True)
                yield from tt(P, i, l, "rcnt", on(SQ, n), on(PA, n), on(SQ, n), ALU.mult)
                yield from tt(P, i, l, "sself", on(SQ, n), on(PA, n), on(SQ, n), ALU.add)
                yield from leaky(P, i, l, "sadd", SQ, 0.2, n)
                yield from tt(P, i, l, "sleaky", on(Y, n), on(MX, n), on(SQ, n), ALU.max)
                yield from tt(P, i, l, "mfin", on(RW, n), on(MX, n), on(Y, n), ALU.subtract)
                yield from tt(P, i, l, "g1", on(RW, n, W), on(SQ, n), on(Y, n), ALU.subtract)
                yield from tt(P, i, l, "gexp", on(Y, n), on(H, n), on(RW, n), ALU.mult)
                yield from tt(P, i, l, "dfac", on(Y, n), on(Y, n), on(RW, n, W), ALU.add)
                yield from tt(P, i, l, "drec", on(Y, n), on(Y, n), on(RW, n), ALU.mult)
                for h, prev, pool in ((0, "bf0", PA), (1, "sf0", PB), (2, "bf2", PA), (3, "sf2", PB)):
                    yield from tt(P, i, l, prev, lambda l: S[l][h], lambda l: S[l][h], on(pool), ALU.mult)
                yield from elu(P, i, l, None, linear=False)
                yield from ln_dve(P, i, l, 3, H, ("g1", XD))
                yield from ln_dve(P, i, l, 4, H, bias="cb1")

            P1.loop(d, layer1)
            handed_on("hold1", "mx1", "den1", "eas1", "s10", "s11", "s12", "s13")

            def layer2(i, l):
                P = P2
                yield from held(P, i, l, False)
                n = 40
                yield from tt(P, i, l, "kv", on(H), on(PB), on(Y), ALU.mult)
                yield from scans(P, i, l, "lg", ("mx0", "mx1"), "mx2", 2, on(MX, 128, 1), on(MC), on(SQ), R8, R8R, ALU.add,
                      ALU.max, before=lambda l: MX[l][:, 0:1])
                yield from tt(P, i, l, "mx1", on(RW, n), on(MX, n), on(MX, n, 1), ALU.subtract)
                yield from tt(P, i, l, "dr", on(RW, n), on(RW, n), on(MC, n), ALU.add)
                yield from tt(P, i, l, "drn", on(RW, n, W), on(SQ, n), on(MX, n, 1), ALU.subtract)
                yield from scans(P, i, l, "exp", ("den0", "den1"), "den2", 3, on(Y), on(RW), on(RW, 128, W), R8, R8R)
                yield from tt(P, i, l, "b", on(WD), on(WD), on(PA), ALU.mult)
                yield from scans(P, i, l, "wv", ("s0", "s1"), "s2", 5, lambda l: S[l][0], on(PB), on(WD), R64, R64)
                yield from tt(P, i, l, "bd", lambda l: S[l][0], lambda l: S[l][0], on(PA), ALU.mult)
                yield from zclip(P, i, l, PA)
                yield from tt(P, i, l, "zg", on(WD), on(XS), lambda l: S[l][0], ALU.subtract)
                yield from tt(P, i, l, "df", on(WD), on(WD), on(SQ), ALU.mult)
                yield from tt(P, i, l, "gd", on(Y), lambda l: S[l][0], on(WD), ALU.add)
                if (yield P.place("u")):
                    d.wait_ge(late_mask[l], i * (16 * 2) + 16 * 2)
                yield from tt(P, i, l, "u", on(SQ), on(Y), lambda l: S[l][3], ALU.mult)
                if (yield P.place("outT")):
                    d.wait_ge(P.store[l], i * (16 * P.stores) + 16 * P.stores)
                    d.wait_ge(P.s[l], P.at(i, l, "outT"))
                    d.tensor_copy(ROWS[l][0:TE, :].rearrange("p (jh k c) -> p jh k c", k=2, c=D)[:, :, 1, :],
                                  PA[l][0:TE, 0:J * 128].rearrange("p (jh c) -> p jh c", c=D)).then_inc(P.s[l], 1)

            P2.loop(d, layer2)
            handed_on("hold2", "mx2", "den2", "s2")

            for l in range(L):
                d.wait_ge(P2.s[l], P2.end(l))
            link(d.tensor_tensor(ADD2[:, 0:64], IDN[:, 0:64], IDN[:, 64:128], ALU.add))
            link(d.tensor_copy(ADD2[:, 64:128], ADD2[:, 0:64]))
            link(d.tensor_reduce(SUMS[:, 0:2], STATD[:, :, :], AX.X, ALU.add))
            link(d.tensor_reduce(SUMS[:, 2:4], STATE[:, :, :], AX.X, ALU.add))
            link(d.tensor_tensor(SUMS[:, 0:2], SUMS[:, 0:2], SUMS[:, 2:4], ALU.add))
            link(d.tensor_reduce(SUMS[:, 2:4], STATF[:, :, :], AX.X, ALU.add))
            link(d.tensor_tensor(SUMS[:, 0:2], SUMS[:, 0:2], SUMS[:, 2:4], ALU.subtract))
            d.sem_inc(stats, 1)
            d.wait_ge(stats_added, 1)
            link(d.tensor_scalar(v["mean"], PA[0][:, 0:1], 1.0 / N, None, ALU.mult))
            link(d.tensor_scalar(v["var"], PA[0][:, 1:2], 1.0 / N, None, ALU.mult))
            link(d.tensor_tensor(v["t0"], v["mean"], v["mean"], ALU.mult))
            link(d.tensor_tensor(v["var"], v["var"], v["t0"], ALU.subtract))
            d.sem_inc(stats, 3)
            d.wait_ge(stats, 6)
            link(d.tensor_tensor(v["bs"], v["bs"], v["g2"], ALU.mult))
            link(d.tensor_tensor(v["t0"], v["mean"], v["bs"], ALU.mult))
            link(d.tensor_tensor(v["bt"], v["b2"], v["t0"], ALU.subtract))

            def x_and_u(P, i, l, turned, scaled, x_, u_):
                yield from cat(P, i, l, turned, x_)
                yield from stage(P, i, l, turned, lambda l: d.tensor_scalar(u_[l][:, :], PB[l][:, 0:W], v["bs"], v["bt"],
                                                                     ALU.mult, ALU.add))
                yield from leaky(P, i, l, scaled, u_, 0.01)

            def dense3(i, l):
                P = P4
                yield from x_and_u(P, i, l, "tT", "catu", XD, XS)
                yield from ln_dve(P, i, l, 1, Y, pool=PA)
                yield from tt(P, i, l, "rstd2", on(Y), on(H), on(SQ), ALU.mult)
                yield from rows_out(P, i, l)

            P4.loop(d, dense3)

            def layer3(i, l):
                P = P3

                def ssp(k, pool, bias, o):
                    yield from stage(P, i, l, f"{k}a", lambda l: d.tensor_scalar(o[l][:, :], pool[l][:, 0:W], v[bias], 0.0,
                                                                          ALU.add, ALU.max))
                    yield from tt(P, i, l, f"{k}l", on(o), on(o), on(SQ), ALU.add)

                for h, pool in enumerate((PA, PB)):
                    yield from stage(P, i, l, "tT", lambda l: d.tensor_copy(XD[l][R64[h], :], pool[l][64:128, 0:W]))
                for h, pool in enumerate((PA, PB)):
                    yield from stage(P, i, l, "tT", lambda l: d.tensor_scalar(
                        XS[l][R64[h], :], pool[l][0:64, 0:W], v["bs"][0:64, :], v["bt"][0:64, :], ALU.mult, ALU.add))
                yield from leaky(P, i, l, "catu1", XS, 0.01)
                yield from x_and_u(P, i, l, "oT", "ocatu", Y, H)
                yield from ln_dve(P, i, l, 1, XD, pool=PA)
                yield from ln_dve(P, i, l, 3, Y, pool=PA)
                yield from ssp("f1", PA, "be1", H)
                yield from ssp("f2", PB, "be2", H)
                yield from stage(P, i, l, "hb", lambda l: d.scalar_tensor_tensor(
                    out=XS[l][:, :], in0=H[l][:, :], scalar=-LN2, in1=XS[l][:, :], op0=ALU.add, op1=ALU.mult))
                yield from scans(P, i, l, "msg", ("agg0", "agg1"), "agg3", 1, on(XD), on(MA), on(XS), R64, R64)
                yield from ssp("c", PB, "bc", H)
                yield from tt(P, i, l, "rstd2", on(Y), on(H), on(SQ), ALU.mult)
                yield from rows_out(P, i, l)

            P3.loop(d, layer3)


_WEIGHTS = ['L0_gnn_W_msg', 'L0_gnn_b_msg', 'L0_gnn_W_upd', 'L0_gnn_b_upd', 'L0_gnn_gamma', 'L0_gnn_beta',
            'L1_gnn_bias', 'L1_gnn_Wp', 'L1_gnn_bp', 'L1_gnn_gamma', 'L1_gnn_beta', 'L2_gnn_Wq', 'L2_gnn_bq',
            'L2_gnn_Wk', 'L2_gnn_bk', 'L2_gnn_Wv', 'L2_gnn_bv', 'L2_gnn_We', 'L2_gnn_be', 'L2_gnn_Wskip',
            'L2_gnn_bskip', 'L2_gnn_Wbeta', 'L2_gnn_gamma', 'L2_gnn_beta_bn', 'L3_gnn_We1', 'L3_gnn_be1',
            'L3_gnn_We2', 'L3_gnn_be2', 'L3_gnn_Wn', 'L3_gnn_bn', 'L3_gnn_Wc', 'L3_gnn_bc', 'L3_gnn_Wo',
            'L3_gnn_bo']
_TURNED = {'WT': 'L1_gnn_W', 'WeT': 'L1_gnn_W_edge', 'att_srcT': 'L1_gnn_att_src', 'att_dstT': 'L1_gnn_att_dst',
           'att_edgeT': 'L1_gnn_att_edge', 'WoT': 'L3_gnn_Wo'}


def kernel(**inputs):
    import numpy as _np
    import concourse.bacc as _bacc
    from concourse import mybir as _mybir
    from concourse.bass_utils import run_bass_kernel_spmd as _run

    nc = _bacc.Bacc("TRN2", target_bir_lowering=False, num_devices=1)
    arrays, aps = {}, {}

    def give(name, a):
        a = _np.ascontiguousarray(a)
        arrays[name] = a
        aps[name] = nc.dram_tensor(name, a.shape, _mybir.dt.from_np(a.dtype), kind="ExternalInput").ap()

    for name in ("x", "src", "dst"):
        give(name, _np.asarray(inputs[name]))
    give("xT", _np.asarray(inputs["x"]).T)
    give("ea16T", _np.asarray(inputs["edge_attr_16"]).T)
    give("ea64T", _np.asarray(inputs["edge_attr_64"]).T)
    for name in _WEIGHTS:
        give(name, _np.asarray(inputs[name]))
    for name, of in _TURNED.items():
        give(name, _np.asarray(inputs[of]).T)
    out = nc.dram_tensor("out", (N, D), F32, kind="ExternalOutput").ap()
    program(nc, aps["x"], aps["xT"], aps["src"], aps["dst"], aps["ea16T"], aps["ea64T"], aps, out)
    r = _run(nc, [arrays], core_ids=[0])
    return r.results[0]["out"]
```
